# Optimizing a Trainium2 kernel written in Bass

```python
import numpy as np
import jax
import jax.numpy as jnp

def _softmax(x, axis=-1):
    return jax.nn.softmax(x, axis=axis)

def _gelu(x):
    return jax.nn.gelu(x, approximate=True)

def _silu(x):
    return jax.nn.silu(x)

def _sigmoid(x):
    return jax.nn.sigmoid(x)

def _layernorm(x, axis=-1, eps=1e-05):
    m = jnp.mean(x, axis=axis, keepdims=True)
    v = jnp.var(x, axis=axis, keepdims=True)
    return (x - m) / jnp.sqrt(v + eps)

def _scatter_add(tgt, idx, src, axis=0):
    return tgt.at[idx].add(src)

def _segment_sum(src, seg, n):
    return jax.ops.segment_sum(src, seg, n)
kernel_name = 'mk_seq_preln_d1_jaxref_r8_e7e0e7'

def setup_inputs(seed: int=0):
    np.random.seed(seed)
    _w = jnp.asarray

    def _L0_attn_setup():
        import jax, jax.numpy as jnp
        import numpy as np
        B, S, E = (2, 512, 128)
        H, DQK, DV = (16, 64, 64)
        ROPE_BASE = 10000.0

        def _rope(t):
            D = t.shape[-1]
            inv_freq = 1.0 / ROPE_BASE ** (jnp.arange(0, D, 2, dtype=jnp.float32) / D)
            pos = jnp.arange(t.shape[2], dtype=jnp.float32)
            ang = pos[:, None] * inv_freq[None, :]
            cos = jnp.cos(ang)[None, None]
            sin = jnp.sin(ang)[None, None]
            t1, t2 = (t[..., :D // 2], t[..., D // 2:])
            return jnp.concatenate([t1 * cos - t2 * sin, t1 * sin + t2 * cos], axis=-1)
        key = jax.random.key(seed)
        ks = jax.random.split(key, 4)
        sE = 1.0 / np.sqrt(E)
        sV = 1.0 / np.sqrt(H * DV)
        return {'x': jax.random.normal(ks[0], (B, S, E), jnp.float32), 'Wq': jax.random.normal(ks[1], (E, H * DQK), jnp.float32) * sE, 'bq': jnp.zeros((H * DQK,), jnp.float32), 'Wkv': jax.random.normal(ks[2], (E, H * (DQK + DV)), jnp.float32) * sE, 'bkv': jnp.zeros((H * (DQK + DV),), jnp.float32), 'Wo': jax.random.normal(ks[3], (H * DV, E), jnp.float32) * sV, 'bo': jnp.zeros((E,), jnp.float32)}
    _L0_attn_in = _L0_attn_setup()

    def _L0_ffn_setup():
        import jax, jax.numpy as jnp
        import numpy as np
        HIDDEN = 128
        INTER = 512
        N_EXPERTS = 8

        def geglu(x, w1, w2, w3):
            return jax.nn.gelu(x @ w1, approximate=False) * (x @ w2) @ w3
        key = jax.random.key(seed)
        ks = jax.random.split(key, 8)
        s = 0.02
        x = jax.random.normal(ks[0], (2, 256, HIDDEN), dtype=jnp.float32)
        w1s = jax.random.normal(ks[1], (HIDDEN, INTER), dtype=jnp.float32) * s
        w2s = jax.random.normal(ks[2], (HIDDEN, INTER), dtype=jnp.float32) * s
        w3s = jax.random.normal(ks[3], (INTER, HIDDEN), dtype=jnp.float32) * s
        W1 = jax.random.normal(ks[4], (N_EXPERTS, HIDDEN, INTER), dtype=jnp.float32) * s
        W2 = jax.random.normal(ks[5], (N_EXPERTS, HIDDEN, INTER), dtype=jnp.float32) * s
        W3 = jax.random.normal(ks[6], (N_EXPERTS, INTER, HIDDEN), dtype=jnp.float32) * s
        Wg = jax.random.normal(ks[7], (HIDDEN, N_EXPERTS), dtype=jnp.float32) * s
        return {'x': x, 'w1s': w1s, 'w2s': w2s, 'w3s': w3s, 'W1': W1, 'W2': W2, 'W3': W3, 'Wg': Wg}
    _L0_ffn_in = _L0_ffn_setup()
    _d = {'L0_attn_x': _L0_attn_in['x'], 'L0_attn_Wq': _L0_attn_in['Wq'], 'L0_attn_bq': _L0_attn_in['bq'], 'L0_attn_Wkv': _L0_attn_in['Wkv'], 'L0_attn_bkv': _L0_attn_in['bkv'], 'L0_attn_Wo': _L0_attn_in['Wo'], 'L0_attn_bo': _L0_attn_in['bo'], 'L0_ffn_w1s': _L0_ffn_in['w1s'], 'L0_ffn_w2s': _L0_ffn_in['w2s'], 'L0_ffn_w3s': _L0_ffn_in['w3s'], 'L0_ffn_W1': _L0_ffn_in['W1'], 'L0_ffn_W2': _L0_ffn_in['W2'], 'L0_ffn_W3': _L0_ffn_in['W3'], 'L0_ffn_Wg': _L0_ffn_in['Wg']}
    _x0 = _d['L0_attn_x']
    _d['L0_attn_x'] = jax.random.normal(jax.random.fold_in(jax.random.key(seed), 1), (8, 512, 128), dtype=_x0.dtype)
    del _x0
    return _d

def reference(L0_attn_x, L0_attn_Wq, L0_attn_bq, L0_attn_Wkv, L0_attn_bkv, L0_attn_Wo, L0_attn_bo, L0_ffn_w1s, L0_ffn_w2s, L0_ffn_w3s, L0_ffn_W1, L0_ffn_W2, L0_ffn_W3, L0_ffn_Wg):

    def _L0_attn_ref(x, Wq, bq, Wkv, bkv, Wo, bo):
        import jax, jax.numpy as jnp
        import numpy as np
        B, S, E = (2, 512, 128)
        H, DQK, DV = (16, 64, 64)
        ROPE_BASE = 10000.0

        def _rope(t):
            D = t.shape[-1]
            inv_freq = 1.0 / ROPE_BASE ** (jnp.arange(0, D, 2, dtype=jnp.float32) / D)
            pos = jnp.arange(t.shape[2], dtype=jnp.float32)
            ang = pos[:, None] * inv_freq[None, :]
            cos = jnp.cos(ang)[None, None]
            sin = jnp.sin(ang)[None, None]
            t1, t2 = (t[..., :D // 2], t[..., D // 2:])
            return jnp.concatenate([t1 * cos - t2 * sin, t1 * sin + t2 * cos], axis=-1)
        b, s, e = x.shape
        q = x @ Wq + bq
        kv = x @ Wkv + bkv
        k, v = jnp.split(kv, [H * DQK], axis=-1)
        q = _rope(q.reshape(b, s, H, DQK).transpose(0, 2, 1, 3))
        k = _rope(k.reshape(b, s, H, DQK).transpose(0, 2, 1, 3))
        v = v.reshape(b, s, H, DV).transpose(0, 2, 1, 3)
        scores = jnp.einsum('bhqd,bhkd->bhqk', q, k) * (1.0 / np.sqrt(DQK))
        causal = jnp.tril(jnp.ones((s, s), dtype=bool))
        scores = jnp.where(causal[None, None], scores, -jnp.inf)
        probs = jax.nn.softmax(scores, axis=-1)
        out = jnp.einsum('bhqk,bhkd->bhqd', probs, v)
        out = out.transpose(0, 2, 1, 3).reshape(b, s, H * DV)
        return out @ Wo + bo

    def _L0_ffn_ref(x, w1s, w2s, w3s, W1, W2, W3, Wg):
        import jax, jax.numpy as jnp
        import numpy as np
        HIDDEN = 128
        INTER = 512
        N_EXPERTS = 8

        def geglu(x, w1, w2, w3):
            return jax.nn.gelu(x @ w1, approximate=False) * (x @ w2) @ w3
        B, T, C = x.shape
        xf = x.reshape(-1, C)
        shared = geglu(xf, w1s, w2s, w3s)
        logits = xf @ Wg
        idx = jnp.argmax(logits, axis=-1)
        final = jnp.zeros_like(xf)
        for e in range(N_EXPERTS):
            y = geglu(xf, W1[e], W2[e], W3[e])
            final = final + jnp.where((idx == e)[:, None], y, 0.0)
        return (shared + final).reshape(B, T, C)
    x = L0_attn_x
    x = x + _L0_attn_ref(_layernorm(x, axis=-1), L0_attn_Wq, L0_attn_bq, L0_attn_Wkv, L0_attn_bkv, L0_attn_Wo, L0_attn_bo)
    x = x + _L0_ffn_ref(_layernorm(x, axis=-1), L0_ffn_w1s, L0_ffn_w2s, L0_ffn_w3s, L0_ffn_W1, L0_ffn_W2, L0_ffn_W3, L0_ffn_Wg)
    return x

_drawn_inputs = setup_inputs


def setup_inputs(seed=0):
    import zlib

    import numpy as np

    out = dict(_drawn_inputs(seed))
    spreads = {'L0_attn_bq': (0.0, 0.572), 'L0_attn_bkv': (0.0, 0.1), 'L0_attn_bo': (0.0, 0.1)}
    factors = {'L0_ffn_w1s': 4.883,
     'L0_ffn_w2s': 4.801,
     'L0_ffn_w3s': 4.781,
     'L0_ffn_W1': 4.877,
     'L0_ffn_W2': 4.804,
     'L0_ffn_W3': 4.81,
     'L0_ffn_Wg': 5.125}
    for name, (base, spread) in spreads.items():
        noise = np.random.default_rng([zlib.crc32(name.encode()), seed]).standard_normal(out[name].shape)
        drawn = base * np.exp(spread * noise) if base else spread * noise
        out[name] = jnp.asarray(drawn.astype(out[name].dtype))
    for name, factor in factors.items():
        out[name] = (out[name] * factor).astype(out[name].dtype)
    return out
```

```python
from contextlib import ExitStack

import concourse.bass as bass
from concourse import mybir

F32 = mybir.dt.float32
F32R = mybir.dt.float32r
BF16 = mybir.dt.bfloat16
F16 = mybir.dt.float16
U32 = mybir.dt.uint32
I32 = mybir.dt.int32
ALU = mybir.AluOpType
ACT = mybir.ActivationFunctionType
AX_X = mybir.AxisListType.X

P = 128
BATCH, SEQ, EMB = 8, 512, 128
HEADS, DHEAD = 16, 64
HALF = DHEAD // 2
GROUP = P // HALF
GROUPS = HEADS // GROUP
QT = SEQ // P
UNITS = [[(0, 0), (1, 0), (1, 1)], [(2, k) for k in range(3)], [(3, k) for k in range(4)]]
NU = len(UNITS)
STEPS = GROUP * NU
BSTEPS = GROUPS * STEPS
GW = GROUP * DHEAD
TILES = BATCH * QT
EPS = 1e-5
EXPERTS, INTER = 8, 512
TOKENS = BATCH * SEQ
ROW = EMB + 1
NOBODY = TOKENS
RTILES = TILES + EXPERTS
SLOTS = RTILES * P
CHUNK = INTER // P
RING = 8
AHEAD = 2
NEG = -1e30

KA, KB, QA, QB, OT0, OT1, V01, V23, WO, BACK, LNT, LN2, LG = range(13)
SLOT_OF = {KA: 0, KB: 1, QA: 2, QB: 3, OT0: 4, OT1: 5, V01: 6, V23: 7, WO: 8, BACK: 10, LNT: 10, LN2: 9, LG: 11}
FIRST_CHUNKS = 8


def chunks_of(hg, last=False):
    if last and hg == GROUPS - 1:
        return [OT0, OT1, WO]
    extra = {0: [BACK], 1: [LN2, LG], 2: [] if last else [LNT]}.get(hg, [])
    return [KA, KB, QA, QB, OT0, OT1, V01, V23, WO] + extra


def chunks_before(hg, kind, last=False):
    return sum(len(chunks_of(i, last)) for i in range(hg)) + chunks_of(hg, last).index(kind)


CHUNKS_PER_BATCH = sum(len(chunks_of(i)) for i in range(GROUPS))


def attention(nc, ctx, x, wqk, wv, wo, bqk, bv, bo, tables, x_res, xn2, logits, xt2_all, zeros_to):
    def sb(name, shape, dt):
        return ctx.enter_context(nc.sbuf_tensor(name, shape, dt))

    def sem(name):
        return ctx.enter_context(nc.semaphore(name))

    NG = GROUPS
    wqk_hi = sb("wqk_hi", [P, NG, 4, P], F32R)
    wqk_lo = sb("wqk_lo", [P, NG, 4, P], F32R)
    wv_hi = sb("wv_hi", [P, NG, GW], F32R)
    wv_lo = sb("wv_lo", [P, NG, GW], F32R)
    wo_s = sb("wo_s", [P, 2 * NG, EMB], F32)
    rope = sb("rope", [P, 2, 2, 2, SEQ], F32)
    bqk_s = sb("bqk_s", [P, NG, 4], F32)
    bv_s = sb("bv_s", [P, 2 * NG], F32)
    bo_s = sb("bo_s", [P, 1], F32)
    ident = sb("ident", [P, P], F32)
    ident_b = sb("ident_b", [P, P], BF16)
    causal = sb("causal", [P, P], BF16)
    zero_row = sb("zero_row", [P, ROW], F32)
    bias_col = sb("bias_col", [P, 1], F32)
    acc = sb("acc", [P, SEQ], F32)
    stats = sb("stats", [P, QT, 6], F32)
    mv = sb("mv", [P, QT, 2], F32)
    veps = sb("veps", [P, QT], F32)
    mhalf = sb("mhalf", [P, QT], F32)
    wait_pad = sb("wait_pad", [P, 1], F32)
    rstd = sb("rstd", [P, QT], F32)
    xn = sb("xn", [P, QT, EMB], F32)
    stats2 = sb("stats2", [P, QT, 6], F32)
    mv2 = sb("mv2", [P, QT, 2], F32)
    veps2 = sb("veps2", [P, QT], F32)
    rstd2 = sb("rstd2", [P, QT], F32)
    xn2_t = sb("xn2_t", [P, QT, EMB], F32)
    xt2 = sb("xt2", [P, SEQ], F32)
    wg_s = sb("wg_s", [P, EXPERTS], F32)
    xt_hi = sb("xt_hi", [P, SEQ], F32R)
    xt_lo = sb("xt_lo", [P, SEQ], F32R)
    prod = sb("prod", [P, 2, 2, 2, SEQ], F32)
    rot = sb("rot", [P, 2, 2, SEQ], F32)
    halves = sb("halves", [P, 2, 4, SEQ], F32R)
    stack = [sb(f"stack{h}", [P, 3, SEQ], F32R) for h in range(GROUP)]
    v_parts = sb("v_parts", [P, 2, 3, QT, GW], BF16)
    v_rest = sb("v_rest", [P, 2, 2 * GW], F32)
    probs = [sb(f"probs{u}", [P, len(UNITS[u]) * P], F32) for u in range(NU)]
    pt_hi = [sb(f"pt_hi{u}", [P, len(UNITS[u]), P], F16) for u in range(NU)]
    pt_lo = [sb(f"pt_lo{u}", [P, len(UNITS[u]), P], F16) for u in range(NU)]
    negmax = sb("negmax", [P, 2, QT, GROUP], F32)
    rowsum = sb("rowsum", [P, 2, QT, GROUP], F32)
    recip = sb("recip", [P, QT, GROUP], F32)
    o_sb = sb("o_sb", [P, QT, GW], F32)
    ot = sb("ot", [P, 2, QT, P], F32)

    with ExitStack() as pctx:
        ps_s = pctx.enter_context(nc.psum_tensor("ps_s", [P, 3, 512], F32))
        ps_pt = pctx.enter_context(nc.psum_tensor("ps_pt", [P, 2, 512], F32))
        ps_o = pctx.enter_context(nc.psum_tensor("ps_o", [P, 2, 2, GW], F32))
        ps_m = pctx.enter_context(nc.psum_tensor("ps_m", [P, 512], F32))

        in_w = sem("in_w")
        in_x0 = sem("in_x0")
        in_x = sem("in_x")
        filled = sem("filled")
        const = sem("const")
        wsplit_hi = sem("wsplit_hi")
        wsplit = sem("wsplit")
        ln = sem("ln")
        ln_rstd = sem("ln_rstd")
        xt_h = sem("xt_h")
        xt_l = sem("xt_l")
        chunk = sem("chunk")
        biased = sem("biased")
        ln2 = sem("ln2")
        xn2_saved = sem("xn2_saved")
        xt2_saved = sem("xt2_saved")
        ln2_rstd = sem("ln2_rstd")
        xt2d = sem("xt2d")
        lgd = sem("lgd")
        rmul = sem("rmul")
        radd = sem("radd")
        rhi = sem("rhi")
        rlo = sem("rlo")
        stacked = [sem(f"stacked{h}") for h in range(GROUP)]
        v1 = sem("v1")
        vr = sem("vr")
        v2 = sem("v2")
        v3 = sem("v3")
        scored = sem("scored")
        maxed = sem("maxed")
        expd = sem("expd")
        turned = sem("turned")
        pthi = sem("pthi")
        ptlo = sem("ptlo")
        pvd = sem("pvd")
        zeroed = sem("zeroed")
        rec = sem("rec")
        normed = sem("normed")
        otd = sem("otd")
        added = sem("added")
        resd = sem("resd")
        block = pctx.enter_context(nc.Block())

        def tiles_of(u):
            blocks = UNITS[u]
            return [(i, slice(P * min(n for n, b in enumerate(blocks) if b[0] == i),
                              P * (1 + max(n for n, b in enumerate(blocks) if b[0] == i))))
                    for i in sorted({b[0] for b in blocks})]

        def place(j):
            return j % NU, (j % STEPS) // NU, (j // STEPS) % 2

        @block.sync
        def _(sp):
            xr = x.rearrange("b (t p) e -> p (b t) e", p=P)
            sp.dma_start(x_res[:, QT:2 * QT, :], xr[:, 0:QT, :]).then_inc(in_x0, 16)
            raw = prod[:, :, :, :, :].rearrange("p a b c s -> p (a b c s)")
            sp.dma_start(raw[:, 0:4 * NG * P], wqk).then_inc(in_w, 16)
            sp.dma_start(raw[:, 4 * NG * P:4 * NG * P + NG * GW], wv).then_inc(in_w, 16)
            sp.dma_start(wo_s[:, :, :].rearrange("p g m -> p (g m)"), wo).then_inc(in_w, 16)
            sp.dma_start(ident[:, :], tables["ident"]).then_inc(in_w, 16)
            sp.dma_start(bqk_s[:, :, :], bqk).then_inc(in_w, 16)
            sp.dma_start(bv_s[:, :], bv).then_inc(in_w, 16)
            sp.dma_start(bo_s[:, :], bo.rearrange("(e o) -> e o", o=1)).then_inc(in_w, 16)
            sp.dma_start(ident_b[:, :], tables["ident_b"]).then_inc(in_w, 16)
            sp.dma_start(causal[:, :], tables["causal"]).then_inc(in_w, 16)
            sp.dma_start(rope[:, :, :, :, :], tables["rope"]).then_inc(in_w, 16)
            sp.dma_start(wg_s[:, :], tables["wg"]).then_inc(in_w, 16)
            sp.dma_start(x_res[:, 2 * QT:, :], xr[:, QT:, :]).then_inc(in_x, 16)

            def stack_head(G, h):
                used = STEPS * (G - 1) + NU * (h + 1)
                if not isinstance(G, int):
                    used = sp.snap(used)
                if h == 0:
                    sp.wait_ge(rlo, 2 * G + 2)
                if not isinstance(G, int) or G > 0:
                    sp.wait_ge(scored, used)
                for ab in range(2):
                    src = halves[HALF * h:HALF * (h + 1), ab, :, :].bitcast(F32)
                    dst = stack[h][HALF * ab:HALF * (ab + 1), :, :].bitcast(F32)
                    sp.dma_start(dst, src[:, 0:3, :]).then_inc(stacked[h], 16)
                    low = stack[h][2 * HALF + HALF * ab:2 * HALF + HALF * (ab + 1), :, :].bitcast(F32)
                    back = bass.AP(tensor=src.tensor, offset=src.offset + 3 * SEQ,
                                   ap=[list(src.ap[0]), [-SEQ, 3], [1, SEQ]])
                    sp.dma_start(low, back).then_inc(stacked[h], 16)

            def save_xn2(b):
                dst = xn2[:, bass.ds(b * QT, QT), 0:EMB] if isinstance(b, int) else xn2_slot(b)
                x_off = b * (P * SEQ) if isinstance(b, int) else sp.snap(b * (P * SEQ))
                sp.wait_ge(ln2, 13 * b + 13)
                sp.dma_start(dst, xn2_t[:, :, :]).then_inc(xn2_saved, 16)
                x_dst = bass.AP(tensor=xt2_all.tensor, offset=x_off, ap=[[SEQ, P], [1, SEQ]])
                sp.wait_ge(xt2d, b + 1)
                sp.dma_start(x_dst, xt2[:, :]).then_inc(xt2_saved, 16)

            def xn2_slot(b):
                full = xn2[:, 0:QT, 0:EMB]
                return bass.AP(tensor=full.tensor, offset=sp.snap(b * (QT * ROW)), ap=[list(a) for a in full.ap])

            def batch(b, last):
                for hg in range(NG - 1 if last else NG):
                    for h in range(GROUP):
                        stack_head(NG * b + hg + 1, h)
                    if hg == 1:
                        save_xn2(b)

            sp.wait_ge(const, 6)
            sp.dma_start(zeros_to, zero_row[:, :].rearrange("p (o r) -> p o r", o=1).broadcast_to([P, SLOTS // P, ROW])).then_inc(filled, 16)
            sp.sem_inc(xn2_saved, 16)
            sp.sem_inc(xt2_saved, 16)
            for h in range(GROUP):
                stack_head(0, h)
            with sp.Fori(0, BATCH - 1) as b:
                batch(b, False)
            batch(BATCH - 1, True)
            save_xn2(BATCH)
            for sm, v in ((xn2_saved, 16 * (BATCH + 2)), (xt2_saved, 16 * (BATCH + 2)), (filled, 16)):
                sp.wait_ge(sm, v)

        @block.gpsimd
        def _(pool):
            nc.gpsimd.memset(mhalf[:, :], -0.5).then_inc(const, 1)
            nc.gpsimd.memset(acc[:, :], 0.0).then_inc(const, 1)
            nc.gpsimd.memset(o_sb[:, :, :], 0.0).then_inc(const, 1)
            nc.gpsimd.memset(x_res[:, 0:QT, :], 0.0).then_inc(const, 1)
            nc.gpsimd.memset(zero_row[:, 0:EMB], 0.0).then_inc(const, 1)
            nc.gpsimd.memset(zero_row[:, EMB:ROW].bitcast(mybir.dt.uint32), NOBODY).then_inc(const, 1)
            pool.wait_ge(const, 4)

            def rstd_of(b):
                pool.wait_ge(ln, 13 * b + 9)
                nc.gpsimd.tensor_tensor(rstd[:, :], veps[:, :], mhalf[:, :], ALU.pow).then_inc(ln_rstd, 1)

            def rstd2_of(b):
                pool.wait_ge(ln2, 13 * b + 9)
                nc.gpsimd.tensor_tensor(rstd2[:, :], veps2[:, :], mhalf[:, :], ALU.pow).then_inc(ln2_rstd, 1)

            def rotate(G, kq, first):
                pool.wait_ge(rmul, 4 * G + 2 * kq + 2)
                if not first:
                    pool.wait_ge(rlo, 2 * (G - 1) + kq + 1)
                nc.gpsimd.tensor_tensor(rot[:, kq, :, :], prod[:, kq, 0, :, :], prod[:, kq, 1, :, :],
                                        ALU.add).then_inc(radd, 1)

            def v_third(G, c, par):
                vp = v_parts[:, par, :, 2 * c:2 * c + 2, :].rearrange("p k t d -> p k (t d)")
                pool.wait_ge(v2, 2 * G + c + 1)
                nc.gpsimd.tensor_tensor(vp[:, 2, :], v_rest[:, c, :], vp[:, 1, :], ALU.subtract).then_inc(v3, 1)

            def k_low(G):
                pool.wait_ge(rhi, 2 * G + 1)
                nc.gpsimd.tensor_tensor(halves[:, :, 3, :], rot[:, 0, :, :], halves[:, :, 0, :].bitcast(F32),
                                        ALU.subtract).then_inc(rlo, 1)

            def q_low(G):
                pool.wait_ge(rhi, 2 * G + 2)
                nc.gpsimd.tensor_tensor(halves[:, :, 2, :], rot[:, 1, :, :], halves[:, :, 1, :].bitcast(F32),
                                        ALU.subtract).then_inc(rlo, 1)

            def group_work(G, par, first, norm_of=None):
                rotate(G, 0, first)
                rotate(G, 1, first)
                k_low(G)
                q_low(G)
                if norm_of is not None:
                    norm_of()
                for c in range(2):
                    v_third(G, c, par)

            def batch(b, last):
                for hg in range(NG):
                    if not (last and hg == NG - 1):
                        group_work(NG * b + hg + 1, (hg + 1) % 2, False, {1: lambda: rstd2_of(b), 2: lambda: rstd_of(b + 1)}.get(hg if not last or hg == 1 else None))

            rstd_of(0)
            pool.wait_ge(wsplit, 2)
            group_work(0, 0, True)
            with pool.Fori(0, BATCH - 1) as b:
                batch(b, False)
            batch(BATCH - 1, True)
            rstd2_of(BATCH)

        @block.scalar
        def _(act):
            act.sem_inc(expd, 3)
            act.wait_ge(in_w, 176)
            raw = prod[:, :, :, :, :].rearrange("p a b c s -> p (a b c s)")
            nqk = 4 * NG * P
            nc.scalar.copy(wqk_hi[:, :, :, :].rearrange("p g k m -> p (g k m)"), raw[:, 0:nqk]).then_inc(wsplit_hi, 1)
            nc.scalar.copy(wv_hi[:, :, :].rearrange("p g m -> p (g m)"), raw[:, nqk:nqk + NG * GW]).then_inc(wsplit_hi, 1)

            def xt_high(b, m):
                act.wait_ge(chunk, m + 1)
                nc.scalar.copy(xt_hi[:, :], ps_m[:, :]).then_inc(xt_h, 1)

            def xt2_copy(b, m):
                act.wait_ge(chunk, m + 1)
                act.wait_ge(xt2_saved, 16 * b + 16)
                nc.scalar.copy(xt2[:, :], ps_m[:, :]).then_inc(xt2d, 1)

            def high(G, kq, first):
                act.wait_ge(radd, 2 * G + kq + 1)
                if not first:
                    for h in range(GROUP):
                        act.wait_ge(stacked[h], 64 * G)
                nc.scalar.copy(halves[:, :, kq, :], rot[:, kq, :, :]).then_inc(rhi, 1)

            def v_first(G, c, par, m, first):
                act.wait_ge(chunk, m + 1)
                if not first:
                    act.wait_ge(pvd, STEPS * (G - 1) + 3)
                nc.scalar.copy(v_parts[:, par, 0, 2 * c:2 * c + 2, :].rearrange("p t d -> p (t d)"),
                               ps_m[:, :]).then_inc(v1, 1)

            def exp(n, j):
                u, h, par = place(j)
                act.wait_ge(maxed, n + 1)
                act.wait_ge(turned, n + 1)
                for i, cols in tiles_of(u):
                    last = nc.scalar.activation(probs[u][:, cols], ps_s[:, u, cols], ACT.Exp, bias=negmax[:, par, i, h:h + 1],
                                                accum_out=rowsum[:, par, i, h:h + 1])
                last.then_inc(expd, 1)

            def pt_high(n, j):
                u = j % NU
                act.wait_ge(turned, n + 4)
                act.wait_ge(pvd, n + 1)
                nc.scalar.copy(pt_hi[u][:, :, :].rearrange("p k q -> p (k q)"),
                               ps_pt[:, j % 2, 0:len(UNITS[u]) * P]).then_inc(pthi, 1)

            def ot_copy(c, m):
                act.wait_ge(chunk, m + 1)
                nc.scalar.copy(ot[:, :, 2 * c:2 * c + 2, :].rearrange("p f t q -> p f (t q)"),
                               ps_m[:, :].rearrange("p (f q) -> p f q", f=2)).then_inc(otd, 1)

            def v_second(G, c, par):
                act.wait_ge(vr, 2 * G + c + 1)
                nc.scalar.copy(v_parts[:, par, 1, 2 * c:2 * c + 2, :].rearrange("p t d -> p (t d)"),
                               v_rest[:, c, :]).then_inc(v2, 1)

            def batch(b, last):
                for hg in range(NG):
                    m0 = FIRST_CHUNKS + CHUNKS_PER_BATCH * b
                    tail = last and hg == NG - 1
                    G = NG * b + hg + 1
                    for t in range(STEPS):
                        j = STEPS * hg + t
                        if not (last and j + 2 >= BSTEPS):
                            exp(BSTEPS * b + j + 2, j + 2)
                        if not (last and j + 1 >= BSTEPS):
                            pt_high(BSTEPS * b + j + 1, j + 1)
                        for c in range(2):
                            if t == SLOT_OF[(OT0, OT1)[c]]:
                                ot_copy(c, m0 + chunks_before(hg, OT0 + c, last))
                        if not tail:
                            for c in range(2):
                                if t == SLOT_OF[(V01, V23)[c]]:
                                    v_first(G, c, (hg + 1) % 2, m0 + chunks_before(hg, (V01, V23)[c]), False)
                                if t == SLOT_OF[(V01, V23)[c]] + 1:
                                    v_second(G, c, (hg + 1) % 2)
                            if t == 3:
                                high(G, 0, False)
                            if t == 5:
                                high(G, 1, False)
                        if hg == 1 and t == SLOT_OF[LN2]:
                            xt2_copy(b, m0 + chunks_before(hg, LN2))
                        if hg == 2 and not last and t == SLOT_OF[LNT]:
                            xt_high(b + 1, m0 + chunks_before(hg, LNT))

            xt_high(0, 1)
            act.wait_ge(wsplit, 2)
            for c in range(2):
                v_first(0, c, 0, 6 + c, True)
                v_second(0, c, 0)
            high(0, 0, True)
            high(0, 1, True)
            exp(0, 0)
            exp(1, 1)
            pt_high(0, 0)
            with act.Fori(0, BATCH - 1) as b:
                batch(b, False)
            batch(BATCH - 1, True)
            m_end = FIRST_CHUNKS + CHUNKS_PER_BATCH * (BATCH - 1) + chunks_before(NG - 1, WO, True) + 1
            for c in range(2):
                ot_copy(c, m_end + c)
            xt2_copy(BATCH, m_end + 4)

        @block.vector
        def _(dve):
            dve.sem_inc(ptlo, 2)
            dve.sem_inc(normed, 1)
            dve.sem_inc(added, 1)
            nc.vector.memset(ps_o[:, 1, :, :], 0.0).then_inc(zeroed, 1)
            nc.vector.memset(recip[:, :, :], 1.0).then_inc(zeroed, 1)
            dve.wait_ge(zeroed, 2)

            def ln_stats(slot, n, stats, mv, veps, ln):
                xs = x_res[:, bass.ds(slot * QT, QT), :]
                for t in range(QT):
                    nc.vector.bn_stats(stats[:, t, :], xs[:, t, :]).then_inc(ln, 1)
                dve.wait_ge(ln, 13 * n + 4)
                nc.vector.memset(wait_pad[:, :], 0.0)
                for t in range(QT):
                    nc.vector.bn_aggr(mv[:, t, :], stats[:, t, :]).then_inc(ln, 1)
                dve.wait_ge(ln, 13 * n + 8)
                nc.vector.tensor_scalar(veps[:, :], mv[:, :, 1], EPS, None, ALU.add).then_inc(ln, 1)

            def ln_apply(slot, n, out, mv, rstd, ln, ln_rstd):
                dve.wait_ge(ln_rstd, n + 1)
                xs = x_res[:, bass.ds(slot * QT, QT), :]
                for t in range(QT):
                    nc.vector.tensor_scalar(out[:, t, :], xs[:, t, :], mv[:, t, 0:1], rstd[:, t:t + 1],
                                            ALU.subtract, ALU.mult).then_inc(ln, 1)

            def take_logits(b, m):
                dve.wait_ge(chunk, m + 1)
                nc.vector.tensor_copy(logits[:, bass.ds(b * QT, QT), :].rearrange("p t e -> p (t e)"),
                                      ps_m[:, 0:QT * EXPERTS]).then_inc(lgd, 1)

            def xt_low(b, m):
                dve.wait_ge(xt_h, b + 1)
                nc.vector.tensor_tensor(xt_lo[:, :], ps_m[:, :], xt_hi[:, :].bitcast(F32), ALU.subtract).then_inc(xt_l, 1)

            def products(G, kind, hg, m, first):
                kq, ab = kind // 2, kind % 2
                dve.wait_ge(chunk, m + 1)
                if not first:
                    dve.wait_ge(radd, 2 * (G - 1) + kq + 1)
                nc.vector.scalar_tensor_tensor(
                    out=prod[:, kq, ab, :, :], in0=ps_m[:, :].rearrange("p (o s) -> p o s", o=1).broadcast_to([P, 2, SEQ]),
                    scalar=bqk_s[:, hg, kind:kind + 1], in1=rope[:, kq, ab, :, :],
                    op0=ALU.add, op1=ALU.mult).then_inc(rmul, 1)

            def v_remainder(G, c, par, first):
                dve.wait_ge(v1, 2 * G + c + 1)
                if not first:
                    dve.wait_ge(v3, 2 * (G - 1) + c + 1)
                vp = v_parts[:, par, :, 2 * c:2 * c + 2, :].rearrange("p k t d -> p k (t d)")
                nc.vector.tensor_tensor(v_rest[:, c, :], ps_m[:, :], vp[:, 0, :], ALU.subtract).then_inc(vr, 1)

            def rowmax(n, j):
                u, h, par = place(j)
                dve.wait_ge(scored, n + 1)
                for i, cols in tiles_of(u):
                    last = nc.vector.tensor_reduce(negmax[:, par, i, h:h + 1], ps_s[:, u, cols], AX_X, ALU.max, negate=True)
                last.then_inc(maxed, 1)

            def pt_low(n, j):
                u = j % NU
                dve.wait_ge(pthi, n + 1)
                nc.vector.tensor_tensor(pt_lo[u][:, :, :].rearrange("p k q -> p (k q)"), ps_pt[:, j % 2, 0:len(UNITS[u]) * P],
                                        pt_hi[u][:, :, :].rearrange("p k q -> p (k q)"), ALU.subtract).then_inc(ptlo, 1)

            def reciprocals(g, par):
                dve.wait_ge(expd, STEPS * g + STEPS + 3)
                nc.vector.reciprocal(recip[:, :, :], rowsum[:, par, :, :]).then_inc(rec, 1)
                dve.wait_ge(rec, g + 1)

            def normalise(g, c):
                dve.wait_ge(pvd, STEPS * g + (STEPS - NU + 1 if c == 0 else STEPS) + 3)
                nc.vector.tensor_tensor(
                    o_sb[:, 2 * c:2 * c + 2, :].rearrange("p t (h d) -> p (t h) d", d=DHEAD),
                    ps_o[:, c, :, :].rearrange("p t (h d) -> p (t h) d", d=DHEAD),
                    recip[:, 2 * c:2 * c + 2, :].rearrange("p t h -> p (t h)").unsqueeze(2).broadcast_to([P, 2 * GROUP, DHEAD]),
                    ALU.mult).then_inc(normed, 1)

            def accumulate(hg, ordinal, m):
                dve.wait_ge(chunk, m + 1)
                if hg == 0:
                    nc.vector.tensor_scalar(acc[:, :], ps_m[:, :], bias_col[:, :], None, ALU.add).then_inc(added, 1)
                else:
                    dve.wait_ge(added, ordinal + 1)
                    nc.vector.tensor_tensor(acc[:, :], ps_m[:, :], acc[:, :], ALU.add).then_inc(added, 1)

            def residual(slot, m):
                dve.wait_ge(chunk, m + 1)
                xs = x_res[:, bass.ds(slot * QT, QT), :].rearrange("p t e -> p (t e)")
                nc.vector.tensor_tensor(xs, ps_m[:, :], xs, ALU.add).then_inc(resd, 1)

            def batch(b, last):
                m0 = FIRST_CHUNKS + CHUNKS_PER_BATCH * b
                for hg in range(NG):
                    tail = last and hg == NG - 1
                    g = NG * b + hg
                    for t in range(STEPS):
                        j = STEPS * hg + t
                        if t == 0:
                            normalise(g - 1, 1)
                        if not (last and j + 3 >= BSTEPS):
                            rowmax(BSTEPS * b + j + 3, j + 3)
                        if not (last and j + 1 >= BSTEPS):
                            pt_low(BSTEPS * b + j + 1, j + 1)
                        if not tail and t < 4:
                            products(g + 1, t, (hg + 1) % NG, m0 + chunks_before(hg, t), False)
                        if not tail:
                            for c in range(2):
                                if t == SLOT_OF[(V01, V23)[c]]:
                                    v_remainder(g + 1, c, (hg + 1) % 2, False)
                        if t == SLOT_OF[WO]:
                            accumulate((hg + NG - 1) % NG, g, m0 + chunks_before(hg, WO, last))
                        if hg == 0 and t == SLOT_OF[BACK]:
                            residual(b, m0 + chunks_before(hg, BACK))
                        if hg == 1:
                            if t == 2:
                                dve.wait_ge(resd, b + 1)
                                nc.vector.memset(wait_pad[:, :], 0.0)
                                ln_stats(b, b, stats2, mv2, veps2, ln2)
                            if t == 7:
                                dve.wait_ge(xn2_saved, 16 * b + 16)
                                ln_apply(b, b, xn2_t, mv2, rstd2, ln2, ln2_rstd)
                            if t == SLOT_OF[LG]:
                                take_logits(b, m0 + chunks_before(hg, LG))
                        if hg == 2 and not last:
                            if t == 4:
                                ln_stats(b + 2, b + 1, stats, mv, veps, ln)
                            if t == 10:
                                ln_apply(b + 2, b + 1, xn, mv, rstd, ln, ln_rstd)
                                xt_low(b + 1, 0)
                        if t == STEPS - 1:
                            reciprocals(g, hg % 2)
                            normalise(g, 0)

            raw = prod[:, :, :, :, :].rearrange("p a b c s -> p (a b c s)")
            nqk = 4 * NG * P
            dve.wait_ge(in_x0, 16)
            ln_stats(1, 0, stats, mv, veps, ln)
            dve.wait_ge(in_w, 176)
            for w, (lo, hi, src) in enumerate((
                    (wqk_lo[:, :, :, :].rearrange("p g k m -> p (g k m)"), wqk_hi[:, :, :, :].rearrange("p g k m -> p (g k m)"), raw[:, 0:nqk]),
                    (wv_lo[:, :, :].rearrange("p g m -> p (g m)"), wv_hi[:, :, :].rearrange("p g m -> p (g m)"), raw[:, nqk:nqk + NG * GW]))):
                dve.wait_ge(wsplit_hi, w + 1)
                nc.vector.tensor_tensor(lo, src, hi.bitcast(F32), ALU.subtract).then_inc(wsplit, 1)
            dve.wait_ge(chunk, 1)
            nc.vector.tensor_tensor(bias_col[:, :], ps_m[:, 0:1], bo_s[:, :], ALU.add).then_inc(biased, 1)
            ln_apply(1, 0, xn, mv, rstd, ln, ln_rstd)
            dve.wait_ge(biased, 1)
            xt_low(0, 1)
            dve.wait_ge(wsplit, 2)
            for k in range(4):
                products(0, k, 0, 2 + k, True)
            for c in range(2):
                v_remainder(0, c, 0, True)
            for n in range(3):
                rowmax(n, n)
            pt_low(0, 0)
            dve.wait_ge(in_x, 16)
            with dve.Fori(0, BATCH - 1) as b:
                batch(b, False)
            batch(BATCH - 1, True)
            normalise(NG * BATCH - 1, 1)
            m_end = FIRST_CHUNKS + CHUNKS_PER_BATCH * (BATCH - 1) + chunks_before(NG - 1, WO, True) + 1
            accumulate(NG - 1, NG * BATCH, m_end + 2)
            residual(BATCH, m_end + 3)
            dve.wait_ge(resd, BATCH + 1)
            ln_stats(BATCH, BATCH, stats2, mv2, veps2, ln2)
            dve.wait_ge(xn2_saved, 16 * BATCH + 16)
            ln_apply(BATCH, BATCH, xn2_t, mv2, rstd2, ln2, ln2_rstd)
            take_logits(BATCH, m_end + 5)

        @block.tensor
        def _(pe):
            pe.sem_inc(turned, 3)
            pe.sem_inc(pvd, 3)

            def split3(out, a_hi, a_lo, b_hi, b_lo, start=True, stop=True):
                nc.tensor.matmul(out, a_hi, b_hi, start=start, stop=False)
                nc.tensor.matmul(out, a_hi, b_lo, start=False, stop=False)
                return nc.tensor.matmul(out, a_lo, b_hi, start=False, stop=stop)

            def bank_read(kind, g, hg, b, tail=False):
                if kind == KA and hg == 1:
                    pe.wait_ge(resd, b + 1)
                elif kind == KA and hg == 2:
                    pe.wait_ge(lgd, b + 1)
                elif kind == LG:
                    pe.wait_ge(xt2d, b + 1)
                elif kind == KA and hg == NG - 1:
                    pe.wait_ge(xt_l, b + 2)
                elif kind == KA or (kind == OT0 and tail):
                    pe.wait_ge(added, g + 1)
                elif kind in (KB, QA, QB, OT0):
                    pe.wait_ge(rmul, 4 * (g + 1) + (4 if kind == OT0 else kind))
                elif kind == OT1:
                    pe.wait_ge(otd, 2 * g + 1)
                elif kind == V01 or (kind == WO and tail):
                    pe.wait_ge(otd, 2 * g + 2)
                elif kind == V23:
                    pe.wait_ge(vr, 2 * (g + 1) + 1)
                elif kind == WO:
                    pe.wait_ge(vr, 2 * (g + 1) + 2)
                elif kind in (BACK, LNT, LN2):
                    pe.wait_ge(added, g + 2)

            def project_qk(kind, hg):
                split3(ps_m[:, :], wqk_hi[:, hg, kind, :], wqk_lo[:, hg, kind, :], xt_hi[:, :], xt_lo[:, :]).then_inc(chunk, 1)

            def project_v(c, hg):
                for u in range(2):
                    t = 2 * c + u
                    last = split3(ps_m[:, u * GW:(u + 1) * GW], xt_hi[:, t * P:(t + 1) * P], xt_lo[:, t * P:(t + 1) * P],
                                  wv_hi[:, hg, :], wv_lo[:, hg, :])
                last.then_inc(chunk, 1)

            def project(kind, hg):
                if kind <= QB:
                    project_qk(kind, hg)
                else:
                    project_v(0 if kind == V01 else 1, hg)

            def turn_x(b, xn, ln):
                pe.wait_ge(ln, 13 * b + 13)
                for t in range(QT):
                    last = nc.tensor.transpose(ps_m[:, t * P:(t + 1) * P], xn[:, t, :], ident[:, :])
                last.then_inc(chunk, 1)

            def router(b):
                pe.wait_ge(xt2d, b + 1)
                for t in range(QT):
                    last = nc.tensor.matmul(ps_m[:, t * EXPERTS:(t + 1) * EXPERTS], xt2[:, t * P:(t + 1) * P], wg_s[:, :],
                                            start=True, stop=True)
                last.then_inc(chunk, 1)

            def turn_o(c, n_norm):
                pe.wait_ge(normed, n_norm)
                for u in range(2):
                    for f in range(2):
                        k = 2 * f + u
                        last = nc.tensor.transpose(ps_m[:, k * P:(k + 1) * P], o_sb[:, 2 * c + u, f * P:(f + 1) * P], ident[:, :])
                last.then_inc(chunk, 1)

            def out_project(hg):
                for f in range(2):
                    last = nc.tensor.matmul(ps_m[:, :], wo_s[:, 2 * hg + f, :], ot[:, f, :, :].rearrange("p t q -> p (t q)"),
                                            start=(f == 0), stop=(f == 1))
                last.then_inc(chunk, 1)

            def turn_back():
                for t in range(QT):
                    last = nc.tensor.transpose(ps_m[:, t * P:(t + 1) * P], acc[:, t * P:(t + 1) * P], ident[:, :])
                last.then_inc(chunk, 1)

            def scores(n, j, g):
                u, h, _ = place(j)
                if u == 0:
                    pe.wait_ge(stacked[h], 64 * (g + 1))
                pe.wait_ge(expd, n + 1)
                st = stack[h]
                for i, cols in tiles_of(u):
                    out = ps_s[:, u, cols]
                    q0, w = i * P, (i + 1) * P
                    nc.tensor.matmul(out, st[:, 1, q0:q0 + P], st[:, 0, 0:w], start=True, stop=False)
                    nc.tensor.matmul(out, st[:, 2, q0:q0 + P], st[:, 0, 0:w], start=False, stop=False)
                    last = nc.tensor.matmul(out[:, i * P:w], ident_b[:, :], causal[:, :], start=False, stop=True)
                last.then_inc(scored, 1)

            def turn_p(n, j):
                u = j % NU
                pe.wait_ge(expd, n + 4)
                pe.wait_ge(ptlo, n + 1)
                for k in range(len(UNITS[u])):
                    last = nc.tensor.transpose(ps_pt[:, j % 2, k * P:(k + 1) * P], probs[u][:, k * P:(k + 1) * P], ident[:, :])
                last.then_inc(turned, 1)

            def values(n, j, g):
                u, h, par = place(j)
                if j % STEPS == 0:
                    pe.wait_ge(v3, 2 * g + 2)
                if h == 0 and u < 2:
                    pe.wait_ge(normed, 2 * g + u + 1)
                pe.wait_ge(ptlo, n + 3)
                for blk, (i, k) in enumerate(UNITS[u]):
                    out = ps_o[:, i // 2, i % 2, h * DHEAD:(h + 1) * DHEAD]
                    for pt, parts in ((pt_hi[u], (0, 1, 2)), (pt_lo[u], (0, 1))):
                        for v in parts:
                            last = nc.tensor.matmul(out, pt[:, blk, :], v_parts[:, par, v, k, h * DHEAD:(h + 1) * DHEAD],
                                                    start=(k == 0 and pt is pt_hi[u] and v == 0),
                                                    stop=(k == i and pt is pt_lo[u] and v == 1))
                last.then_inc(pvd, 1)

            def batch(b, last):
                m0 = FIRST_CHUNKS + CHUNKS_PER_BATCH * b
                for hg in range(NG):
                    tail = last and hg == NG - 1
                    g = NG * b + hg
                    for t in range(STEPS):
                        j = STEPS * hg + t
                        n = BSTEPS * b + j
                        if not (last and j + 3 >= BSTEPS):
                            scores(n + 3, j + 3, g + (t + 3) // STEPS)
                        if not (last and j + 1 >= BSTEPS):
                            turn_p(n + 1, j + 1)
                        for kind in (KA, KB, QA, QB, V01, V23):
                            if t == SLOT_OF[kind] and not tail:
                                bank_read(kind, g, hg, b)
                                project(kind, (hg + 1) % NG)
                        for c in range(2):
                            if t == SLOT_OF[OT0 + c]:
                                bank_read(OT0 + c, g, hg, b, tail)
                                turn_o(c, 2 * g + c + 1)
                        if t == SLOT_OF[WO]:
                            bank_read(WO, g, hg, b, tail)
                            out_project((hg + NG - 1) % NG)
                        if hg == 0 and t == SLOT_OF[BACK]:
                            bank_read(BACK, g, hg, b)
                            turn_back()
                        if hg == 1 and t == SLOT_OF[LN2]:
                            bank_read(LN2, g, hg, b)
                            turn_x(b, xn2_t, ln2)
                        if hg == 1 and t == SLOT_OF[LG]:
                            router(b)
                        if hg == 2 and not last and t == SLOT_OF[LNT]:
                            bank_read(LNT, g, hg, b)
                            turn_x(b + 1, xn, ln)
                        values(n, j, g)

            pe.wait_ge(const, 4)
            pe.wait_ge(in_w, 176)
            for k in range(2 * NG):
                last = nc.tensor.matmul(ps_m[:, 0:1], wo_s[:, k, :], bv_s[:, k:k + 1], start=(k == 0), stop=(k == 2 * NG - 1))
            last.then_inc(chunk, 1)
            pe.wait_ge(biased, 1)
            turn_x(0, xn, ln)
            pe.wait_ge(wsplit, 2)
            pe.wait_ge(xt_l, 1)
            for kind in (KA, KB, QA, QB, V01, V23):
                if KA < kind <= QB:
                    pe.wait_ge(rmul, kind)
                elif kind == V01:
                    pe.wait_ge(rmul, 4)
                elif kind == V23:
                    pe.wait_ge(vr, 1)
                project(kind, 0)
            for n in range(3):
                scores(n, n, 0)
            turn_p(0, 0)
            pe.wait_ge(vr, 2)
            with pe.Fori(0, BATCH - 1) as b:
                batch(b, False)
            batch(BATCH - 1, True)
            for c in range(2):
                if c == 0:
                    pe.wait_ge(added, NG * BATCH + 1)
                else:
                    pe.wait_ge(otd, 2 * NG * BATCH + 1)
                turn_o(c, 2 * NG * BATCH + c + 1)
            pe.wait_ge(otd, 2 * NG * BATCH + 2)
            out_project(NG - 1)
            pe.wait_ge(added, NG * BATCH + 2)
            turn_back()
            pe.wait_ge(resd, BATCH + 1)
            turn_x(BATCH, xn2_t, ln2)
            router(BATCH)


def mixture(nc, ctx, x_res, xn2, logits, xt2_all, routed, base, w_shared, w_experts, tables, out):
    def sb(name, shape, dt):
        return ctx.enter_context(nc.sbuf_tensor(name, shape, dt))

    def sem(name):
        return ctx.enter_context(nc.semaphore(name))

    E, T = EXPERTS, TILES
    WALL = 3 * INTER
    ws_hi = sb("ws_hi", [P, WALL], F32R)
    ws_lo = sb("ws_lo", [P, WALL], F32R)
    w_raw = sb("w_raw", [P, 2, WALL], F32)
    we_hi = sb("we_hi", [P, E, WALL], F32R)
    we_lo = sb("we_lo", [P, E, WALL], F32R)
    ident = sb("ident2", [P, P], F32)
    tri = sb("tri", [P, P], BF16)
    ones = sb("ones2", [P, P], BF16)
    rev = sb("rev", [P, E], F32)
    tile_no = sb("tile_no", [P, RTILES], F32)
    token_no = sb("token_no", [P, T], U32)
    top = sb("top", [P, T], F32)
    hit = sb("hit", [P, T, E], F32)
    hot = sb("hot", [P, T, E], F32)
    hot_b = sb("hot_b", [P, T, E], BF16)
    cum = [sb(f"cum{i}", [P, E, T], F32) for i in range(2)]
    excl = sb("excl", [P, E, T], F32)
    count_i = sb("count_i", [P, E], I32)
    tiles_i = sb("tiles_i", [P, E], I32)
    ends = [sb(f"ends{i}", [P, E], F32) for i in range(2)]
    starts = sb("starts", [P, E], F32)
    slot_f = sb("slot_f", [P, T], F32)
    slot_u = sb("slot_u", [P, T], U32)
    past = sb("past", [P, RTILES, E], F32)
    owner_f = sb("owner_f", [P, RTILES], F32)
    owner = sb("owner", [P, RTILES], I32)
    xt_raw = sb("xt_raw", [P, 2, SEQ], F32)
    xt_hi = sb("fxt_hi", [P, 2, SEQ], F32R)
    xt_lo = sb("fxt_lo", [P, 2, SEQ], F32R)
    rxt_hi = sb("rxt_hi", [P, 2, P], F32R)
    rxt_lo = sb("rxt_lo", [P, 2, P], F32R)
    acts = sb("acts", [P, 4, INTER], F32)
    gate, hid = acts[:, 0:2, :], acts[:, 2:4, :]
    ws_raw = acts[:, 0:3, :].rearrange("p c w -> p (c w)")
    ht_hi = sb("ht_hi", [P, 2, INTER], F32R)
    ht_lo = sb("ht_lo", [P, 2, INTER], F32R)
    rows = sb("rows", [P, RING, ROW], F32)
    res = sb("res", [P, RING, EMB], F32)

    ps_h = ctx.enter_context(nc.psum_tensor("ps_h", [P, 2, 2, 512], F32))
    ps_x = ctx.enter_context(nc.psum_tensor("ps_x", [P, 512], F32))
    ps_t = ctx.enter_context(nc.psum_tensor("ps_t", [P, 512], F32))
    ps_y = ctx.enter_context(nc.psum_tensor("ps_y", [P, 2, 512], F32))

    in_c = sem("fin_c")
    in_ws = sem("fin_ws")
    in_w = [sem(f"fin_w{i}") for i in range(2)]
    in_x = [sem(f"fin_x{i}") for i in range(2)]
    wshi = sem("wshi")
    wslo = sem("wslo")
    whi = sem("whi")
    wlo = sem("wlo")
    rt = sem("rt")
    hotd = sem("hotd")
    counted = sem("counted")
    slotted = sem("slotted")
    owned = sem("owned")
    spread = sem("spread")
    sxh = sem("sxh")
    sxl = sem("sxl")
    sh = sem("sh")
    sg = sem("sg")
    shm = sem("shm")
    shh = sem("shh")
    shl = sem("shl")
    syc = sem("syc")
    sr = sem("sr")
    based = sem("based")
    rin = [sem(f"rin{i}") for i in range(RING)]
    gin = [sem(f"gin{i}") for i in range(RING)]
    outd = [sem(f"outd{i}") for i in range(RING)]
    rxt = sem("rxt")
    rxh = sem("rxh")
    rxl = sem("rxl")
    rh = sem("rh")
    rg = sem("rg")
    rhm = sem("rhm")
    rht = sem("rht")
    rhh = sem("rhh")
    rhl = sem("rhl")
    ry = sem("ry")
    ra = sem("ra")
    zero = sem("zero")
    block = ctx.enter_context(nc.Block())
    PAIRS = BATCH // 2
    TURNS = RTILES // RING

    @block.sync
    def _(sp):
        sp.dma_start(ws_raw[:, :], w_shared).then_inc(in_ws, 16)
        for dst, name in ((ident[:, :], "ident"), (tri[:, :], "tri"), (ones[:, :], "ones_b"), (rev[:, :], "rev"),
                          (tile_no[:, :], "tile_no"), (token_no[:, :], "token_no")):
            sp.dma_start(dst, tables[name]).then_inc(in_c, 16)
        for v in range(2):
            sp.dma_start(xt_raw[:, v, :], xt2_all[v + 1]).then_inc(in_x[v], 16)
            sp.dma_start(w_raw[:, v, :], w_experts[v]).then_inc(in_w[v], 16)

        def pair(k, last):
            for v in range(2):
                b = 2 * k + v
                if not last:
                    e_off = sp.snap((b + 2) * (P * WALL))
                    x_off = sp.snap((b + 3) * (P * SEQ))
                    sp.wait_ge(sxl, b + 1)
                    sp.dma_start(xt_raw[:, v, :], bass.AP(tensor=xt2_all.tensor, offset=x_off, ap=[[SEQ, P], [1, SEQ]])
                                 ).then_inc(in_x[v], 16)
                    sp.wait_ge(wlo, b + 1)
                    sp.dma_start(w_raw[:, v, :], bass.AP(tensor=w_experts.tensor, offset=e_off, ap=[[WALL, P], [1, WALL]])
                                 ).then_inc(in_w[v], 16)
            for v in range(2):
                b = 2 * k + v
                dst, src = base[bass.ds(b * SEQ, SEQ), :], x_res[:, bass.ds((b + 1) * QT, QT), :]
                if not last:
                    d_off, s_off = sp.snap(b * (SEQ * EMB)), sp.snap((b + 1) * (QT * EMB))
                    full = x_res[:, 0:QT, :]
                    dst = bass.AP(tensor=base.tensor, offset=d_off, ap=[[EMB, P], [P * EMB, QT], [1, EMB]])
                    src = bass.AP(tensor=full.tensor, offset=s_off, ap=[list(a) for a in full.ap])
                else:
                    dst = dst.rearrange("(t p) e -> p t e", p=P)
                sp.wait_ge(sr, b + 3)
                sp.dma_start(dst, src).then_inc(based, 16)

        with sp.Fori(0, PAIRS - 1) as k:
            pair(k, False)
        pair(PAIRS - 1, True)

        sp.wait_ge(spread, 16 * T)

        for v in range(RING):
            sp.dma_start(rows[:, v, :], routed[v * P:(v + 1) * P, :]).then_inc(rin[v], 16)
        with sp.Fori(1, TURNS) as k:
            for v in range(RING):
                src = bass.AP(tensor=routed.tensor, offset=sp.snap((RING * k + v) * (P * ROW)), ap=[[ROW, P], [1, ROW]])
                sp.wait_ge(outd[v], 16 * k)
                sp.dma_start(rows[:, v, :], src).then_inc(rin[v], 16)
        sp.wait_ge(based, 16 * BATCH)
        for v in range(RING):
            sp.wait_ge(outd[v], 16 * TURNS)

    @block.gpsimd
    def _(pool):
        nc.gpsimd.memset(res[:, :, :], 0.0).then_inc(zero, 1)
        pool.wait_ge(slotted, 2)
        pool.wait_ge(zero, 1)
        for b in range(BATCH):
            for t in range(QT * b, QT * (b + 1)):
                nc.gpsimd.indirect_dma_start(
                    out=routed, out_offset=bass.IndirectOffsetOnAxis(ap=slot_u[:, t:t + 1], axis=0),
                    in_=xn2[:, QT + t, :], in_offset=None).then_inc(spread, 16)
            pool.wait_ge(whi, b + 1)
            nc.gpsimd.tensor_tensor(we_lo[:, b, :], w_raw[:, b % 2, :], we_hi[:, b, :].bitcast(F32), ALU.subtract).then_inc(wlo, 1)

        bound = pool.to_reg(TOKENS - 1)

        def gather(k, v):
            pool.wait_ge(rin[v], 16 * k + 16)
            nc.gpsimd.indirect_dma_start(
                out=res[:, v, :], out_offset=None, in_=base,
                in_offset=bass.IndirectOffsetOnAxis(ap=rows[:, v, EMB:ROW].bitcast(U32), axis=0),
                bounds_check=bound, oob_is_err=False).then_inc(gin[v], 16)

        def scatter(k, v):
            pool.wait_ge(ra, RING * k + v + 3)
            nc.gpsimd.indirect_dma_start(
                out=out, out_offset=bass.IndirectOffsetOnAxis(ap=rows[:, v, EMB:ROW].bitcast(U32), axis=0),
                in_=res[:, v, :], in_offset=None, bounds_check=bound, oob_is_err=False).then_inc(outd[v], 16)

        pool.wait_ge(based, 16 * BATCH)
        for v in range(AHEAD):
            gather(0, v)

        def turn(k, last):
            for v in range(RING):
                if v + AHEAD < RING:
                    gather(k, v + AHEAD)
                elif not last:
                    gather(k + 1, v + AHEAD - RING)
                scatter(k, v)

        for k in range(TURNS):
            turn(k, k == TURNS - 1)

    @block.scalar
    def _(act):
        act.wait_ge(in_ws, 16)
        nc.scalar.copy(ws_hi[:, :], ws_raw[:, :]).then_inc(wshi, 1)

        def x_high(k, v):
            act.wait_ge(in_x[v], 16 * k + 16)
            nc.scalar.copy(xt_hi[:, v, :], xt_raw[:, v, :]).then_inc(sxh, 1)

        def gelu(s, p):
            act.wait_ge(sh, s + 1)
            act.wait_ge(shm, s + 1)
            nc.scalar.activation(gate[:, p, :], ps_h[:, p, 0, :], ACT.Gelu).then_inc(sg, 1)

        def h_high(s, p):
            act.wait_ge(shm, s + 3)
            act.wait_ge(syc, s + 1)
            nc.scalar.copy(ht_hi[:, p, :], hid[:, p, :]).then_inc(shh, 1)

        def w_high(k, v):
            act.wait_ge(in_w[v], 16 * k + 16)
            e = 2 * k + v
            nc.scalar.copy(we_hi[:, bass.ds(e, 1), :].rearrange("p o w -> p (o w)"), w_raw[:, v, :]).then_inc(whi, 1)

        def pair(k, last):
            for v in range(2):
                for c in range(CHUNK):
                    s, p = 8 * k + CHUNK * v + c, c % 2
                    if not (last and v == 1 and c == CHUNK - 1):
                        if c == CHUNK - 1:
                            x_high(k + v, 1 - v)
                        gelu(s + 1, 1 - p)
                    h_high(s, p)
                    if c == 2:
                        w_high(k, v)

        x_high(0, 0)
        gelu(0, 0)
        with act.Fori(0, PAIRS - 1) as k:
            pair(k, False)
        pair(PAIRS - 1, True)

        def row_high(j, v):
            act.wait_ge(rxt, j + 1)
            nc.scalar.copy(rxt_hi[:, v % 2, :], ps_x[:, 0:P]).then_inc(rxh, 1)

        def row_gelu(j, v):
            act.wait_ge(rh, j + 1)
            act.wait_ge(rhm, j + 1)
            nc.scalar.activation(gate[:, v % 2, :], ps_h[:, v % 2, 0, :], ACT.Gelu).then_inc(rg, 1)

        def turned_high(j, v):
            act.wait_ge(rht, j + 1)
            nc.scalar.copy(ht_hi[:, v % 2, :], ps_t[:, :]).then_inc(rhh, 1)

        def turn(k, last):
            for v in range(RING):
                j = RING * k + v
                if not (last and v + 3 >= RING):
                    row_high(j + 3, v + 3)
                if not (last and v + 2 >= RING):
                    row_gelu(j + 2, v)
                if not (last and v + 1 >= RING):
                    turned_high(j + 1, v + 1)

        for v in range(2):
            row_high(v, v)
            row_gelu(v, v)
        row_high(2, 2)
        turned_high(0, 0)
        with act.Fori(0, TURNS - 1) as k:
            turn(k, False)
        turn(TURNS - 1, True)

    @block.vector
    def _(dve):
        dve.sem_inc(shm, 2)
        dve.sem_inc(sr, 2)
        dve.sem_inc(rhm, 2)
        dve.sem_inc(rxl, 1)
        dve.sem_inc(rhl, 1)
        dve.sem_inc(ra, 2)
        dve.wait_ge(wshi, 1)
        nc.vector.tensor_tensor(ws_lo[:, :], ws_raw[:, :], ws_hi[:, :].bitcast(F32), ALU.subtract).then_inc(wslo, 1)

        steps = [0]

        def link(ins):
            steps[0] += 1
            ins.then_inc(rt, 1)
            dve.wait_ge(rt, steps[0])

        V = nc.vector
        lg = logits[:, QT:, :]
        by_t = lambda a: a[:, :].unsqueeze(2).broadcast_to([P, T, E])
        by_e = lambda a: a[:, :].unsqueeze(1).broadcast_to([P, T, E])
        dve.wait_ge(in_c, 96)
        link(V.tensor_reduce(top[:, :], lg, AX_X, ALU.max))
        link(V.tensor_tensor(hit[:, :, :], lg, by_t(top), ALU.is_equal))
        link(V.tensor_tensor(hit[:, :, :], hit[:, :, :], by_e(rev), ALU.mult))
        link(V.tensor_reduce(top[:, :], hit[:, :, :], AX_X, ALU.max))
        link(V.tensor_tensor(hot[:, :, :], by_e(rev), by_t(top), ALU.is_equal))
        V.tensor_copy(hot_b[:, :, :], hot[:, :, :]).then_inc(hotd, 1)
        V.tensor_copy(xn2[:, QT:, EMB:ROW].bitcast(U32), token_no[:, :].unsqueeze(2)).then_inc(slotted, 1)
        dve.wait_ge(counted, 1)
        ranks = ps_t[:, 0:T * E].rearrange("p (t e) -> p t e", e=E)
        counts = ps_t[:, T * E:2 * T * E].rearrange("p (t e) -> p e t", e=E)
        link(V.tensor_copy(cum[0][:, :, :], counts))
        src, d = 0, 1
        while d < T:
            V.tensor_copy(cum[1 - src][:, :, 0:d], cum[src][:, :, 0:d])
            link(V.tensor_tensor(cum[1 - src][:, :, d:], cum[src][:, :, d:], cum[src][:, :, 0:T - d], ALU.add))
            src, d = 1 - src, 2 * d
        link(V.tensor_tensor(excl[:, :, :], counts, cum[src][:, :, :], ALU.subtract))
        link(V.tensor_scalar(count_i[:, :], cum[src][:, :, T - 1], float(P - 1), None, ALU.add))
        link(V.tensor_scalar(tiles_i[:, :], count_i[:, :], P.bit_length() - 1, None, ALU.arith_shift_right))
        link(V.tensor_copy(ends[0][:, :], tiles_i[:, :]))
        esrc, d = 0, 1
        while d < E:
            V.tensor_copy(ends[1 - esrc][:, 0:d], ends[esrc][:, 0:d])
            link(V.tensor_tensor(ends[1 - esrc][:, d:], ends[esrc][:, d:], ends[esrc][:, 0:E - d], ALU.add))
            esrc, d = 1 - esrc, 2 * d
        link(V.tensor_tensor(starts[:, :], ends[esrc][:, :], tiles_i[:, :], ALU.subtract))
        link(V.tensor_tensor(hit[:, :, :], ranks, excl[:, :, :].rearrange("p e t -> p t e"), ALU.subtract))
        link(V.scalar_tensor_tensor(out=hit[:, :, :], in0=by_e(starts), scalar=float(P), in1=hit[:, :, :],
                                    op0=ALU.mult, op1=ALU.add))
        link(V.tensor_tensor(hit[:, :, :], hit[:, :, :], hot[:, :, :], ALU.mult))
        link(V.tensor_reduce(slot_f[:, :], hit[:, :, :], AX_X, ALU.add))
        V.tensor_copy(slot_u[:, :], slot_f[:, :]).then_inc(slotted, 1)
        tiles_by_e = [P, RTILES, E]
        link(V.tensor_tensor(past[:, :, :], tile_no[:, :].unsqueeze(2).broadcast_to(tiles_by_e),
                             ends[esrc][:, :].unsqueeze(1).broadcast_to(tiles_by_e), ALU.is_ge))
        link(V.tensor_reduce(owner_f[:, :], past[:, :, :], AX_X, ALU.add))
        V.tensor_scalar(owner[:, :], owner_f[:, :], float(E - 1), None, ALU.min).then_inc(owned, 1)

        def x_low(b, v):
            dve.wait_ge(sxh, b + 1)
            V.tensor_tensor(xt_lo[:, v, :], xt_raw[:, v, :], xt_hi[:, v, :].bitcast(F32), ALU.subtract).then_inc(sxl, 1)

        def multiply(s, p):
            dve.wait_ge(sg, s + 1)
            V.tensor_tensor(hid[:, p, :], ps_h[:, p, 1, :], gate[:, p, :], ALU.mult).then_inc(shm, 1)

        def h_low(s, p):
            dve.wait_ge(shh, s + 1)
            V.tensor_tensor(ht_lo[:, p, :], hid[:, p, :], ht_hi[:, p, :].bitcast(F32), ALU.subtract).then_inc(shl, 1)

        def add_shared(b, v):
            dve.wait_ge(syc, CHUNK * b + CHUNK + 2)
            xs = x_res[:, bass.ds((b + 1) * QT, QT), :].rearrange("p t e -> p (t e)")
            V.tensor_tensor(xs, ps_y[:, v, :], xs, ALU.add).then_inc(sr, 1)

        def pair(k, last):
            for v in range(2):
                b = 2 * k + v
                for c in range(CHUNK):
                    s, p = 8 * k + CHUNK * v + c, c % 2
                    if not (last and v == 1 and c == CHUNK - 1):
                        if c == CHUNK - 1:
                            x_low(b + 1, 1 - v)
                        multiply(s + 1, 1 - p)
                    h_low(s, p)
                add_shared(b, v)

        x_low(0, 0)
        multiply(0, 0)
        with dve.Fori(0, PAIRS - 1) as k:
            pair(k, False)
        pair(PAIRS - 1, True)

        def row_low(j, v):
            dve.wait_ge(rxh, j + 1)
            V.tensor_tensor(rxt_lo[:, v % 2, :], ps_x[:, 0:P], rxt_hi[:, v % 2, :].bitcast(F32), ALU.subtract).then_inc(rxl, 1)

        def row_multiply(j, v):
            dve.wait_ge(rg, j + 1)
            V.tensor_tensor(hid[:, v % 2, :], ps_h[:, v % 2, 1, :], gate[:, v % 2, :], ALU.mult).then_inc(rhm, 1)

        def turned_low(j, v):
            dve.wait_ge(rhh, j + 1)
            V.tensor_tensor(ht_lo[:, v % 2, :], ps_t[:, :], ht_hi[:, v % 2, :].bitcast(F32), ALU.subtract).then_inc(rhl, 1)

        def add_rows(j, k, v):
            dve.wait_ge(ry, j + 1)
            dve.wait_ge(gin[v], 16 * k + 16)
            V.tensor_tensor(res[:, v, :], ps_y[:, v % 2, 0:EMB], res[:, v, :], ALU.add).then_inc(ra, 1)

        def turn(k, last):
            for v in range(RING):
                j = RING * k + v
                if not (last and v + 3 >= RING):
                    row_low(j + 3, v + 3)
                if not (last and v + 2 >= RING):
                    row_multiply(j + 2, v)
                if not (last and v + 1 >= RING):
                    turned_low(j + 1, v + 1)
                add_rows(j, k, v)

        for v in range(2):
            row_low(v, v)
            row_multiply(v, v)
        row_low(2, 2)
        turned_low(0, 0)
        with dve.Fori(0, TURNS - 1) as k:
            turn(k, False)
        turn(TURNS - 1, True)

    @block.tensor
    def _(pe):
        pe.sem_inc(syc, 2)

        def split3(o, a_hi, a_lo, b_hi, b_lo, start, stop, skip=False):
            nc.tensor.matmul(o, a_hi, b_hi, start=start, stop=False, skip_group_check=skip)
            nc.tensor.matmul(o, a_hi, b_lo, start=False, stop=False, skip_group_check=skip)
            return nc.tensor.matmul(o, a_lo, b_hi, start=False, stop=stop, skip_group_check=skip)

        pe.wait_ge(in_c, 96)
        pe.wait_ge(hotd, 1)
        oh = hot_b[:, :, :].rearrange("p t e -> p (t e)")
        nc.tensor.matmul(ps_t[:, 0:T * E], tri[:, :], oh, start=True, stop=True)
        nc.tensor.matmul(ps_t[:, T * E:2 * T * E], ones[:, :], oh, start=True, stop=True).then_inc(counted, 1)

        def hidden(s, v, c):
            pe.wait_ge(shm, s + 1)
            for w in range(2):
                cols = slice(w * INTER + c * P, w * INTER + (c + 1) * P)
                last = split3(ps_h[:, c % 2, w, :], ws_hi[:, cols], ws_lo[:, cols], xt_hi[:, v, :], xt_lo[:, v, :], True, True)
            last.then_inc(sh, 1)

        def project(s, b, v, c):
            if c == 0:
                pe.wait_ge(sr, b + 1)
            pe.wait_ge(shl, s + 1)
            w3 = slice(2 * INTER + c * EMB, 2 * INTER + (c + 1) * EMB)
            for i in range(QT):
                rows_i = slice(i * P, (i + 1) * P)
                last = split3(ps_y[:, v, i * EMB:(i + 1) * EMB], ht_hi[:, c % 2, rows_i], ht_lo[:, c % 2, rows_i],
                              ws_hi[:, w3], ws_lo[:, w3], c == 0 and i == 0, c == CHUNK - 1, True)
            last.then_inc(syc, 1)

        def pair(k, last):
            for v in range(2):
                b = 2 * k + v
                for c in range(CHUNK):
                    s = 8 * k + CHUNK * v + c
                    if c < CHUNK - 1:
                        hidden(s + 1, v, c + 1)
                    elif not (last and v == 1):
                        pe.wait_ge(sxl, b + 2)
                        hidden(s + 1, 1 - v, 0)
                    project(s, b, v, c)

        pe.wait_ge(wslo, 1)
        pe.wait_ge(sxl, 1)
        hidden(0, 0, 0)
        with pe.Fori(0, PAIRS - 1) as k:
            pair(k, False)
        pair(PAIRS - 1, True)

        def expert(j):
            return pe.value_load(owner[0:1, bass.ds(j, 1)], min_val=0, max_val=E - 1)

        def weights(w, e, first, width):
            return w[:, bass.ds(e, 1), first:first + width].rearrange("p o w -> p (o w)")

        def turn_rows(j, k, v):
            pe.wait_ge(rin[v % RING], 16 * k + 16)
            pe.wait_ge(rxl, j + 1)
            nc.tensor.transpose(ps_x[:, 0:P], rows[:, v % RING, 0:EMB], ident[:, :]).then_inc(rxt, 1)

        def row_hidden(j, v, e):
            pe.wait_ge(rxl, j + 2)
            pe.wait_ge(rhm, j + 1)
            for w in range(2):
                last = split3(ps_h[:, v % 2, w, :], rxt_hi[:, v % 2, :], rxt_lo[:, v % 2, :],
                              weights(we_hi, e, w * INTER, INTER), weights(we_lo, e, w * INTER, INTER), True, True)
            last.then_inc(rh, 1)

        def turn_hidden(j, v):
            pe.wait_ge(rhm, j + 3)
            pe.wait_ge(rhl, j + 1)
            for c in range(CHUNK):
                last = nc.tensor.transpose(ps_t[:, c * P:(c + 1) * P], hid[:, v % 2, c * P:(c + 1) * P], ident[:, :])
            last.then_inc(rht, 1)

        def row_project(j, v, e):
            pe.wait_ge(rhl, j + 2)
            pe.wait_ge(ra, j + 1)
            for c in range(CHUNK):
                cols = slice(c * P, (c + 1) * P)
                last = split3(ps_y[:, v % 2, 0:EMB], ht_hi[:, v % 2, cols], ht_lo[:, v % 2, cols],
                              weights(we_hi, e, 2 * INTER + c * EMB, EMB), weights(we_lo, e, 2 * INTER + c * EMB, EMB),
                              c == 0, c == CHUNK - 1)
            last.then_inc(ry, 1)

        def turn(k, last):
            for v in range(RING):
                j = RING * k + v
                e_now = expert(j)
                if not (last and v + 2 >= RING):
                    e_next = expert(j + 2)
                if not (last and v + 3 >= RING):
                    turn_rows(j + 3, k + (v + 3) // RING, v + 3)
                if not (last and v + 2 >= RING):
                    row_hidden(j + 2, v, e_next)
                if not (last and v + 1 >= RING):
                    turn_hidden(j + 1, v + 1)
                row_project(j, v, e_now)

        pe.wait_ge(owned, 1)
        pe.wait_ge(wlo, E)
        pe.wait_ge(sr, BATCH + 2)
        firsts = [expert(v) for v in range(2)]
        for v in range(2):
            turn_rows(v, 0, v)
            row_hidden(v, v, firsts[v])
        turn_rows(2, 0, 2)
        turn_hidden(0, 0)
        with pe.Fori(0, TURNS - 1) as k:
            turn(k, False)
        turn(TURNS - 1, True)


def build(nc, t, out):
    dram = lambda name, shape: nc.dram_tensor(name, shape, F32, kind="Internal").ap()
    routed = dram("routed", [SLOTS, ROW])
    base = dram("base", [TOKENS, EMB])
    xt2_all = dram("xt2_all", [BATCH + 1, P, SEQ])
    with ExitStack() as ctx:
        sb = lambda name, shape, dt: ctx.enter_context(nc.sbuf_tensor(name, shape, dt))
        x_res = sb("x_res", [P, (BATCH + 1) * QT, EMB], F32)
        xn2 = sb("xn2", [P, (BATCH + 1) * QT, ROW], F32)
        logits = sb("logits", [P, (BATCH + 1) * QT, EXPERTS], F32)
        with ExitStack() as actx:
            attention(nc, actx, t["x_in"], t["wqk"], t["wv"], t["wo"], t["bqk"], t["bv"], t["bo"], t, x_res, xn2, logits,
                      xt2_all, routed.rearrange("(t p) r -> p t r", p=P))
        with ExitStack() as fctx:
            mixture(nc, fctx, x_res, xn2, logits, xt2_all, routed, base, t["w_shared"], t["w_experts"], t,
                    out.rearrange("b s e -> (b s) e"))


def kernel(**inputs):
    import numpy as np
    import concourse.bacc as _bacc
    from concourse import mybir as _mybir
    from concourse.bass_utils import run_bass_kernel_spmd as _run

    a = {k: np.ascontiguousarray(v) for k, v in inputs.items()}
    D, H = DHEAD, HEADS
    def halves(w):
        w = w.reshape(w.shape[0], GROUPS, GROUP, 2, HALF)
        return w.transpose(0, 1, 3, 2, 4).reshape(w.shape[0], GROUPS, 2, P)
    wq, wkv = a["L0_attn_Wq"], a["L0_attn_Wkv"]
    wqk = np.concatenate([halves(wkv[:, :H * D]), halves(wq)], axis=2).reshape(P, -1)
    bqk = np.concatenate([halves(a["L0_attn_bkv"][None, :H * D]), halves(a["L0_attn_bq"][None])], axis=2)
    inv = (np.float32(1.0) / np.float32(10000.0) ** (np.arange(0, D, 2, dtype=np.float32) / np.float32(D))).astype(np.float32)
    ang = np.arange(SEQ, dtype=np.float32)[:, None] * inv[None, :]
    cos, sin = (np.tile(f(ang).astype(np.float32).T, (GROUP, 1)) for f in (np.cos, np.sin))
    rope = np.stack([np.stack([np.stack([cos, sin], 1), np.stack([-sin, cos], 1)], 1) * s
                     for s in (np.float32(1.0), np.float32(D ** -0.5))], 1).astype(np.float32)
    import ml_dtypes
    q, k = np.arange(P)[:, None], np.arange(P)[None, :]
    arrays = {
        "x_in": a["L0_attn_x"], "wqk": wqk, "wv": wkv[:, H * D:],
        "wo": a["L0_attn_Wo"].reshape(2 * GROUPS, P, EMB).transpose(1, 0, 2).reshape(P, -1),
        "bqk": bqk[0].transpose(2, 0, 1), "bv": a["L0_attn_bkv"][H * D:].reshape(2 * GROUPS, P).T, "bo": a["L0_attn_bo"],
        "rope": rope, "ident": np.eye(P, dtype=np.float32), "ident_b": np.eye(P).astype(ml_dtypes.bfloat16),
        "causal": np.where(k > q, NEG, 0.0).astype(ml_dtypes.bfloat16),
    }
    def expert(w1, w2, w3):
        lead = w1.shape[:-2]
        w3 = np.moveaxis(w3.reshape(*lead, CHUNK, P, EMB), -3, -2).reshape(*lead, P, CHUNK * EMB)
        return np.concatenate([w1, w2, w3], axis=-1)
    arrays.update({
        "wg": a["L0_ffn_Wg"], "w_shared": expert(a["L0_ffn_w1s"], a["L0_ffn_w2s"], a["L0_ffn_w3s"]),
        "w_experts": expert(a["L0_ffn_W1"], a["L0_ffn_W2"], a["L0_ffn_W3"]),
        "tri": (q < k).astype(ml_dtypes.bfloat16), "ones_b": np.ones((P, P), ml_dtypes.bfloat16),
        "rev": np.tile(np.arange(EXPERTS, 0, -1, dtype=np.float32), (P, 1)),
        "tile_no": np.tile(np.arange(RTILES, dtype=np.float32), (P, 1)),
        "token_no": (np.arange(TILES)[None, :] * P + np.arange(P)[:, None]).astype(np.uint32),
    })
    arrays = {k: np.ascontiguousarray(v) for k, v in arrays.items()}
    nc = _bacc.Bacc("TRN2", target_bir_lowering=False, num_devices=1)
    t = {k: nc.dram_tensor(k + "_dram", v.shape, _mybir.dt.from_np(v.dtype), kind="ExternalInput").ap() for k, v in arrays.items()}
    out = nc.dram_tensor("out_dram", a["L0_attn_x"].shape, F32, kind="ExternalOutput").ap()
    build(nc, t, out)
    r = _run(nc, [{k + "_dram": v for k, v in arrays.items()}], core_ids=[0])
    return r.results[0]["out_dram"]
```

```python
from contextlib import ExitStack

import concourse.bass as bass
from concourse import mybir

F32 = mybir.dt.float32
F32R = mybir.dt.float32r
BF16 = mybir.dt.bfloat16
F16 = mybir.dt.float16
U32 = mybir.dt.uint32
I32 = mybir.dt.int32
ALU = mybir.AluOpType
ACT = mybir.ActivationFunctionType
AX_X = mybir.AxisListType.X

P = 128
BATCH, SEQ, EMB = 8, 512, 128
HEADS, DHEAD = 16, 64
HALF = DHEAD // 2
GROUP = P // HALF
GROUPS = HEADS // GROUP
QT = SEQ // P
UNITS = [[(0, 0), (1, 0), (1, 1)], [(2, k) for k in range(3)], [(3, k) for k in range(4)]]
NU = len(UNITS)
STEPS = GROUP * NU
BSTEPS = GROUPS * STEPS
GW = GROUP * DHEAD
TILES = BATCH * QT
EPS = 1e-5
EXPERTS, INTER = 8, 512
TOKENS = BATCH * SEQ
ROW = EMB + 1
NOBODY = TOKENS
RTILES = TILES + EXPERTS
SLOTS = RTILES * P
CHUNK = INTER // P
RING = 8
AHEAD = 2
NEG = -1e30

KA, KB, QA, QB, OT0, OT1, V01, V23, WO, BACK, LNT, LN2, LG = range(13)
SLOT_OF = {LG: 0, QA: 0, OT0: 1, QB: 2, OT1: 3, V01: 4, V23: 5, LNT: 6, WO: 7, KA: 8, KB: 9, BACK: 10, LN2: 10}
FIRST_CHUNKS = 10


def chunks_of(hg, last=False):
    kinds = [OT0, OT1, WO]
    kinds += [] if last and hg == GROUPS - 1 else [QA, QB, V01, V23]
    kinds += [] if last and hg >= GROUPS - 2 else [KA, KB]
    kinds += {0: [BACK], 1: [LN2], 2: [LG] if last else [LG, LNT]}.get(hg, [])
    return sorted(kinds, key=SLOT_OF.get)


def chunks_before(hg, kind, last=False):
    return sum(len(chunks_of(i, last)) for i in range(hg)) + chunks_of(hg, last).index(kind)


CHUNKS_PER_BATCH = sum(len(chunks_of(i)) for i in range(GROUPS))
assert CHUNKS_PER_BATCH % 2 == 0 and FIRST_CHUNKS % 2 == 0


def chunk_at(b, hg, kind, last=False):
    n = chunks_before(hg, kind, last)
    return FIRST_CHUNKS + CHUNKS_PER_BATCH * b + n, n % 2


def end_chunk(i):
    m, bank = chunk_at(BATCH - 1, GROUPS - 1, WO, True)
    return m + 1 + i, (bank + 1 + i) % 2


def attention(nc, ctx, x, wqk, wv, wo, bqk, bv, bo, tables, x_res, xn2, logits, xt2_all, zeros_to):
    def sb(name, shape, dt):
        return ctx.enter_context(nc.sbuf_tensor(name, shape, dt))

    def sem(name):
        return ctx.enter_context(nc.semaphore(name))

    NG = GROUPS
    wqk_hi = sb("wqk_hi", [P, NG, 4, P], F32R)
    wqk_lo = sb("wqk_lo", [P, NG, 4, P], F32R)
    wv_hi = sb("wv_hi", [P, NG, GW], F32R)
    wv_lo = sb("wv_lo", [P, NG, GW], F32R)
    wo_s = sb("wo_s", [P, 2 * NG, EMB], F32)
    rope = sb("rope", [P, 2, 2, 2, SEQ], F32)
    bqk_s = sb("bqk_s", [P, NG, 4], F32)
    bv_s = sb("bv_s", [P, 2 * NG], F32)
    bo_s = sb("bo_s", [P, 1], F32)
    ident = sb("ident", [P, P], F32)
    ident_b = sb("ident_b", [P, P], BF16)
    causal = sb("causal", [P, P], BF16)
    zero_row = sb("zero_row", [P, ROW], F32)
    bias_col = sb("bias_col", [P, 1], F32)
    acc = sb("acc", [P, SEQ], F32)
    stats = sb("stats", [P, QT, 6], F32)
    mv = sb("mv", [P, QT, 2], F32)
    veps = sb("veps", [P, QT], F32)
    mhalf = sb("mhalf", [P, QT], F32)
    wait_pad = sb("wait_pad", [P, 1], F32)
    rstd = sb("rstd", [P, QT], F32)
    xn = sb("xn", [P, QT, EMB], F32)
    stats2 = sb("stats2", [P, QT, 6], F32)
    mv2 = sb("mv2", [P, QT, 2], F32)
    veps2 = sb("veps2", [P, QT], F32)
    rstd2 = sb("rstd2", [P, QT], F32)
    xn2_t = sb("xn2_t", [P, QT, EMB], F32)
    xt2 = sb("xt2", [P, SEQ], F32)
    wg_s = sb("wg_s", [P, EXPERTS], F32)
    xt_hi = sb("xt_hi", [P, SEQ], F32R)
    xt_lo = sb("xt_lo", [P, SEQ], F32R)
    prod = sb("prod", [P, 2, 2, 2, SEQ], F32)
    rot = sb("rot", [P, 2, 2, SEQ], F32)
    halves = sb("halves", [P, 2, 4, SEQ], F32R)
    stack = [sb(f"stack{h}", [P, 3, SEQ], F32R) for h in range(GROUP)]
    v_parts = sb("v_parts", [P, 2, 3, QT, GW], BF16)
    v_rest = sb("v_rest", [P, 2, 2 * GW], F32)
    probs = [sb(f"probs{u}", [P, len(UNITS[u]) * P], F32) for u in range(NU)]
    pt_hi = [sb(f"pt_hi{u}", [P, len(UNITS[u]), P], F16) for u in range(NU)]
    pt_lo = [sb(f"pt_lo{u}", [P, len(UNITS[u]), P], F16) for u in range(NU)]
    negmax = sb("negmax", [P, 2, QT, GROUP], F32)
    rowsum = sb("rowsum", [P, 2, QT, GROUP], F32)
    recip = sb("recip", [P, QT, GROUP], F32)
    o_sb = sb("o_sb", [P, QT, GW], F32)
    ot = sb("ot", [P, 2, QT, P], F32)

    with ExitStack() as pctx:
        ps_s = pctx.enter_context(nc.psum_tensor("ps_s", [P, 2, 512], F32))
        ps_pt = pctx.enter_context(nc.psum_tensor("ps_pt", [P, 2, 512], F32))
        ps_o = pctx.enter_context(nc.psum_tensor("ps_o", [P, 2, 2, GW], F32))
        ps_m = pctx.enter_context(nc.psum_tensor("ps_m", [P, 2, 512], F32))

        in_w = sem("in_w")
        in_x0 = sem("in_x0")
        in_x = sem("in_x")
        filled = sem("filled")
        const = sem("const")
        wsplit_hi = sem("wsplit_hi")
        wsplit = sem("wsplit")
        ln = sem("ln")
        ln_rstd = sem("ln_rstd")
        xt_h = sem("xt_h")
        xt_l = sem("xt_l")
        chunk = sem("chunk")
        biased = sem("biased")
        ln2 = sem("ln2")
        xn2_saved = sem("xn2_saved")
        xt2_saved = sem("xt2_saved")
        ln2_rstd = sem("ln2_rstd")
        xt2d = sem("xt2d")
        lgd = sem("lgd")
        rmul = sem("rmul")
        radd = sem("radd")
        rhi = sem("rhi")
        rlo = sem("rlo")
        stacked = [sem(f"stacked{h}") for h in range(GROUP)]
        v1 = sem("v1")
        vr = sem("vr")
        v2 = sem("v2")
        v3 = sem("v3")
        scored = sem("scored")
        maxed = sem("maxed")
        expd = sem("expd")
        turned = sem("turned")
        pthi = sem("pthi")
        ptlo = sem("ptlo")
        pvd = sem("pvd")
        zeroed = sem("zeroed")
        rec = sem("rec")
        normed = sem("normed")
        otd = sem("otd")
        added = sem("added")
        resd = sem("resd")
        block = pctx.enter_context(nc.Block())

        def tiles_of(u):
            blocks = UNITS[u]
            return [(i, slice(P * min(n for n, b in enumerate(blocks) if b[0] == i),
                              P * (1 + max(n for n, b in enumerate(blocks) if b[0] == i))))
                    for i in sorted({b[0] for b in blocks})]

        def place(j):
            return j % NU, (j % STEPS) // NU, (j // STEPS) % 2

        @block.sync
        def _(sp):
            xr = x.rearrange("b (t p) e -> p (b t) e", p=P)
            sp.dma_start(x_res[:, QT:2 * QT, :], xr[:, 0:QT, :]).then_inc(in_x0, 16)
            raw = prod[:, :, :, :, :].rearrange("p a b c s -> p (a b c s)")
            sp.dma_start(raw[:, 0:4 * NG * P], wqk).then_inc(in_w, 16)
            sp.dma_start(raw[:, 4 * NG * P:4 * NG * P + NG * GW], wv).then_inc(in_w, 16)
            sp.dma_start(wo_s[:, :, :].rearrange("p g m -> p (g m)"), wo).then_inc(in_w, 16)
            sp.dma_start(ident[:, :], tables["ident"]).then_inc(in_w, 16)
            sp.dma_start(bqk_s[:, :, :], bqk).then_inc(in_w, 16)
            sp.dma_start(bv_s[:, :], bv).then_inc(in_w, 16)
            sp.dma_start(bo_s[:, :], bo.rearrange("(e o) -> e o", o=1)).then_inc(in_w, 16)
            sp.dma_start(ident_b[:, :], tables["ident_b"]).then_inc(in_w, 16)
            sp.dma_start(causal[:, :], tables["causal"]).then_inc(in_w, 16)
            sp.dma_start(rope[:, :, :, :, :], tables["rope"]).then_inc(in_w, 16)
            sp.dma_start(wg_s[:, :], tables["wg"]).then_inc(in_w, 16)
            sp.dma_start(x_res[:, 2 * QT:, :], xr[:, QT:, :]).then_inc(in_x, 16)

            def stack_head(G, h):
                used = STEPS * (G - 1) + NU * (h + 1)
                if not isinstance(G, int):
                    used = sp.snap(used)
                if h == 0:
                    sp.wait_ge(rlo, 2 * G + 2)
                if not isinstance(G, int) or G > 0:
                    sp.wait_ge(scored, used)
                for ab in range(2):
                    src = halves[HALF * h:HALF * (h + 1), ab, :, :].bitcast(F32)
                    dst = stack[h][HALF * ab:HALF * (ab + 1), :, :].bitcast(F32)
                    sp.dma_start(dst, src[:, 0:3, :]).then_inc(stacked[h], 16)
                    low = stack[h][2 * HALF + HALF * ab:2 * HALF + HALF * (ab + 1), :, :].bitcast(F32)
                    back = bass.AP(tensor=src.tensor, offset=src.offset + 3 * SEQ,
                                   ap=[list(src.ap[0]), [-SEQ, 3], [1, SEQ]])
                    sp.dma_start(low, back).then_inc(stacked[h], 16)

            def save_xn2(b):
                dst = xn2[:, bass.ds(b * QT, QT), 0:EMB] if isinstance(b, int) else xn2_slot(b)
                x_off = b * (P * SEQ) if isinstance(b, int) else sp.snap(b * (P * SEQ))
                sp.wait_ge(ln2, 13 * b + 13)
                sp.dma_start(dst, xn2_t[:, :, :]).then_inc(xn2_saved, 16)
                x_dst = bass.AP(tensor=xt2_all.tensor, offset=x_off, ap=[[SEQ, P], [1, SEQ]])
                sp.wait_ge(xt2d, b + 1)
                sp.dma_start(x_dst, xt2[:, :]).then_inc(xt2_saved, 16)

            def xn2_slot(b):
                full = xn2[:, 0:QT, 0:EMB]
                return bass.AP(tensor=full.tensor, offset=sp.snap(b * (QT * ROW)), ap=[list(a) for a in full.ap])

            def batch(b, last):
                for hg in range(NG - 1 if last else NG):
                    for h in range(GROUP):
                        stack_head(NG * b + hg + 1, h)
                    if hg == 1:
                        save_xn2(b)

            sp.wait_ge(const, 6)
            sp.dma_start(zeros_to, zero_row[:, :].rearrange("p (o r) -> p o r", o=1).broadcast_to([P, SLOTS // P, ROW])).then_inc(filled, 16)
            sp.sem_inc(xn2_saved, 16)
            sp.sem_inc(xt2_saved, 16)
            for h in range(GROUP):
                stack_head(0, h)
            with sp.Fori(0, BATCH - 1) as b:
                batch(b, False)
            batch(BATCH - 1, True)
            save_xn2(BATCH)
            for sm, v in ((xn2_saved, 16 * (BATCH + 2)), (xt2_saved, 16 * (BATCH + 2)), (filled, 16)):
                sp.wait_ge(sm, v)

        @block.gpsimd
        def _(pool):
            nc.gpsimd.memset(mhalf[:, :], -0.5).then_inc(const, 1)
            nc.gpsimd.memset(acc[:, :], 0.0).then_inc(const, 1)
            nc.gpsimd.memset(o_sb[:, :, :], 0.0).then_inc(const, 1)
            nc.gpsimd.memset(x_res[:, 0:QT, :], 0.0).then_inc(const, 1)
            nc.gpsimd.memset(zero_row[:, 0:EMB], 0.0).then_inc(const, 1)
            nc.gpsimd.memset(zero_row[:, EMB:ROW].bitcast(mybir.dt.uint32), NOBODY).then_inc(const, 1)
            pool.wait_ge(const, 4)

            def rstd_of(b):
                pool.wait_ge(ln, 13 * b + 9)
                nc.gpsimd.tensor_tensor(rstd[:, :], veps[:, :], mhalf[:, :], ALU.pow).then_inc(ln_rstd, 1)

            def rstd2_of(b):
                pool.wait_ge(ln2, 13 * b + 9)
                nc.gpsimd.tensor_tensor(rstd2[:, :], veps2[:, :], mhalf[:, :], ALU.pow).then_inc(ln2_rstd, 1)

            def rotate(G, kq, first):
                pool.wait_ge(rmul, 4 * G + 2 * kq + 2)
                if not first:
                    pool.wait_ge(rlo, 2 * (G - 1) + kq + 1)
                nc.gpsimd.tensor_tensor(rot[:, kq, :, :], prod[:, kq, 0, :, :], prod[:, kq, 1, :, :],
                                        ALU.add).then_inc(radd, 1)

            def v_third(G, c, par):
                vp = v_parts[:, par, :, 2 * c:2 * c + 2, :].rearrange("p k t d -> p k (t d)")
                pool.wait_ge(v2, 2 * G + c + 1)
                nc.gpsimd.tensor_tensor(vp[:, 2, :], v_rest[:, c, :], vp[:, 1, :], ALU.subtract).then_inc(v3, 1)

            def k_low(G):
                pool.wait_ge(rhi, 2 * G + 1)
                nc.gpsimd.tensor_tensor(halves[:, :, 3, :], rot[:, 0, :, :], halves[:, :, 0, :].bitcast(F32),
                                        ALU.subtract).then_inc(rlo, 1)

            def q_low(G):
                pool.wait_ge(rhi, 2 * G + 2)
                nc.gpsimd.tensor_tensor(halves[:, :, 2, :], rot[:, 1, :, :], halves[:, :, 1, :].bitcast(F32),
                                        ALU.subtract).then_inc(rlo, 1)

            def group_work(G, par, first, norm_of=None, next_k=True):
                k_low(G)
                rotate(G, 1, first)
                if norm_of is not None:
                    norm_of()
                q_low(G)
                for c in range(2):
                    v_third(G, c, par)
                if next_k:
                    rotate(G + 1, 0, False)

            def batch(b, last):
                for hg in range(NG):
                    if not (last and hg == NG - 1):
                        group_work(NG * b + hg + 1, (hg + 1) % 2, False, {1: lambda: rstd2_of(b), 2: lambda: rstd_of(b + 1)}.get(hg if not last or hg == 1 else None),
                                   not (last and hg == NG - 2))

            rstd_of(0)
            pool.wait_ge(wsplit, 2)
            rotate(0, 0, True)
            group_work(0, 0, True)
            with pool.Fori(0, BATCH - 1) as b:
                batch(b, False)
            batch(BATCH - 1, True)
            rstd2_of(BATCH)

        @block.scalar
        def _(act):
            act.sem_inc(expd, 3)
            act.wait_ge(in_w, 176)
            raw = prod[:, :, :, :, :].rearrange("p a b c s -> p (a b c s)")
            nqk = 4 * NG * P
            nc.scalar.copy(wqk_hi[:, :, :, :].rearrange("p g k m -> p (g k m)"), raw[:, 0:nqk]).then_inc(wsplit_hi, 1)
            nc.scalar.copy(wv_hi[:, :, :].rearrange("p g m -> p (g m)"), raw[:, nqk:nqk + NG * GW]).then_inc(wsplit_hi, 1)

            def xt_high(b, at):
                m, bank = at
                act.wait_ge(chunk, m + 1)
                nc.scalar.copy(xt_hi[:, :], ps_m[:, bank, :]).then_inc(xt_h, 1)

            def xt2_copy(b, at):
                m, bank = at
                act.wait_ge(chunk, m + 1)
                act.wait_ge(xt2_saved, 16 * b + 16)
                nc.scalar.copy(xt2[:, :], ps_m[:, bank, :]).then_inc(xt2d, 1)

            def high(G, kq, first):
                act.wait_ge(radd, 2 * G + kq + 1)
                if not first:
                    for h in range(GROUP):
                        act.wait_ge(stacked[h], 64 * G)
                nc.scalar.copy(halves[:, :, kq, :], rot[:, kq, :, :]).then_inc(rhi, 1)

            def v_first(G, c, par, at, first):
                m, bank = at
                act.wait_ge(chunk, m + 1)
                if not first:
                    act.wait_ge(pvd, STEPS * (G - 1) + 3)
                nc.scalar.copy(v_parts[:, par, 0, 2 * c:2 * c + 2, :].rearrange("p t d -> p (t d)"),
                               ps_m[:, bank, :]).then_inc(v1, 1)

            def exp(n, j):
                u, h, par = place(j)
                act.wait_ge(maxed, n + 1)
                act.wait_ge(turned, n + 1)
                for i, cols in tiles_of(u):
                    last = nc.scalar.activation(probs[u][:, cols], ps_s[:, j % 2, cols], ACT.Exp, bias=negmax[:, par, i, h:h + 1],
                                                accum_out=rowsum[:, par, i, h:h + 1])
                last.then_inc(expd, 1)

            def pt_high(n, j):
                u = j % NU
                act.wait_ge(turned, n + 4)
                act.wait_ge(pvd, n + 1)
                nc.scalar.copy(pt_hi[u][:, :, :].rearrange("p k q -> p (k q)"),
                               ps_pt[:, j % 2, 0:len(UNITS[u]) * P]).then_inc(pthi, 1)

            def ot_copy(c, at):
                m, bank = at
                act.wait_ge(chunk, m + 1)
                nc.scalar.copy(ot[:, :, 2 * c:2 * c + 2, :].rearrange("p f t q -> p f (t q)"),
                               ps_m[:, bank, :].rearrange("p (f q) -> p f q", f=2)).then_inc(otd, 1)

            def v_second(G, c, par):
                act.wait_ge(vr, 2 * G + c + 1)
                nc.scalar.copy(v_parts[:, par, 1, 2 * c:2 * c + 2, :].rearrange("p t d -> p (t d)"),
                               v_rest[:, c, :]).then_inc(v2, 1)

            def batch(b, last):
                for hg in range(NG):
                    tail = last and hg == NG - 1
                    G = NG * b + hg + 1
                    for t in range(STEPS):
                        j = STEPS * hg + t
                        if not (last and j + 2 >= BSTEPS):
                            exp(BSTEPS * b + j + 2, j + 2)
                        if not (last and j + 1 >= BSTEPS):
                            pt_high(BSTEPS * b + j + 1, j + 1)
                        for c in range(2):
                            if t == SLOT_OF[(OT0, OT1)[c]]:
                                ot_copy(c, chunk_at(b, hg, OT0 + c, last))
                        if not tail:
                            for c in range(2):
                                if t == SLOT_OF[(V01, V23)[c]]:
                                    v_first(G, c, (hg + 1) % 2, chunk_at(b, hg, (V01, V23)[c]), False)
                                if t == SLOT_OF[(V01, V23)[c]] + 1:
                                    v_second(G, c, (hg + 1) % 2)
                            if t == 1:
                                high(G, 0, False)
                            if t == 4:
                                high(G, 1, False)
                        if hg == 1 and t == SLOT_OF[LN2]:
                            xt2_copy(b, chunk_at(b, hg, LN2))
                        if hg == 2 and not last and t == SLOT_OF[LNT]:
                            xt_high(b + 1, chunk_at(b, hg, LNT))

            xt_high(0, (1, 1))
            act.wait_ge(wsplit, 2)
            for c in range(2):
                v_first(0, c, 0, (6 + c, c), True)
                v_second(0, c, 0)
            high(0, 0, True)
            high(0, 1, True)
            exp(0, 0)
            exp(1, 1)
            pt_high(0, 0)
            with act.Fori(0, BATCH - 1) as b:
                batch(b, False)
            batch(BATCH - 1, True)
            for c in range(2):
                ot_copy(c, end_chunk(c))
            xt2_copy(BATCH, end_chunk(4))

        @block.vector
        def _(dve):
            dve.sem_inc(ptlo, 2)
            dve.sem_inc(normed, 1)
            dve.sem_inc(added, 1)
            nc.vector.memset(ps_o[:, 1, :, :], 0.0).then_inc(zeroed, 1)
            nc.vector.memset(recip[:, :, :], 1.0).then_inc(zeroed, 1)
            dve.wait_ge(zeroed, 2)

            def ln_stats(slot, n, stats, mv, veps, ln):
                xs = x_res[:, bass.ds(slot * QT, QT), :]
                for t in range(QT):
                    nc.vector.bn_stats(stats[:, t, :], xs[:, t, :]).then_inc(ln, 1)
                dve.wait_ge(ln, 13 * n + 4)
                nc.vector.memset(wait_pad[:, :], 0.0)
                for t in range(QT):
                    nc.vector.bn_aggr(mv[:, t, :], stats[:, t, :]).then_inc(ln, 1)
                dve.wait_ge(ln, 13 * n + 8)
                nc.vector.tensor_scalar(veps[:, :], mv[:, :, 1], EPS, None, ALU.add).then_inc(ln, 1)

            def ln_apply(slot, n, out, mv, rstd, ln, ln_rstd):
                dve.wait_ge(ln_rstd, n + 1)
                xs = x_res[:, bass.ds(slot * QT, QT), :]
                for t in range(QT):
                    nc.vector.tensor_scalar(out[:, t, :], xs[:, t, :], mv[:, t, 0:1], rstd[:, t:t + 1],
                                            ALU.subtract, ALU.mult).then_inc(ln, 1)

            def take_logits(b, at):
                m, bank = at
                dve.wait_ge(chunk, m + 1)
                nc.vector.tensor_copy(logits[:, bass.ds(b * QT, QT), :].rearrange("p t e -> p (t e)"),
                                      ps_m[:, bank, 0:QT * EXPERTS]).then_inc(lgd, 1)

            def xt_low(b, bank):
                dve.wait_ge(xt_h, b + 1)
                nc.vector.tensor_tensor(xt_lo[:, :], ps_m[:, bank, :], xt_hi[:, :].bitcast(F32), ALU.subtract).then_inc(xt_l, 1)

            def products(G, kind, hg, at, first):
                m, bank = at
                kq, ab = kind // 2, kind % 2
                dve.wait_ge(chunk, m + 1)
                if not first:
                    dve.wait_ge(radd, 2 * (G - 1) + kq + 1)
                nc.vector.scalar_tensor_tensor(
                    out=prod[:, kq, ab, :, :], in0=ps_m[:, bank, :].rearrange("p (o s) -> p o s", o=1).broadcast_to([P, 2, SEQ]),
                    scalar=bqk_s[:, hg, kind:kind + 1], in1=rope[:, kq, ab, :, :],
                    op0=ALU.add, op1=ALU.mult).then_inc(rmul, 1)

            def v_remainder(G, c, par, bank, first):
                dve.wait_ge(v1, 2 * G + c + 1)
                if not first:
                    dve.wait_ge(v3, 2 * (G - 1) + c + 1)
                vp = v_parts[:, par, :, 2 * c:2 * c + 2, :].rearrange("p k t d -> p k (t d)")
                nc.vector.tensor_tensor(v_rest[:, c, :], ps_m[:, bank, :], vp[:, 0, :], ALU.subtract).then_inc(vr, 1)

            def rowmax(n, j):
                u, h, par = place(j)
                dve.wait_ge(scored, n + 1)
                for i, cols in tiles_of(u):
                    last = nc.vector.tensor_reduce(negmax[:, par, i, h:h + 1], ps_s[:, j % 2, cols], AX_X, ALU.max, negate=True)
                last.then_inc(maxed, 1)

            def pt_low(n, j):
                u = j % NU
                dve.wait_ge(pthi, n + 1)
                nc.vector.tensor_tensor(pt_lo[u][:, :, :].rearrange("p k q -> p (k q)"), ps_pt[:, j % 2, 0:len(UNITS[u]) * P],
                                        pt_hi[u][:, :, :].rearrange("p k q -> p (k q)"), ALU.subtract).then_inc(ptlo, 1)

            def reciprocals(g, par):
                dve.wait_ge(expd, STEPS * g + STEPS + 3)
                nc.vector.reciprocal(recip[:, :, :], rowsum[:, par, :, :]).then_inc(rec, 1)
                dve.wait_ge(rec, g + 1)

            def normalise(g, c):
                dve.wait_ge(pvd, STEPS * g + (STEPS - NU + 1 if c == 0 else STEPS) + 3)
                nc.vector.tensor_tensor(
                    o_sb[:, 2 * c:2 * c + 2, :].rearrange("p t (h d) -> p (t h) d", d=DHEAD),
                    ps_o[:, c, :, :].rearrange("p t (h d) -> p (t h) d", d=DHEAD),
                    recip[:, 2 * c:2 * c + 2, :].rearrange("p t h -> p (t h)").unsqueeze(2).broadcast_to([P, 2 * GROUP, DHEAD]),
                    ALU.mult).then_inc(normed, 1)

            def accumulate(hg, ordinal, at):
                m, bank = at
                dve.wait_ge(chunk, m + 1)
                if hg == 0:
                    nc.vector.tensor_scalar(acc[:, :], ps_m[:, bank, :], bias_col[:, :], None, ALU.add).then_inc(added, 1)
                else:
                    dve.wait_ge(added, ordinal + 1)
                    nc.vector.tensor_tensor(acc[:, :], ps_m[:, bank, :], acc[:, :], ALU.add).then_inc(added, 1)

            def residual(slot, at):
                m, bank = at
                dve.wait_ge(chunk, m + 1)
                xs = x_res[:, bass.ds(slot * QT, QT), :].rearrange("p t e -> p (t e)")
                nc.vector.tensor_tensor(xs, ps_m[:, bank, :], xs, ALU.add).then_inc(resd, 1)

            def batch(b, last):
                for hg in range(NG):
                    tail = last and hg == NG - 1
                    g = NG * b + hg
                    for t in range(STEPS):
                        j = STEPS * hg + t
                        if not (last and j + 3 >= BSTEPS):
                            rowmax(BSTEPS * b + j + 3, j + 3)
                        if t == STEPS - 1:
                            reciprocals(g, hg % 2)
                            normalise(g, 0)
                        if t == 0:
                            normalise(g - 1, 1)
                        if not (last and j + 1 >= BSTEPS):
                            pt_low(BSTEPS * b + j + 1, j + 1)
                        for kind in (QA, QB):
                            if t == SLOT_OF[kind] and not tail:
                                products(g + 1, kind, (hg + 1) % NG, chunk_at(b, hg, kind), False)
                        for kind in (KA, KB):
                            if t == SLOT_OF[kind] and not (last and hg >= NG - 2):
                                products(g + 2, kind, (hg + 2) % NG, chunk_at(b, hg, kind), False)
                        if not tail:
                            for c in range(2):
                                if t == SLOT_OF[(V01, V23)[c]]:
                                    v_remainder(g + 1, c, (hg + 1) % 2, chunk_at(b, hg, (V01, V23)[c])[1], False)
                        if t == SLOT_OF[WO]:
                            accumulate((hg + NG - 1) % NG, g, chunk_at(b, hg, WO, last))
                        if hg == 0 and t == SLOT_OF[BACK]:
                            residual(b, chunk_at(b, hg, BACK))
                        if hg == 1:
                            if t == 2:
                                dve.wait_ge(resd, b + 1)
                                nc.vector.memset(wait_pad[:, :], 0.0)
                                ln_stats(b, b, stats2, mv2, veps2, ln2)
                            if t == 7:
                                dve.wait_ge(xn2_saved, 16 * b + 16)
                                ln_apply(b, b, xn2_t, mv2, rstd2, ln2, ln2_rstd)
                        if hg == 2 and t == SLOT_OF[LG]:
                            take_logits(b, chunk_at(b, hg, LG, last))
                        if hg == 2 and not last:
                            if t == 0:
                                ln_stats(b + 2, b + 1, stats, mv, veps, ln)
                            if t == 5:
                                ln_apply(b + 2, b + 1, xn, mv, rstd, ln, ln_rstd)
                            if t == SLOT_OF[LNT]:
                                xt_low(b + 1, chunk_at(b, hg, LNT)[1])

            raw = prod[:, :, :, :, :].rearrange("p a b c s -> p (a b c s)")
            nqk = 4 * NG * P
            dve.wait_ge(in_x0, 16)
            ln_stats(1, 0, stats, mv, veps, ln)
            dve.wait_ge(in_w, 176)
            for w, (lo, hi, src) in enumerate((
                    (wqk_lo[:, :, :, :].rearrange("p g k m -> p (g k m)"), wqk_hi[:, :, :, :].rearrange("p g k m -> p (g k m)"), raw[:, 0:nqk]),
                    (wv_lo[:, :, :].rearrange("p g m -> p (g m)"), wv_hi[:, :, :].rearrange("p g m -> p (g m)"), raw[:, nqk:nqk + NG * GW]))):
                dve.wait_ge(wsplit_hi, w + 1)
                nc.vector.tensor_tensor(lo, src, hi.bitcast(F32), ALU.subtract).then_inc(wsplit, 1)
            dve.wait_ge(chunk, 1)
            nc.vector.tensor_tensor(bias_col[:, :], ps_m[:, 0, 0:1], bo_s[:, :], ALU.add).then_inc(biased, 1)
            ln_apply(1, 0, xn, mv, rstd, ln, ln_rstd)
            dve.wait_ge(biased, 1)
            xt_low(0, 1)
            dve.wait_ge(wsplit, 2)
            for k in range(4):
                products(0, k, 0, (2 + k, k % 2), True)
            for c in range(2):
                v_remainder(0, c, 0, c, True)
            for kind in (KA, KB):
                products(1, kind, 1, (8 + kind, kind % 2), False)
            for n in range(3):
                rowmax(n, n)
            pt_low(0, 0)
            dve.wait_ge(in_x, 16)
            with dve.Fori(0, BATCH - 1) as b:
                batch(b, False)
            batch(BATCH - 1, True)
            normalise(NG * BATCH - 1, 1)
            accumulate(NG - 1, NG * BATCH, end_chunk(2))
            residual(BATCH, end_chunk(3))
            dve.wait_ge(resd, BATCH + 1)
            ln_stats(BATCH, BATCH, stats2, mv2, veps2, ln2)
            dve.wait_ge(xn2_saved, 16 * BATCH + 16)
            ln_apply(BATCH, BATCH, xn2_t, mv2, rstd2, ln2, ln2_rstd)
            take_logits(BATCH, end_chunk(5))

        @block.tensor
        def _(pe):
            pe.sem_inc(turned, 3)
            pe.sem_inc(pvd, 3)

            def split3(out, a_hi, a_lo, b_hi, b_lo, start=True, stop=True):
                nc.tensor.matmul(out, a_hi, b_hi, start=start, stop=False)
                nc.tensor.matmul(out, a_hi, b_lo, start=False, stop=False)
                return nc.tensor.matmul(out, a_lo, b_hi, start=False, stop=stop)

            def bank_read(kind, g, hg, b, last):
                order = [(i, k) for i in range(NG) for k in chunks_of(i, last)]
                at = order.index((hg, kind))
                if at >= 2:
                    hg_of, before = order[at - 2]
                    g = g + hg_of - hg
                else:
                    before = (KA, KB)[at]
                    g = g - 1
                if before in (KA, KB):
                    pe.wait_ge(rmul, 4 * (g + 2) + before + 1)
                elif before in (QA, QB):
                    pe.wait_ge(rmul, 4 * (g + 1) + before + 1)
                elif before in (OT0, OT1):
                    pe.wait_ge(otd, 2 * g + 1 + before - OT0)
                elif before in (V01, V23):
                    pe.wait_ge(vr, 2 * (g + 1) + 1 + before - V01)
                elif before == WO:
                    pe.wait_ge(added, g + 2)
                elif before == BACK:
                    pe.wait_ge(resd, b + 1)
                elif before == LNT:
                    pe.wait_ge(xt_l, b + 2)
                elif before == LN2:
                    pe.wait_ge(xt2d, b + 1)
                elif before == LG:
                    pe.wait_ge(lgd, b + 1)

            def project_qk(kind, hg, bank):
                split3(ps_m[:, bank, :], wqk_hi[:, hg, kind, :], wqk_lo[:, hg, kind, :], xt_hi[:, :], xt_lo[:, :]).then_inc(chunk, 1)

            def project_v(c, hg, bank):
                for u in range(2):
                    t = 2 * c + u
                    last = split3(ps_m[:, bank, u * GW:(u + 1) * GW], xt_hi[:, t * P:(t + 1) * P], xt_lo[:, t * P:(t + 1) * P],
                                  wv_hi[:, hg, :], wv_lo[:, hg, :])
                last.then_inc(chunk, 1)

            def project(kind, hg, bank):
                if kind <= QB:
                    project_qk(kind, hg, bank)
                else:
                    project_v(0 if kind == V01 else 1, hg, bank)

            def turn_x(b, xn, ln, bank):
                pe.wait_ge(ln, 13 * b + 13)
                for t in range(QT):
                    last = nc.tensor.transpose(ps_m[:, bank, t * P:(t + 1) * P], xn[:, t, :], ident[:, :])
                last.then_inc(chunk, 1)

            def router(b, bank):
                pe.wait_ge(xt2d, b + 1)
                for t in range(QT):
                    last = nc.tensor.matmul(ps_m[:, bank, t * EXPERTS:(t + 1) * EXPERTS], xt2[:, t * P:(t + 1) * P], wg_s[:, :],
                                            start=True, stop=True)
                last.then_inc(chunk, 1)

            def turn_o(c, n_norm, bank):
                pe.wait_ge(normed, n_norm)
                for u in range(2):
                    for f in range(2):
                        k = 2 * f + u
                        last = nc.tensor.transpose(ps_m[:, bank, k * P:(k + 1) * P], o_sb[:, 2 * c + u, f * P:(f + 1) * P], ident[:, :])
                last.then_inc(chunk, 1)

            def out_project(hg, bank):
                for f in range(2):
                    last = nc.tensor.matmul(ps_m[:, bank, :], wo_s[:, 2 * hg + f, :], ot[:, f, :, :].rearrange("p t q -> p (t q)"),
                                            start=(f == 0), stop=(f == 1))
                last.then_inc(chunk, 1)

            def turn_back(bank):
                for t in range(QT):
                    last = nc.tensor.transpose(ps_m[:, bank, t * P:(t + 1) * P], acc[:, t * P:(t + 1) * P], ident[:, :])
                last.then_inc(chunk, 1)

            def scores(n, j, g):
                u, h, _ = place(j)
                if u == 0:
                    pe.wait_ge(stacked[h], 64 * (g + 1))
                pe.wait_ge(expd, n + 2)
                st = stack[h]
                for i, cols in tiles_of(u):
                    out = ps_s[:, j % 2, cols]
                    q0, w = i * P, (i + 1) * P
                    nc.tensor.matmul(out, st[:, 1, q0:q0 + P], st[:, 0, 0:w], start=True, stop=False)
                    nc.tensor.matmul(out, st[:, 2, q0:q0 + P], st[:, 0, 0:w], start=False, stop=False)
                    last = nc.tensor.matmul(out[:, i * P:w], ident_b[:, :], causal[:, :], start=False, stop=True)
                last.then_inc(scored, 1)

            def turn_p(n, j):
                u = j % NU
                pe.wait_ge(expd, n + 4)
                pe.wait_ge(ptlo, n + 1)
                for k in range(len(UNITS[u])):
                    last = nc.tensor.transpose(ps_pt[:, j % 2, k * P:(k + 1) * P], probs[u][:, k * P:(k + 1) * P], ident[:, :])
                last.then_inc(turned, 1)

            def values(n, j, g):
                u, h, par = place(j)
                if j % STEPS == 0:
                    pe.wait_ge(v3, 2 * g + 2)
                if h == 0 and u < 2:
                    pe.wait_ge(normed, 2 * g + u + 1)
                pe.wait_ge(ptlo, n + 3)
                for blk, (i, k) in enumerate(UNITS[u]):
                    out = ps_o[:, i // 2, i % 2, h * DHEAD:(h + 1) * DHEAD]
                    for pt, parts in ((pt_hi[u], (0, 1, 2)), (pt_lo[u], (0, 1))):
                        for v in parts:
                            last = nc.tensor.matmul(out, pt[:, blk, :], v_parts[:, par, v, k, h * DHEAD:(h + 1) * DHEAD],
                                                    start=(k == 0 and pt is pt_hi[u] and v == 0),
                                                    stop=(k == i and pt is pt_lo[u] and v == 1))
                last.then_inc(pvd, 1)

            def issue(kind, g, hg, b, bank):
                if kind in (KA, KB):
                    if hg == 2:
                        pe.wait_ge(xt_l, b + 2)
                    project(kind, (hg + 2) % NG, bank)
                elif kind in (QA, QB, V01, V23):
                    project(kind, (hg + 1) % NG, bank)
                elif kind in (OT0, OT1):
                    turn_o(kind - OT0, 2 * g + kind - OT0 + 1, bank)
                elif kind == WO:
                    pe.wait_ge(otd, 2 * g + 2)
                    out_project((hg + NG - 1) % NG, bank)
                elif kind == BACK:
                    pe.wait_ge(added, g + 2)
                    turn_back(bank)
                elif kind == LNT:
                    turn_x(b + 1, xn, ln, bank)
                elif kind == LN2:
                    turn_x(b, xn2_t, ln2, bank)
                elif kind == LG:
                    router(b, bank)

            def batch(b, last):
                for hg in range(NG):
                    g = NG * b + hg
                    for t in range(STEPS):
                        j = STEPS * hg + t
                        n = BSTEPS * b + j
                        if not (last and j + 3 >= BSTEPS):
                            scores(n + 3, j + 3, g + (t + 3) // STEPS)
                        if not (last and j + 1 >= BSTEPS):
                            turn_p(n + 1, j + 1)
                        for kind in chunks_of(hg, last):
                            if t == SLOT_OF[kind]:
                                bank_read(kind, g, hg, b, last)
                                issue(kind, g, hg, b, chunk_at(b, hg, kind, last)[1])
                        values(n, j, g)

            pe.wait_ge(const, 4)
            pe.wait_ge(in_w, 176)
            for k in range(2 * NG):
                last = nc.tensor.matmul(ps_m[:, 0, 0:1], wo_s[:, k, :], bv_s[:, k:k + 1], start=(k == 0), stop=(k == 2 * NG - 1))
            last.then_inc(chunk, 1)
            turn_x(0, xn, ln, 1)
            pe.wait_ge(wsplit, 2)
            pe.wait_ge(xt_l, 1)
            for m, (kind, hg, read, value) in enumerate((
                    (KA, 0, biased, 1), (KB, 0, xt_l, 1), (QA, 0, rmul, 1), (QB, 0, rmul, 2), (V01, 0, rmul, 3),
                    (V23, 0, rmul, 4), (KA, 1, vr, 1), (KB, 1, vr, 2))):
                pe.wait_ge(read, value)
                project(kind, hg, m % 2)
            for n in range(3):
                scores(n, n, 0)
            turn_p(0, 0)
            with pe.Fori(0, BATCH - 1) as b:
                batch(b, False)
            batch(BATCH - 1, True)
            ends = NG * BATCH
            pe.wait_ge(otd, 2 * ends)
            turn_o(0, 2 * ends + 1, end_chunk(0)[1])
            pe.wait_ge(added, ends + 1)
            turn_o(1, 2 * ends + 2, end_chunk(1)[1])
            pe.wait_ge(otd, 2 * ends + 2)
            out_project(NG - 1, end_chunk(2)[1])
            pe.wait_ge(added, ends + 2)
            turn_back(end_chunk(3)[1])
            turn_x(BATCH, xn2_t, ln2, end_chunk(4)[1])
            pe.wait_ge(resd, BATCH + 1)
            router(BATCH, end_chunk(5)[1])


def mixture(nc, ctx, x_res, xn2, logits, xt2_all, routed, base, w_shared, w_experts, tables, out):
    def sb(name, shape, dt):
        return ctx.enter_context(nc.sbuf_tensor(name, shape, dt))

    def sem(name):
        return ctx.enter_context(nc.semaphore(name))

    E, T = EXPERTS, TILES
    WALL = 3 * INTER
    ws_hi = sb("ws_hi", [P, WALL], F32R)
    ws_lo = sb("ws_lo", [P, WALL], F32R)
    w_raw = sb("w_raw", [P, 2, WALL], F32)
    we = sb("we", [P, 2, E, WALL], F32R)
    we_hi, we_lo = we[:, 0, :, :], we[:, 1, :, :]
    ident = sb("ident2", [P, P], F32)
    tri = sb("tri", [P, P], BF16)
    ones = sb("ones2", [P, P], BF16)
    rev = sb("rev", [P, E], F32)
    tile_no = sb("tile_no", [P, RTILES], F32)
    token_no = sb("token_no", [P, T], U32)
    top = sb("top", [P, T], F32)
    hit = sb("hit", [P, T, E], F32)
    hot = sb("hot", [P, T, E], F32)
    hot_b = sb("hot_b", [P, T, E], BF16)
    cum = [sb(f"cum{i}", [P, E, T], F32) for i in range(2)]
    excl = sb("excl", [P, E, T], F32)
    count_i = sb("count_i", [P, E], I32)
    tiles_i = sb("tiles_i", [P, E], I32)
    ends = [sb(f"ends{i}", [P, E], F32) for i in range(2)]
    starts = sb("starts", [P, E], F32)
    slot_f = sb("slot_f", [P, T], F32)
    slot_u = sb("slot_u", [P, T], U32)
    past = sb("past", [P, RTILES, E], F32)
    owner_f = sb("owner_f", [P, RTILES], F32)
    owner = sb("owner", [P, RTILES], I32)
    xt_raw = sb("xt_raw", [P, 2, SEQ], F32)
    xt_hi = sb("fxt_hi", [P, 2, SEQ], F32R)
    xt_lo = sb("fxt_lo", [P, 2, SEQ], F32R)
    rxt_hi = sb("rxt_hi", [P, 2, P], F32R)
    rxt_lo = sb("rxt_lo", [P, 2, P], F32R)
    acts = sb("acts", [P, 4, INTER], F32)
    gate, hid = acts[:, 0:2, :], acts[:, 2:4, :]
    ws_raw = acts[:, 0:3, :].rearrange("p c w -> p (c w)")
    ht_hi = sb("ht_hi", [P, 2, INTER], F32R)
    ht_lo = sb("ht_lo", [P, 2, INTER], F32R)
    rows = sb("rows", [P, RING, ROW], F32)
    yt = rows[:, :, :].rearrange("p v r -> p (v r)")[:, 0:2 * SEQ].rearrange("p (v s) -> p v s", v=2)
    res = sb("res", [P, RING, EMB], F32)

    ps_h = ctx.enter_context(nc.psum_tensor("ps_h", [P, 2, 2, 512], F32))
    ps_x = ctx.enter_context(nc.psum_tensor("ps_x", [P, 512], F32))
    ps_t = ctx.enter_context(nc.psum_tensor("ps_t", [P, 512], F32))
    ps_y = ctx.enter_context(nc.psum_tensor("ps_y", [P, 2, 512], F32))

    in_c = sem("fin_c")
    in_ws = sem("fin_ws")
    in_w = [sem(f"fin_w{i}") for i in range(2)]
    in_x = [sem(f"fin_x{i}") for i in range(2)]
    wshi = sem("wshi")
    wslo = sem("wslo")
    whi = sem("whi")
    wlo = sem("wlo")
    rt = sem("rt")
    hotd = sem("hotd")
    counted = sem("counted")
    slotted = sem("slotted")
    owned = sem("owned")
    spread = sem("spread")
    sxh = sem("sxh")
    sxl = sem("sxl")
    sh = sem("sh")
    sg = sem("sg")
    shm = sem("shm")
    shh = sem("shh")
    shl = sem("shl")
    syc = sem("syc")
    sye = sem("sye")
    syt = sem("syt")
    sr = sem("sr")
    based = sem("based")
    rin = [sem(f"rin{i}") for i in range(RING)]
    gin = [sem(f"gin{i}") for i in range(RING)]
    outd = [sem(f"outd{i}") for i in range(RING)]
    rxt = sem("rxt")
    rxh = sem("rxh")
    rxl = sem("rxl")
    rh = sem("rh")
    rg = sem("rg")
    rhm = sem("rhm")
    rht = sem("rht")
    rhh = sem("rhh")
    rhl = sem("rhl")
    ry = sem("ry")
    rp = sem("rp")
    ra = sem("ra")
    zero = sem("zero")
    block = ctx.enter_context(nc.Block())
    PAIRS = BATCH // 2
    TURNS = RTILES // RING

    @block.sync
    def _(sp):
        sp.dma_start(ws_raw[:, :], w_shared).then_inc(in_ws, 16)
        for dst, name in ((ident[:, :], "ident"), (tri[:, :], "tri"), (ones[:, :], "ones_b"), (rev[:, :], "rev"),
                          (tile_no[:, :], "tile_no"), (token_no[:, :], "token_no")):
            sp.dma_start(dst, tables[name]).then_inc(in_c, 16)
        for v in range(2):
            sp.dma_start(xt_raw[:, v, :], xt2_all[v + 1]).then_inc(in_x[v], 16)
            sp.dma_start(w_raw[:, v, :], w_experts[v]).then_inc(in_w[v], 16)

        def pair(k, last):
            for v in range(2):
                b = 2 * k + v
                if not last:
                    e_off = sp.snap((b + 2) * (P * WALL))
                    x_off = sp.snap((b + 3) * (P * SEQ))
                    sp.wait_ge(sxl, b + 1)
                    sp.dma_start(xt_raw[:, v, :], bass.AP(tensor=xt2_all.tensor, offset=x_off, ap=[[SEQ, P], [1, SEQ]])
                                 ).then_inc(in_x[v], 16)
                    sp.wait_ge(wlo, b + 1)
                    sp.dma_start(w_raw[:, v, :], bass.AP(tensor=w_experts.tensor, offset=e_off, ap=[[WALL, P], [1, WALL]])
                                 ).then_inc(in_w[v], 16)
            for v in range(2):
                b = 2 * k + v
                dst, src = base[bass.ds(b * SEQ, SEQ), :], x_res[:, bass.ds((b + 1) * QT, QT), :]
                if not last:
                    d_off, s_off = sp.snap(b * (SEQ * EMB)), sp.snap((b + 1) * (QT * EMB))
                    full = x_res[:, 0:QT, :]
                    dst = bass.AP(tensor=base.tensor, offset=d_off, ap=[[EMB, P], [P * EMB, QT], [1, EMB]])
                    src = bass.AP(tensor=full.tensor, offset=s_off, ap=[list(a) for a in full.ap])
                else:
                    dst = dst.rearrange("(t p) e -> p t e", p=P)
                sp.wait_ge(sr, b + 3)
                sp.dma_start(dst, src).then_inc(based, 16)

        with sp.Fori(0, PAIRS - 1) as k:
            pair(k, False)
        pair(PAIRS - 1, True)

        sp.wait_ge(spread, 16 * T)

        for v in range(RING):
            sp.dma_start(rows[:, v, :], routed[v * P:(v + 1) * P, :]).then_inc(rin[v], 16)
        with sp.Fori(1, TURNS) as k:
            for v in range(RING):
                src = bass.AP(tensor=routed.tensor, offset=sp.snap((RING * k + v) * (P * ROW)), ap=[[ROW, P], [1, ROW]])
                sp.wait_ge(outd[v], 16 * k)
                sp.dma_start(rows[:, v, :], src).then_inc(rin[v], 16)
        sp.wait_ge(based, 16 * BATCH)
        for v in range(RING):
            sp.wait_ge(outd[v], 16 * TURNS)

    @block.gpsimd
    def _(pool):
        nc.gpsimd.memset(res[:, :, :], 0.0).then_inc(zero, 1)
        pool.wait_ge(slotted, 2)
        pool.wait_ge(zero, 1)
        for b in range(BATCH):
            for t in range(QT * b, QT * (b + 1)):
                nc.gpsimd.indirect_dma_start(
                    out=routed, out_offset=bass.IndirectOffsetOnAxis(ap=slot_u[:, t:t + 1], axis=0),
                    in_=xn2[:, QT + t, :], in_offset=None).then_inc(spread, 16)
            pool.wait_ge(whi, b + 1)
            nc.gpsimd.tensor_tensor(we_lo[:, b, :], w_raw[:, b % 2, :], we_hi[:, b, :].bitcast(F32), ALU.subtract).then_inc(wlo, 1)

        bound = pool.to_reg(TOKENS - 1)

        def gather(k, v):
            pool.wait_ge(rin[v], 16 * k + 16)
            nc.gpsimd.indirect_dma_start(
                out=res[:, v, :], out_offset=None, in_=base,
                in_offset=bass.IndirectOffsetOnAxis(ap=rows[:, v, EMB:ROW].bitcast(U32), axis=0),
                bounds_check=bound, oob_is_err=False).then_inc(gin[v], 16)

        def scatter(k, v):
            pool.wait_ge(ra, RING * k + v + 3)
            nc.gpsimd.indirect_dma_start(
                out=out, out_offset=bass.IndirectOffsetOnAxis(ap=rows[:, v, EMB:ROW].bitcast(U32), axis=0),
                in_=res[:, v, :], in_offset=None, bounds_check=bound, oob_is_err=False).then_inc(outd[v], 16)

        pool.wait_ge(based, 16 * BATCH)
        for v in range(AHEAD):
            gather(0, v)

        def turn(k, last):
            for v in range(RING):
                if v + AHEAD < RING:
                    gather(k, v + AHEAD)
                elif not last:
                    gather(k + 1, v + AHEAD - RING)
                scatter(k, v)

        for k in range(TURNS):
            turn(k, k == TURNS - 1)

    @block.scalar
    def _(act):
        act.sem_inc(sye, 2)
        act.wait_ge(in_ws, 16)
        nc.scalar.copy(ws_hi[:, :], ws_raw[:, :]).then_inc(wshi, 1)

        def x_high(k, v):
            act.wait_ge(in_x[v], 16 * k + 16)
            nc.scalar.copy(xt_hi[:, v, :], xt_raw[:, v, :]).then_inc(sxh, 1)

        def gelu(s, p):
            act.wait_ge(sh, s + 1)
            act.wait_ge(shm, s + 1)
            nc.scalar.activation(gate[:, p, :], ps_h[:, p, 0, :], ACT.Gelu).then_inc(sg, 1)

        def h_high(s, p):
            act.wait_ge(shm, s + 3)
            act.wait_ge(syc, s + 1)
            nc.scalar.copy(ht_hi[:, p, :], hid[:, p, :]).then_inc(shh, 1)

        def w_high(k, v):
            act.wait_ge(in_w[v], 16 * k + 16)
            e = 2 * k + v
            nc.scalar.copy(we_hi[:, bass.ds(e, 1), :].rearrange("p o w -> p (o w)"), w_raw[:, v, :]).then_inc(whi, 1)

        def y_copy(b, v):
            act.wait_ge(syc, CHUNK * b + CHUNK + 2)
            act.wait_ge(syt, b + 1)
            nc.scalar.copy(yt[:, v, :], ps_y[:, v, :]).then_inc(sye, 1)

        def pair(k, last):
            for v in range(2):
                for c in range(CHUNK):
                    s, p = 8 * k + CHUNK * v + c, c % 2
                    ending = last and v == 1
                    if c == 1 and not ending:
                        x_high(k + v, 1 - v)
                    if not (ending and c == CHUNK - 1):
                        h_high(s + 1, 1 - p)
                    if not (ending and c >= CHUNK - 2):
                        gelu(s + 2, p)
                    if c == 2:
                        w_high(k, v)
                y_copy(2 * k + v, v)

        x_high(0, 0)
        gelu(0, 0)
        h_high(0, 0)
        gelu(1, 1)
        with act.Fori(0, PAIRS - 1) as k:
            pair(k, False)
        pair(PAIRS - 1, True)

        def row_high(j, v):
            act.wait_ge(rxt, j + 1)
            nc.scalar.copy(rxt_hi[:, v % 2, :], ps_x[:, 0:P]).then_inc(rxh, 1)

        def row_gelu(j, v):
            act.wait_ge(rh, j + 1)
            act.wait_ge(rhm, j + 1)
            nc.scalar.activation(gate[:, v % 2, :], ps_h[:, v % 2, 0, :], ACT.Gelu).then_inc(rg, 1)

        def turned_high(j, v):
            act.wait_ge(rht, j + 1)
            nc.scalar.copy(ht_hi[:, v % 2, :], ps_t[:, :]).then_inc(rhh, 1)

        def turn(k, last):
            for v in range(RING):
                j = RING * k + v
                if not (last and v + 3 >= RING):
                    row_high(j + 3, v + 3)
                if not (last and v + 2 >= RING):
                    row_gelu(j + 2, v)
                if not (last and v + 1 >= RING):
                    turned_high(j + 1, v + 1)

        for v in range(2):
            row_high(v, v)
            row_gelu(v, v)
        row_high(2, 2)
        turned_high(0, 0)
        with act.Fori(0, TURNS - 1) as k:
            turn(k, False)
        turn(TURNS - 1, True)

    @block.vector
    def _(dve):
        dve.sem_inc(shm, 2)
        dve.sem_inc(sr, 2)
        dve.sem_inc(rhm, 2)
        dve.sem_inc(rxl, 1)
        dve.sem_inc(rhl, 1)
        dve.sem_inc(ra, 2)
        V = nc.vector
        dve.wait_ge(wshi, 1)
        nc.vector.tensor_tensor(ws_lo[:, :], ws_raw[:, :], ws_hi[:, :].bitcast(F32), ALU.subtract).then_inc(wslo, 1)

        def x_low(b, v):
            dve.wait_ge(sxh, b + 1)
            V.tensor_tensor(xt_lo[:, v, :], xt_raw[:, v, :], xt_hi[:, v, :].bitcast(F32), ALU.subtract).then_inc(sxl, 1)

        x_low(0, 0)

        steps = [0]

        def link(ins):
            steps[0] += 1
            ins.then_inc(rt, 1)
            dve.wait_ge(rt, steps[0])

        lg = logits[:, QT:, :]
        by_t = lambda a: a[:, :].unsqueeze(2).broadcast_to([P, T, E])
        by_e = lambda a: a[:, :].unsqueeze(1).broadcast_to([P, T, E])
        dve.wait_ge(in_c, 96)
        link(V.tensor_reduce(top[:, :], lg, AX_X, ALU.max))
        link(V.tensor_tensor(hit[:, :, :], lg, by_t(top), ALU.is_equal))
        link(V.tensor_tensor(hit[:, :, :], hit[:, :, :], by_e(rev), ALU.mult))
        link(V.tensor_reduce(top[:, :], hit[:, :, :], AX_X, ALU.max))
        link(V.tensor_tensor(hot[:, :, :], by_e(rev), by_t(top), ALU.is_equal))
        V.tensor_copy(hot_b[:, :, :], hot[:, :, :]).then_inc(hotd, 1)
        V.tensor_copy(xn2[:, QT:, EMB:ROW].bitcast(U32), token_no[:, :].unsqueeze(2)).then_inc(slotted, 1)
        dve.wait_ge(counted, 1)
        ranks = ps_t[:, 0:T * E].rearrange("p (t e) -> p t e", e=E)
        counts = ps_t[:, T * E:2 * T * E].rearrange("p (t e) -> p e t", e=E)
        link(V.tensor_copy(cum[0][:, :, :], counts))
        src, d = 0, 1
        while d < T:
            V.tensor_copy(cum[1 - src][:, :, 0:d], cum[src][:, :, 0:d])
            link(V.tensor_tensor(cum[1 - src][:, :, d:], cum[src][:, :, d:], cum[src][:, :, 0:T - d], ALU.add))
            src, d = 1 - src, 2 * d
        link(V.tensor_tensor(excl[:, :, :], counts, cum[src][:, :, :], ALU.subtract))
        link(V.tensor_scalar(count_i[:, :], cum[src][:, :, T - 1], float(P - 1), None, ALU.add))
        link(V.tensor_scalar(tiles_i[:, :], count_i[:, :], P.bit_length() - 1, None, ALU.arith_shift_right))
        link(V.tensor_copy(ends[0][:, :], tiles_i[:, :]))
        esrc, d = 0, 1
        while d < E:
            V.tensor_copy(ends[1 - esrc][:, 0:d], ends[esrc][:, 0:d])
            link(V.tensor_tensor(ends[1 - esrc][:, d:], ends[esrc][:, d:], ends[esrc][:, 0:E - d], ALU.add))
            esrc, d = 1 - esrc, 2 * d
        link(V.tensor_tensor(starts[:, :], ends[esrc][:, :], tiles_i[:, :], ALU.subtract))
        link(V.tensor_tensor(hit[:, :, :], ranks, excl[:, :, :].rearrange("p e t -> p t e"), ALU.subtract))
        link(V.scalar_tensor_tensor(out=hit[:, :, :], in0=by_e(starts), scalar=float(P), in1=hit[:, :, :],
                                    op0=ALU.mult, op1=ALU.add))
        link(V.tensor_tensor(hit[:, :, :], hit[:, :, :], hot[:, :, :], ALU.mult))
        link(V.tensor_reduce(slot_f[:, :], hit[:, :, :], AX_X, ALU.add))
        V.tensor_copy(slot_u[:, :], slot_f[:, :]).then_inc(slotted, 1)
        tiles_by_e = [P, RTILES, E]
        link(V.tensor_tensor(past[:, :, :], tile_no[:, :].unsqueeze(2).broadcast_to(tiles_by_e),
                             ends[esrc][:, :].unsqueeze(1).broadcast_to(tiles_by_e), ALU.is_ge))
        link(V.tensor_reduce(owner_f[:, :], past[:, :, :], AX_X, ALU.add))
        V.tensor_scalar(owner[:, :], owner_f[:, :], float(E - 1), None, ALU.min).then_inc(owned, 1)

        def multiply(s, p):
            dve.wait_ge(sg, s + 1)
            V.tensor_tensor(hid[:, p, :], ps_h[:, p, 1, :], gate[:, p, :], ALU.mult).then_inc(shm, 1)

        def h_low(s, p):
            dve.wait_ge(shh, s + 1)
            V.tensor_tensor(ht_lo[:, p, :], hid[:, p, :], ht_hi[:, p, :].bitcast(F32), ALU.subtract).then_inc(shl, 1)

        def add_shared(b):
            dve.wait_ge(syt, b + 3)
            xs = x_res[:, bass.ds((b + 1) * QT, QT), :].rearrange("p t e -> p (t e)")
            V.tensor_tensor(xs, ps_t[:, :], xs, ALU.add).then_inc(sr, 1)

        def pair(k, last):
            for v in range(2):
                b = 2 * k + v
                for c in range(CHUNK):
                    s, p = 8 * k + CHUNK * v + c, c % 2
                    ending = last and v == 1
                    if c == 1 and not ending:
                        x_low(b + 1, 1 - v)
                    if not (ending and c == CHUNK - 1):
                        h_low(s + 1, 1 - p)
                    if not (ending and c >= CHUNK - 2):
                        multiply(s + 2, p)
                    if v == 1 and c == 0:
                        add_shared(b - 1)
            add_shared(b)

        multiply(0, 0)
        h_low(0, 0)
        multiply(1, 1)
        with dve.Fori(0, PAIRS - 1) as k:
            pair(k, False)
        pair(PAIRS - 1, True)

        def row_low(j, v):
            dve.wait_ge(rxh, j + 1)
            V.tensor_tensor(rxt_lo[:, v % 2, :], ps_x[:, 0:P], rxt_hi[:, v % 2, :].bitcast(F32), ALU.subtract).then_inc(rxl, 1)

        def row_multiply(j, v):
            dve.wait_ge(rg, j + 1)
            V.tensor_tensor(hid[:, v % 2, :], ps_h[:, v % 2, 1, :], gate[:, v % 2, :], ALU.mult).then_inc(rhm, 1)

        def turned_low(j, v):
            dve.wait_ge(rhh, j + 1)
            V.tensor_tensor(ht_lo[:, v % 2, :], ps_t[:, :], ht_hi[:, v % 2, :].bitcast(F32), ALU.subtract).then_inc(rhl, 1)

        def add_rows(j, k, v):
            dve.wait_ge(ry, j + 1)
            dve.wait_ge(gin[v], 16 * k + 16)
            V.tensor_tensor(res[:, v, :], ps_y[:, v % 2, 0:EMB], res[:, v, :], ALU.add).then_inc(rp, 1)
            dve.wait_ge(rp, j + 1)
            V.tensor_tensor(res[:, v, :], ps_y[:, v % 2, EMB:2 * EMB], res[:, v, :], ALU.add).then_inc(ra, 1)

        def turn(k, last):
            for v in range(RING):
                j = RING * k + v
                if not (last and v + 3 >= RING):
                    row_low(j + 3, v + 3)
                if not (last and v + 2 >= RING):
                    row_multiply(j + 2, v)
                if not (last and v + 1 >= RING):
                    turned_low(j + 1, v + 1)
                add_rows(j, k, v)

        for v in range(2):
            row_low(v, v)
            row_multiply(v, v)
        row_low(2, 2)
        turned_low(0, 0)
        with dve.Fori(0, TURNS - 1) as k:
            turn(k, False)
        turn(TURNS - 1, True)

    @block.tensor
    def _(pe):
        pe.sem_inc(syc, 2)
        pe.sem_inc(syt, 2)

        def split3(o, a_hi, a_lo, b_hi, b_lo, start, stop, skip=False):
            nc.tensor.matmul(o, a_hi, b_hi, start=start, stop=False, skip_group_check=skip)
            nc.tensor.matmul(o, a_hi, b_lo, start=False, stop=False, skip_group_check=skip)
            return nc.tensor.matmul(o, a_lo, b_hi, start=False, stop=stop, skip_group_check=skip)

        pe.wait_ge(in_c, 96)
        pe.wait_ge(hotd, 1)
        oh = hot_b[:, :, :].rearrange("p t e -> p (t e)")
        nc.tensor.matmul(ps_t[:, 0:T * E], tri[:, :], oh, start=True, stop=True)
        nc.tensor.matmul(ps_t[:, T * E:2 * T * E], ones[:, :], oh, start=True, stop=True).then_inc(counted, 1)

        def hidden(s, v, c):
            pe.wait_ge(shm, s + 1)
            for w in range(2):
                cols = slice(w * INTER + c * P, w * INTER + (c + 1) * P)
                last = split3(ps_h[:, c % 2, w, :], ws_hi[:, cols], ws_lo[:, cols], xt_hi[:, v, :], xt_lo[:, v, :], True, True)
            last.then_inc(sh, 1)

        def project(s, b, v, c):
            if c == 0:
                pe.wait_ge(sye, b + 1)
            pe.wait_ge(shl, s + 1)
            w3 = slice(2 * INTER + c * EMB, 2 * INTER + (c + 1) * EMB)
            split3(ps_y[:, v, :], ws_hi[:, w3], ws_lo[:, w3], ht_hi[:, c % 2, :], ht_lo[:, c % 2, :],
                   c == 0, c == CHUNK - 1).then_inc(syc, 1)

        def turn_y(b, v):
            pe.wait_ge(sye, b + 3)
            pe.wait_ge(sr, b + 2)
            for i in range(QT):
                last = nc.tensor.transpose(ps_t[:, i * P:(i + 1) * P], yt[:, v, i * P:(i + 1) * P], ident[:, :])
            last.then_inc(syt, 1)

        def pair(k, last):
            for v in range(2):
                b = 2 * k + v
                for c in range(CHUNK):
                    s = 8 * k + CHUNK * v + c
                    if c < CHUNK - 2:
                        hidden(s + 2, v, c + 2)
                    elif not (last and v == 1):
                        if c == CHUNK - 2:
                            pe.wait_ge(sxl, b + 2)
                        hidden(s + 2, 1 - v, c + 2 - CHUNK)
                    if v == 1 and c == 0:
                        turn_y(b - 1, 0)
                    project(s, b, v, c)
            turn_y(b, 1)

        pe.wait_ge(wslo, 1)
        pe.wait_ge(sxl, 1)
        hidden(0, 0, 0)
        hidden(1, 0, 1)
        with pe.Fori(0, PAIRS - 1) as k:
            pair(k, False)
        pair(PAIRS - 1, True)

        def expert(j):
            return pe.value_load(owner[0:1, bass.ds(j, 1)], min_val=0, max_val=E - 1)

        def weights(w, e, first, width):
            return w[:, bass.ds(e, 1), first:first + width].rearrange("p o w -> p (o w)")

        def turn_rows(j, k, v):
            pe.wait_ge(rin[v % RING], 16 * k + 16)
            pe.wait_ge(rxl, j + 1)
            nc.tensor.transpose(ps_x[:, 0:P], rows[:, v % RING, 0:EMB], ident[:, :]).then_inc(rxt, 1)

        def row_hidden(j, v, e):
            pe.wait_ge(rxl, j + 2)
            pe.wait_ge(rhm, j + 1)
            for w in range(2):
                last = split3(ps_h[:, v % 2, w, :], rxt_hi[:, v % 2, :], rxt_lo[:, v % 2, :],
                              weights(we_hi, e, w * INTER, INTER), weights(we_lo, e, w * INTER, INTER), True, True)
            last.then_inc(rh, 1)

        def turn_hidden(j, v):
            pe.wait_ge(rhm, j + 3)
            pe.wait_ge(rhl, j + 1)
            for c in range(CHUNK):
                last = nc.tensor.transpose(ps_t[:, c * P:(c + 1) * P], hid[:, v % 2, c * P:(c + 1) * P], ident[:, :])
            last.then_inc(rht, 1)

        def row_project(j, v, e):
            pe.wait_ge(rhl, j + 2)
            pe.wait_ge(ra, j + 1)
            for c in range(CHUNK):
                cols = slice(c * P, (c + 1) * P)
                w3 = slice(2 * INTER + c * EMB, 2 * INTER + (c + 1) * EMB)
                both = we[:, :, bass.ds(e, 1), w3].rearrange("p s o w -> p s (o w)")
                nc.tensor.matmul(ps_y[:, v % 2, 0:2 * EMB].rearrange("p (s w) -> p s w", s=2), ht_hi[:, v % 2, cols], both,
                                 start=(c == 0), stop=False)
                last = nc.tensor.matmul(ps_y[:, v % 2, 0:EMB], ht_lo[:, v % 2, cols],
                                        weights(we_hi, e, 2 * INTER + c * EMB, EMB), start=False, stop=(c == CHUNK - 1))
            last.then_inc(ry, 1)

        def turn(k, last):
            for v in range(RING):
                j = RING * k + v
                e_now = expert(j)
                if not (last and v + 2 >= RING):
                    e_next = expert(j + 2)
                if not (last and v + 3 >= RING):
                    turn_rows(j + 3, k + (v + 3) // RING, v + 3)
                if not (last and v + 2 >= RING):
                    row_hidden(j + 2, v, e_next)
                if not (last and v + 1 >= RING):
                    turn_hidden(j + 1, v + 1)
                row_project(j, v, e_now)

        pe.wait_ge(owned, 1)
        pe.wait_ge(wlo, E)
        pe.wait_ge(sr, BATCH + 2)
        firsts = [expert(v) for v in range(2)]
        for v in range(2):
            turn_rows(v, 0, v)
            row_hidden(v, v, firsts[v])
        turn_rows(2, 0, 2)
        turn_hidden(0, 0)
        with pe.Fori(0, TURNS - 1) as k:
            turn(k, False)
        turn(TURNS - 1, True)


def build(nc, t, out):
    dram = lambda name, shape: nc.dram_tensor(name, shape, F32, kind="Internal").ap()
    routed = dram("routed", [SLOTS, ROW])
    base = dram("base", [TOKENS, EMB])
    xt2_all = dram("xt2_all", [BATCH + 1, P, SEQ])
    with ExitStack() as ctx:
        sb = lambda name, shape, dt: ctx.enter_context(nc.sbuf_tensor(name, shape, dt))
        x_res = sb("x_res", [P, (BATCH + 1) * QT, EMB], F32)
        xn2 = sb("xn2", [P, (BATCH + 1) * QT, ROW], F32)
        logits = sb("logits", [P, (BATCH + 1) * QT, EXPERTS], F32)
        with ExitStack() as actx:
            attention(nc, actx, t["x_in"], t["wqk"], t["wv"], t["wo"], t["bqk"], t["bv"], t["bo"], t, x_res, xn2, logits,
                      xt2_all, routed.rearrange("(t p) r -> p t r", p=P))
        with ExitStack() as fctx:
            mixture(nc, fctx, x_res, xn2, logits, xt2_all, routed, base, t["w_shared"], t["w_experts"], t,
                    out.rearrange("b s e -> (b s) e"))


def kernel(**inputs):
    import numpy as np
    import concourse.bacc as _bacc
    from concourse import mybir as _mybir
    from concourse.bass_utils import run_bass_kernel_spmd as _run

    a = {k: np.ascontiguousarray(v) for k, v in inputs.items()}
    D, H = DHEAD, HEADS
    def halves(w):
        w = w.reshape(w.shape[0], GROUPS, GROUP, 2, HALF)
        return w.transpose(0, 1, 3, 2, 4).reshape(w.shape[0], GROUPS, 2, P)
    wq, wkv = a["L0_attn_Wq"], a["L0_attn_Wkv"]
    wqk = np.concatenate([halves(wkv[:, :H * D]), halves(wq)], axis=2).reshape(P, -1)
    bqk = np.concatenate([halves(a["L0_attn_bkv"][None, :H * D]), halves(a["L0_attn_bq"][None])], axis=2)
    inv = (np.float32(1.0) / np.float32(10000.0) ** (np.arange(0, D, 2, dtype=np.float32) / np.float32(D))).astype(np.float32)
    ang = np.arange(SEQ, dtype=np.float32)[:, None] * inv[None, :]
    cos, sin = (np.tile(f(ang).astype(np.float32).T, (GROUP, 1)) for f in (np.cos, np.sin))
    rope = np.stack([np.stack([np.stack([cos, sin], 1), np.stack([-sin, cos], 1)], 1) * s
                     for s in (np.float32(1.0), np.float32(D ** -0.5))], 1).astype(np.float32)
    import ml_dtypes
    q, k = np.arange(P)[:, None], np.arange(P)[None, :]
    arrays = {
        "x_in": a["L0_attn_x"], "wqk": wqk, "wv": wkv[:, H * D:],
        "wo": a["L0_attn_Wo"].reshape(2 * GROUPS, P, EMB).transpose(1, 0, 2).reshape(P, -1),
        "bqk": bqk[0].transpose(2, 0, 1), "bv": a["L0_attn_bkv"][H * D:].reshape(2 * GROUPS, P).T, "bo": a["L0_attn_bo"],
        "rope": rope, "ident": np.eye(P, dtype=np.float32), "ident_b": np.eye(P).astype(ml_dtypes.bfloat16),
        "causal": np.where(k > q, NEG, 0.0).astype(ml_dtypes.bfloat16),
    }
    def expert(w1, w2, w3):
        lead = w1.shape[:-2]
        w3 = np.moveaxis(w3.reshape(*lead, CHUNK, P, EMB), -3, -2).reshape(*lead, P, CHUNK * EMB)
        return np.concatenate([w1, w2, w3], axis=-1)
    arrays.update({
        "wg": a["L0_ffn_Wg"], "w_shared": expert(a["L0_ffn_w1s"], a["L0_ffn_w2s"], a["L0_ffn_w3s"]),
        "w_experts": expert(a["L0_ffn_W1"], a["L0_ffn_W2"], a["L0_ffn_W3"]),
        "tri": (q < k).astype(ml_dtypes.bfloat16), "ones_b": np.ones((P, P), ml_dtypes.bfloat16),
        "rev": np.tile(np.arange(EXPERTS, 0, -1, dtype=np.float32), (P, 1)),
        "tile_no": np.tile(np.arange(RTILES, dtype=np.float32), (P, 1)),
        "token_no": (np.arange(TILES)[None, :] * P + np.arange(P)[:, None]).astype(np.uint32),
    })
    arrays = {k: np.ascontiguousarray(v) for k, v in arrays.items()}
    nc = _bacc.Bacc("TRN2", target_bir_lowering=False, num_devices=1)
    t = {k: nc.dram_tensor(k + "_dram", v.shape, _mybir.dt.from_np(v.dtype), kind="ExternalInput").ap() for k, v in arrays.items()}
    out = nc.dram_tensor("out_dram", a["L0_attn_x"].shape, F32, kind="ExternalOutput").ap()
    build(nc, t, out)
    r = _run(nc, [{k + "_dram": v for k, v in arrays.items()}], core_ids=[0])
    return r.results[0]["out_dram"]
```

```python
from contextlib import ExitStack

import concourse.bass as bass
from concourse import mybir

F32 = mybir.dt.float32
F32R = mybir.dt.float32r
BF16 = mybir.dt.bfloat16
F16 = mybir.dt.float16
U32 = mybir.dt.uint32
I32 = mybir.dt.int32
ALU = mybir.AluOpType
ACT = mybir.ActivationFunctionType
AX_X = mybir.AxisListType.X

P = 128
BATCH, SEQ, EMB = 8, 512, 128
HEADS, DHEAD = 16, 64
HALF = DHEAD // 2
GROUP = P // HALF
GROUPS = HEADS // GROUP
QT = SEQ // P
UNITS = [[(0, 0), (1, 0), (1, 1)], [(2, k) for k in range(3)], [(3, k) for k in range(4)]]
NU = len(UNITS)
STEPS = GROUP * NU
BSTEPS = GROUPS * STEPS
GW = GROUP * DHEAD
TILES = BATCH * QT
EPS = 1e-5
EXPERTS, INTER = 8, 512
TOKENS = BATCH * SEQ
ROW = EMB + 1
NOBODY = TOKENS
RTILES = TILES + EXPERTS - 1
SLOTS = RTILES * P
CHUNK = INTER // P
RING = 8
AHEAD = 2
NEG = -1e30

KA, KB, QA, QB, OT0, OT1, V01, V23, WO, BACK, LNT, LN2, LG = range(13)
SLOT_OF = {QB: 0, OT0: 1, OT1: 2, LG: 3, BACK: 3, V01: 4, V23: 5, LNT: 6, WO: 7, QA: 8, KA: 9, KB: 10, LN2: 11}
FIRST_CHUNKS = 10


def chunks_of(hg, last=False):
    kinds = [OT0, OT1, WO]
    kinds += [] if last and hg == GROUPS - 1 else [QB, V01, V23]
    kinds += [] if last and hg >= GROUPS - 2 else [KA, KB, QA]
    kinds += {1: [BACK, LN2], 2: [LG] if last else [LG, LNT]}.get(hg, [])
    return sorted(kinds, key=lambda k: (SLOT_OF[k], -k))


def chunks_before(hg, kind, last=False):
    return sum(len(chunks_of(i, last)) for i in range(hg)) + chunks_of(hg, last).index(kind)


CHUNKS_PER_BATCH = sum(len(chunks_of(i)) for i in range(GROUPS))
assert CHUNKS_PER_BATCH % 2 == 0


def chunk_at(b, hg, kind, last=False):
    n = chunks_before(hg, kind, last)
    return FIRST_CHUNKS + CHUNKS_PER_BATCH * b + n, (FIRST_CHUNKS + n) % 2


def first_chunk(m):
    return m, m % 2


def end_chunk(i):
    m, bank = chunk_at(BATCH - 1, GROUPS - 1, WO, True)
    return m + 1 + i, (bank + 1 + i) % 2


def attention(nc, ctx, x, wqk, wv, wo, bqk, bv, bo, tables, x_res, xn2, logits, xt2_all, zeros_to, consts):
    def sb(name, shape, dt):
        return ctx.enter_context(nc.sbuf_tensor(name, shape, dt))

    def sem(name):
        return ctx.enter_context(nc.semaphore(name))

    NG = GROUPS
    wqk_hi = sb("wqk_hi", [P, NG, 4, P], F32R)
    wqk_lo = sb("wqk_lo", [P, NG, 4, P], F32R)
    wv_hi = sb("wv_hi", [P, NG, GW], F32R)
    wv_lo = sb("wv_lo", [P, NG, GW], F32R)
    wo_hi = sb("wo_hi", [P, 2 * NG, EMB], F32R)
    wo_lo = sb("wo_lo", [P, 2 * NG, EMB], F32R)
    wo_raw = xn2[:, :, :].rearrange("p t r -> p (t r)")[:, 0:2 * NG * EMB].rearrange("p (g m) -> p g m", m=EMB)
    rope = sb("rope", [P, 2, 2, 2, SEQ], F32)
    bqk_s = sb("bqk_s", [P, NG, 4], F32)
    bv_s = sb("bv_s", [P, 2 * NG], F32)
    bo_s = sb("bo_s", [P, 1], F32)
    ident = consts["ident"]
    ident_b = sb("ident_b", [P, P], BF16)
    causal = sb("causal", [P, P], BF16)
    zero_row = sb("zero_row", [P, ROW], F32)
    bias_col = sb("bias_col", [P, 1], F32)
    acc = sb("acc", [P, SEQ], F32)
    stats = sb("stats", [P, QT, 6], F32)
    mv = sb("mv", [P, QT, 2], F32)
    veps = sb("veps", [P, QT], F32)
    mhalf = sb("mhalf", [P, QT], F32)
    wait_pad = sb("wait_pad", [P, 1], F32)
    rstd = sb("rstd", [P, QT], F32)
    xn = sb("xn", [P, QT, EMB], F32)
    stats2 = sb("stats2", [P, QT, 6], F32)
    mv2 = sb("mv2", [P, QT, 2], F32)
    veps2 = sb("veps2", [P, QT], F32)
    rstd2 = sb("rstd2", [P, QT], F32)
    xn2_t = sb("xn2_t", [P, QT, EMB], F32)
    xt2 = sb("xt2", [P, SEQ], F32)
    wg_s = sb("wg_s", [P, EXPERTS], F32)
    xt_hi = sb("xt_hi", [P, SEQ], F32R)
    xt_lo = sb("xt_lo", [P, SEQ], F32R)
    k_half = sb("k_half", [P, 2, SEQ], F32)
    prod = sb("prod", [P, 2, 2, 2, SEQ], F32)
    rot = sb("rot", [P, 2, 2, SEQ], F32)
    halves = sb("halves", [P, 2, 4, SEQ], F32R)
    stack = [sb(f"stack{h}", [P, 3, SEQ], F32R) for h in range(GROUP)]
    v_parts = sb("v_parts", [P, 2, 3, QT, GW], BF16)
    v_rest = sb("v_rest", [P, 2, 2 * GW], F32)
    probs = [sb(f"probs{u}", [P, len(UNITS[u]) * P], F32) for u in range(NU)]
    pt_hi = [sb(f"pt_hi{u}", [P, len(UNITS[u]), P], F16) for u in range(NU)]
    pt_lo = [sb(f"pt_lo{u}", [P, len(UNITS[u]), P], F16) for u in range(NU)]
    negmax = sb("negmax", [P, 2, QT, GROUP], F32)
    rowsum = sb("rowsum", [P, 2, QT, GROUP], F32)
    recip = sb("recip", [P, QT, GROUP], F32)
    o_sb = sb("o_sb", [P, QT, GW], F32)
    ot_hi = sb("ot_hi", [P, 2, QT, P], F32R)
    ot_lo = sb("ot_lo", [P, 2, QT, P], F32R)

    with ExitStack() as pctx:
        ps_s = pctx.enter_context(nc.psum_tensor("ps_s", [P, 2, 512], F32))
        ps_pt = pctx.enter_context(nc.psum_tensor("ps_pt", [P, 2, 512], F32))
        ps_o = pctx.enter_context(nc.psum_tensor("ps_o", [P, 2, 2, GW], F32))
        ps_m = pctx.enter_context(nc.psum_tensor("ps_m", [P, 2, 512], F32))

        in_qkv = sem("in_qkv")
        in_rope = sem("in_rope")
        in_w = sem("in_w")
        in_next = sem("in_next")
        in_x0 = sem("in_x0")
        in_x = sem("in_x")
        filled = sem("filled")
        const = sem("const")
        wsplit_hi = sem("wsplit_hi")
        wsplit = sem("wsplit")
        ln = sem("ln")
        ln_rstd = sem("ln_rstd")
        xt_h = sem("xt_h")
        xt_l = sem("xt_l")
        chunk = sem("chunk")
        bsum = sem("bsum")
        biased = sem("biased")
        ln2 = sem("ln2")
        xn2_saved = sem("xn2_saved")
        xt2_saved = sem("xt2_saved")
        ln2_rstd = sem("ln2_rstd")
        xt2d = sem("xt2d")
        lgd = sem("lgd")
        kbd = sem("kbd")
        kmul = sem("kmul")
        qmul = sem("qmul")
        radd = sem("radd")
        rhi = sem("rhi")
        rlo = sem("rlo")
        stacked = [sem(f"stacked{h}") for h in range(GROUP)]
        v1 = sem("v1")
        vr = sem("vr")
        v2 = sem("v2")
        v3 = sem("v3")
        scored = sem("scored")
        maxed = sem("maxed")
        expd = sem("expd")
        turned = sem("turned")
        pthi = sem("pthi")
        ptlo = sem("ptlo")
        pvd = sem("pvd")
        zeroed = sem("zeroed")
        rec = sem("rec")
        normed = sem("normed")
        otd = sem("otd")
        otl = sem("otl")
        woh = sem("woh")
        wol = sem("wol")
        added = sem("added")
        resd = sem("resd")
        block = pctx.enter_context(nc.Block())

        def tiles_of(u):
            blocks = UNITS[u]
            return [(i, slice(P * min(n for n, b in enumerate(blocks) if b[0] == i),
                              P * (1 + max(n for n, b in enumerate(blocks) if b[0] == i))))
                    for i in sorted({b[0] for b in blocks})]

        def place(j):
            return j % NU, (j % STEPS) // NU, (j // STEPS) % 2

        @block.sync
        def _(sp):
            xr = x.rearrange("b (t p) e -> p (b t) e", p=P)
            sp.dma_start(x_res[:, QT:2 * QT, :], xr[:, 0:QT, :]).then_inc(in_x0, 16)
            raw = prod[:, :, :, :, :].rearrange("p a b c s -> p (a b c s)")
            sp.dma_start(raw[:, 0:4 * NG * P], wqk).then_inc(in_qkv, 16)
            sp.dma_start(raw[:, 4 * NG * P:4 * NG * P + NG * GW], wv).then_inc(in_qkv, 16)
            sp.dma_start(ident[:, :], tables["ident"]).then_inc(in_qkv, 16)
            sp.dma_start(bqk_s[:, :, :], bqk).then_inc(in_qkv, 16)
            sp.dma_start(rope[:, :, :, :, :], tables["rope"]).then_inc(in_rope, 16)
            for dst, src in ((wo_raw.rearrange("p g m -> p (g m)"), wo), (bv_s[:, :], bv),
                             (bo_s[:, :], bo.rearrange("(e o) -> e o", o=1)), (ident_b[:, :], tables["ident_b"]),
                             (causal[:, :], tables["causal"]), (wg_s[:, :], tables["wg"])):
                sp.dma_start(dst, src).then_inc(in_w, 16)
            next_consts = [name for name in consts if name != "ident"]
            for name in next_consts:
                sp.dma_start(consts[name][:, :], tables[name]).then_inc(in_next, 16)
            sp.dma_start(x_res[:, 2 * QT:, :], xr[:, QT:, :]).then_inc(in_x, 16)

            def stack_head(G, h):
                used = STEPS * (G - 1) + NU * (h + 1)
                if not isinstance(G, int):
                    used = sp.snap(used)
                if h == 0:
                    sp.wait_ge(rlo, 2 * G + 2)
                if not isinstance(G, int) or G > 0:
                    sp.wait_ge(scored, used)
                for ab in range(2):
                    src = halves[HALF * h:HALF * (h + 1), ab, :, :].bitcast(F32)
                    dst = stack[h][HALF * ab:HALF * (ab + 1), :, :].bitcast(F32)
                    sp.dma_start(dst, src[:, 0:3, :]).then_inc(stacked[h], 16)
                    low = stack[h][2 * HALF + HALF * ab:2 * HALF + HALF * (ab + 1), :, :].bitcast(F32)
                    back = bass.AP(tensor=src.tensor, offset=src.offset + 3 * SEQ,
                                   ap=[list(src.ap[0]), [-SEQ, 3], [1, SEQ]])
                    sp.dma_start(low, back).then_inc(stacked[h], 16)

            def save_xn2(b):
                dst = xn2[:, bass.ds(b * QT, QT), 0:EMB] if isinstance(b, int) else xn2_slot(b)
                x_off = b * (P * SEQ) if isinstance(b, int) else sp.snap(b * (P * SEQ))
                sp.wait_ge(ln2, 13 * b + 13)
                sp.dma_start(dst, xn2_t[:, :, :]).then_inc(xn2_saved, 16)
                x_dst = bass.AP(tensor=xt2_all.tensor, offset=x_off, ap=[[SEQ, P], [1, SEQ]])
                sp.wait_ge(xt2d, b + 1)
                sp.dma_start(x_dst, xt2[:, :]).then_inc(xt2_saved, 16)

            def xn2_slot(b):
                full = xn2[:, 0:QT, 0:EMB]
                return bass.AP(tensor=full.tensor, offset=sp.snap(b * (QT * ROW)), ap=[list(a) for a in full.ap])

            def batch(b, last):
                for hg in range(NG - 1 if last else NG):
                    for h in range(GROUP):
                        stack_head(NG * b + hg + 1, h)
                    if hg == 1:
                        save_xn2(b)

            sp.wait_ge(const, 6)
            sp.dma_start(zeros_to, zero_row[:, :].rearrange("p (o r) -> p o r", o=1).broadcast_to([P, SLOTS // P, ROW])).then_inc(filled, 16)
            sp.sem_inc(xn2_saved, 16)
            sp.sem_inc(xt2_saved, 16)
            for h in range(GROUP):
                stack_head(0, h)
            with sp.Fori(0, BATCH - 1) as b:
                batch(b, False)
            batch(BATCH - 1, True)
            save_xn2(BATCH)
            for sm, v in ((xn2_saved, 16 * (BATCH + 2)), (xt2_saved, 16 * (BATCH + 2)), (filled, 16),
                          (in_next, 16 * len(next_consts))):
                sp.wait_ge(sm, v)

        @block.gpsimd
        def _(pool):
            nc.gpsimd.memset(mhalf[:, :], -0.5).then_inc(const, 1)
            nc.gpsimd.memset(acc[:, :], 0.0).then_inc(const, 1)
            nc.gpsimd.memset(o_sb[:, :, :], 0.0).then_inc(const, 1)
            nc.gpsimd.memset(x_res[:, 0:QT, :], 0.0).then_inc(const, 1)
            nc.gpsimd.memset(zero_row[:, 0:EMB], 0.0).then_inc(const, 1)
            nc.gpsimd.memset(zero_row[:, EMB:ROW].bitcast(mybir.dt.uint32), NOBODY).then_inc(const, 1)
            pool.wait_ge(const, 4)

            def rstd_of(b):
                pool.wait_ge(ln, 13 * b + 9)
                nc.gpsimd.tensor_tensor(rstd[:, :], veps[:, :], mhalf[:, :], ALU.pow).then_inc(ln_rstd, 1)

            def rstd2_of(b):
                pool.wait_ge(ln2, 13 * b + 9)
                nc.gpsimd.tensor_tensor(rstd2[:, :], veps2[:, :], mhalf[:, :], ALU.pow).then_inc(ln2_rstd, 1)

            def k_products(G):
                for ab in range(2):
                    pool.wait_ge(kbd, 2 * G + ab + 1)
                    nc.gpsimd.tensor_tensor(prod[:, 0, ab, :, :], k_half[:, ab:ab + 1, :].broadcast_to([P, 2, SEQ]),
                                            rope[:, 0, ab, :, :], ALU.mult).then_inc(kmul, 1)

            def rotate(G, kq):
                pool.wait_ge(qmul if kq else kmul, 2 * G + 2)
                pool.wait_ge(rlo, 2 * (G - 1) + kq + 1)
                nc.gpsimd.tensor_tensor(rot[:, kq, :, :], prod[:, kq, 0, :, :], prod[:, kq, 1, :, :],
                                        ALU.add).then_inc(radd, 1)

            def v_third(G, c, par):
                vp = v_parts[:, par, :, 2 * c:2 * c + 2, :].rearrange("p k t d -> p k (t d)")
                pool.wait_ge(v2, 2 * G + c + 1)
                nc.gpsimd.tensor_tensor(vp[:, 2, :], v_rest[:, c, :], vp[:, 1, :], ALU.subtract).then_inc(v3, 1)

            def k_low(G):
                pool.wait_ge(rhi, 2 * G + 1)
                nc.gpsimd.tensor_tensor(halves[:, :, 3, :], rot[:, 0, :, :], halves[:, :, 0, :].bitcast(F32),
                                        ALU.subtract).then_inc(rlo, 1)

            def q_low(G):
                pool.wait_ge(rhi, 2 * G + 2)
                nc.gpsimd.tensor_tensor(halves[:, :, 2, :], rot[:, 1, :, :], halves[:, :, 1, :].bitcast(F32),
                                        ALU.subtract).then_inc(rlo, 1)

            def group_work(G, par, norm=None, norm2=None, next_k=True):
                rotate(G, 1)
                k_low(G)
                if norm is not None:
                    rstd_of(norm)
                q_low(G)
                if norm2 is not None:
                    rstd2_of(norm2)
                for c in range(2):
                    v_third(G, c, par)
                if next_k:
                    k_products(G + 1)
                    rotate(G + 1, 0)

            def batch(b, last):
                for hg in range(NG):
                    if not (last and hg == NG - 1):
                        group_work(NG * b + hg + 1, (hg + 1) % 2, b + 1 if hg == 1 and not last else None,
                                   b if hg == 1 else None, not (last and hg == NG - 2))

            rstd_of(0)
            pool.wait_ge(wsplit, 2)
            pool.wait_ge(in_rope, 16)
            k_products(0)
            for c in range(2):
                v_third(0, c, 0)
            k_products(1)
            rotate(1, 0)
            with pool.Fori(0, BATCH - 1) as b:
                batch(b, False)
            batch(BATCH - 1, True)
            rstd2_of(BATCH)

        @block.scalar
        def _(act):
            act.sem_inc(expd, 3)
            act.wait_ge(in_qkv, 64)
            raw = prod[:, :, :, :, :].rearrange("p a b c s -> p (a b c s)")
            nqk = 4 * NG * P
            nc.scalar.copy(wqk_hi[:, :, :, :].rearrange("p g k m -> p (g k m)"), raw[:, 0:nqk]).then_inc(wsplit_hi, 1)
            nc.scalar.copy(wv_hi[:, :, :].rearrange("p g m -> p (g m)"), raw[:, nqk:nqk + NG * GW]).then_inc(wsplit_hi, 1)

            def xt_high(b, at):
                m, bank = at
                act.wait_ge(chunk, m + 1)
                nc.scalar.copy(xt_hi[:, :], ps_m[:, bank, :]).then_inc(xt_h, 1)

            def xt2_copy(b, at):
                m, bank = at
                act.wait_ge(chunk, m + 1)
                act.wait_ge(xt2_saved, 16 * b + 16)
                nc.scalar.copy(xt2[:, :], ps_m[:, bank, :]).then_inc(xt2d, 1)

            def high(G, kq, first):
                act.wait_ge(radd, 2 * G + kq + 1)
                if not first:
                    for h in range(GROUP):
                        act.wait_ge(stacked[h], 64 * G)
                nc.scalar.copy(halves[:, :, kq, :], rot[:, kq, :, :]).then_inc(rhi, 1)

            def k_bias(G, ab, hg, at, first):
                m, bank = at
                act.wait_ge(chunk, m + 1)
                if not first:
                    act.wait_ge(kmul, 2 * (G - 1) + ab + 1)
                nc.scalar.activation(k_half[:, ab, :], ps_m[:, bank, :], ACT.Identity, bias=bqk_s[:, hg, ab:ab + 1]).then_inc(kbd, 1)

            def v_first(G, c, par, at, first):
                m, bank = at
                act.wait_ge(chunk, m + 1)
                if not first:
                    act.wait_ge(pvd, STEPS * (G - 1) + 3)
                nc.scalar.copy(v_parts[:, par, 0, 2 * c:2 * c + 2, :].rearrange("p t d -> p (t d)"),
                               ps_m[:, bank, :]).then_inc(v1, 1)

            def exp(n, j):
                u, h, par = place(j)
                act.wait_ge(maxed, n + 1)
                act.wait_ge(turned, n + 1)
                for i, cols in tiles_of(u):
                    last = nc.scalar.activation(probs[u][:, cols], ps_s[:, j % 2, cols], ACT.Exp, bias=negmax[:, par, i, h:h + 1],
                                                accum_out=rowsum[:, par, i, h:h + 1])
                last.then_inc(expd, 1)

            def pt_high(n, j):
                u = j % NU
                act.wait_ge(turned, n + 4)
                act.wait_ge(pvd, n + 1)
                nc.scalar.copy(pt_hi[u][:, :, :].rearrange("p k q -> p (k q)"),
                               ps_pt[:, j % 2, 0:len(UNITS[u]) * P]).then_inc(pthi, 1)

            def ot_copy(c, at):
                m, bank = at
                act.wait_ge(chunk, m + 1)
                nc.scalar.copy(ot_hi[:, :, 2 * c:2 * c + 2, :].rearrange("p f t q -> p f (t q)"),
                               ps_m[:, bank, :].rearrange("p (f q) -> p f q", f=2)).then_inc(otd, 1)

            def v_second(G, c, par):
                act.wait_ge(vr, 2 * G + c + 1)
                nc.scalar.copy(v_parts[:, par, 1, 2 * c:2 * c + 2, :].rearrange("p t d -> p (t d)"),
                               v_rest[:, c, :]).then_inc(v2, 1)

            def batch(b, last):
                for hg in range(NG):
                    tail = last and hg == NG - 1
                    G = NG * b + hg + 1
                    for t in range(STEPS):
                        j = STEPS * hg + t
                        if not (last and j + 2 >= BSTEPS):
                            exp(BSTEPS * b + j + 2, j + 2)
                        if not (last and j + 1 >= BSTEPS):
                            pt_high(BSTEPS * b + j + 1, j + 1)
                        for c in range(2):
                            if t == SLOT_OF[(OT0, OT1)[c]]:
                                ot_copy(c, chunk_at(b, hg, OT0 + c, last))
                        if not tail:
                            for c in range(2):
                                if t == SLOT_OF[(V01, V23)[c]]:
                                    v_first(G, c, (hg + 1) % 2, chunk_at(b, hg, (V01, V23)[c]), False)
                                if t == SLOT_OF[(V01, V23)[c]] + 1:
                                    v_second(G, c, (hg + 1) % 2)
                            if t == 1:
                                high(G, 0, False)
                            if t == 3:
                                high(G, 1, False)
                        for kind in (KA, KB):
                            if t == SLOT_OF[kind] and not (last and hg >= NG - 2):
                                k_bias(G + 1, kind, (hg + 2) % NG, chunk_at(b, hg, kind), False)
                        if hg == 1 and t == SLOT_OF[LN2]:
                            xt2_copy(b, chunk_at(b, hg, LN2))
                        if hg == 2 and not last and t == SLOT_OF[LNT]:
                            xt_high(b + 1, chunk_at(b, hg, LNT))

            xt_high(0, first_chunk(0))
            act.wait_ge(wsplit, 2)
            for ab in range(2):
                k_bias(0, ab, 0, first_chunk(1 + ab), True)
            for c in range(2):
                v_first(0, c, 0, first_chunk(5 + c), True)
                v_second(0, c, 0)
            high(0, 0, True)
            for ab in range(2):
                k_bias(1, ab, 1, first_chunk(8 + ab), False)
            high(0, 1, True)
            act.wait_ge(in_w, 96)
            nc.scalar.copy(wo_hi[:, :, :], wo_raw).then_inc(woh, 1)
            exp(0, 0)
            exp(1, 1)
            pt_high(0, 0)
            with act.Fori(0, BATCH - 1) as b:
                batch(b, False)
            batch(BATCH - 1, True)
            for c in range(2):
                ot_copy(c, end_chunk(c))
            xt2_copy(BATCH, end_chunk(4))

        @block.vector
        def _(dve):
            dve.sem_inc(ptlo, 2)
            dve.sem_inc(normed, 1)
            dve.sem_inc(added, 1)
            nc.vector.memset(ps_o[:, 1, :, :], 0.0).then_inc(zeroed, 1)
            nc.vector.memset(recip[:, :, :], 1.0).then_inc(zeroed, 1)
            dve.wait_ge(zeroed, 2)

            def ln_stats(slot, n, stats, mv, veps, ln):
                xs = x_res[:, bass.ds(slot * QT, QT), :]
                for t in range(QT):
                    nc.vector.bn_stats(stats[:, t, :], xs[:, t, :]).then_inc(ln, 1)
                dve.wait_ge(ln, 13 * n + 4)
                nc.vector.memset(wait_pad[:, :], 0.0)
                for t in range(QT):
                    nc.vector.bn_aggr(mv[:, t, :], stats[:, t, :]).then_inc(ln, 1)
                dve.wait_ge(ln, 13 * n + 8)
                nc.vector.tensor_scalar(veps[:, :], mv[:, :, 1], EPS, None, ALU.add).then_inc(ln, 1)

            def ln_apply(slot, n, out, mv, rstd, ln, ln_rstd):
                dve.wait_ge(ln_rstd, n + 1)
                xs = x_res[:, bass.ds(slot * QT, QT), :]
                for t in range(QT):
                    nc.vector.tensor_scalar(out[:, t, :], xs[:, t, :], mv[:, t, 0:1], rstd[:, t:t + 1],
                                            ALU.subtract, ALU.mult).then_inc(ln, 1)

            def take_logits(b, at):
                m, bank = at
                dve.wait_ge(chunk, m + 1)
                nc.vector.tensor_copy(logits[:, bass.ds(b * QT, QT), :].rearrange("p t e -> p (t e)"),
                                      ps_m[:, bank, 0:QT * EXPERTS]).then_inc(lgd, 1)

            def xt_low(b, bank):
                dve.wait_ge(xt_h, b + 1)
                nc.vector.tensor_tensor(xt_lo[:, :], ps_m[:, bank, :], xt_hi[:, :].bitcast(F32), ALU.subtract).then_inc(xt_l, 1)

            def q_products(G, ab, hg, at, first):
                m, bank = at
                dve.wait_ge(chunk, m + 1)
                if not first:
                    dve.wait_ge(radd, 2 * G)
                nc.vector.scalar_tensor_tensor(
                    out=prod[:, 1, ab, :, :], in0=ps_m[:, bank, :].rearrange("p (o s) -> p o s", o=1).broadcast_to([P, 2, SEQ]),
                    scalar=bqk_s[:, hg, QA + ab:QA + ab + 1], in1=rope[:, 1, ab, :, :],
                    op0=ALU.add, op1=ALU.mult).then_inc(qmul, 1)

            def v_remainder(G, c, par, bank, first):
                dve.wait_ge(v1, 2 * G + c + 1)
                if not first:
                    dve.wait_ge(v3, 2 * (G - 1) + c + 1)
                vp = v_parts[:, par, :, 2 * c:2 * c + 2, :].rearrange("p k t d -> p k (t d)")
                nc.vector.tensor_tensor(v_rest[:, c, :], ps_m[:, bank, :], vp[:, 0, :], ALU.subtract).then_inc(vr, 1)

            def rowmax(n, j):
                u, h, par = place(j)
                dve.wait_ge(scored, n + 1)
                for i, cols in tiles_of(u):
                    last = nc.vector.tensor_reduce(negmax[:, par, i, h:h + 1], ps_s[:, j % 2, cols], AX_X, ALU.max, negate=True)
                last.then_inc(maxed, 1)

            def pt_low(n, j):
                u = j % NU
                dve.wait_ge(pthi, n + 1)
                nc.vector.tensor_tensor(pt_lo[u][:, :, :].rearrange("p k q -> p (k q)"), ps_pt[:, j % 2, 0:len(UNITS[u]) * P],
                                        pt_hi[u][:, :, :].rearrange("p k q -> p (k q)"), ALU.subtract).then_inc(ptlo, 1)

            def reciprocals(g, par):
                dve.wait_ge(expd, STEPS * g + STEPS + 3)
                nc.vector.reciprocal(recip[:, :, :], rowsum[:, par, :, :]).then_inc(rec, 1)
                dve.wait_ge(rec, g + 1)

            def normalise(g, c):
                dve.wait_ge(pvd, STEPS * g + (STEPS - NU + 1 if c == 0 else STEPS) + 3)
                nc.vector.tensor_tensor(
                    o_sb[:, 2 * c:2 * c + 2, :].rearrange("p t (h d) -> p (t h) d", d=DHEAD),
                    ps_o[:, c, :, :].rearrange("p t (h d) -> p (t h) d", d=DHEAD),
                    recip[:, 2 * c:2 * c + 2, :].rearrange("p t h -> p (t h)").unsqueeze(2).broadcast_to([P, 2 * GROUP, DHEAD]),
                    ALU.mult).then_inc(normed, 1)

            def ot_low(G, c, at):
                m, bank = at
                dve.wait_ge(otd, 2 * G + c + 1)
                hi = ot_hi[:, :, 2 * c:2 * c + 2, :].rearrange("p f t q -> p f (t q)").bitcast(F32)
                nc.vector.tensor_tensor(ot_lo[:, :, 2 * c:2 * c + 2, :].rearrange("p f t q -> p f (t q)"),
                                        ps_m[:, bank, :].rearrange("p (f q) -> p f q", f=2), hi, ALU.subtract).then_inc(otl, 1)

            def accumulate(hg, ordinal, at):
                m, bank = at
                dve.wait_ge(chunk, m + 1)
                if hg == 0:
                    nc.vector.tensor_scalar(acc[:, :], ps_m[:, bank, :], bias_col[:, :], None, ALU.add).then_inc(added, 1)
                else:
                    dve.wait_ge(added, ordinal + 1)
                    nc.vector.tensor_tensor(acc[:, :], ps_m[:, bank, :], acc[:, :], ALU.add).then_inc(added, 1)

            def residual(slot, at):
                m, bank = at
                dve.wait_ge(chunk, m + 1)
                xs = x_res[:, bass.ds(slot * QT, QT), :].rearrange("p t e -> p (t e)")
                nc.vector.tensor_tensor(xs, ps_m[:, bank, :], xs, ALU.add).then_inc(resd, 1)

            def batch(b, last):
                for hg in range(NG):
                    tail = last and hg == NG - 1
                    g = NG * b + hg
                    for t in range(STEPS):
                        j = STEPS * hg + t
                        if t == STEPS - 1:
                            normalise(g, 0)
                        if not (last and j + 3 >= BSTEPS):
                            rowmax(BSTEPS * b + j + 3, j + 3)
                        if t == 0:
                            normalise(g - 1, 1)
                        if not (last and j + 1 >= BSTEPS):
                            pt_low(BSTEPS * b + j + 1, j + 1)
                        if t == SLOT_OF[QB] and not tail:
                            q_products(g + 1, 1, (hg + 1) % NG, chunk_at(b, hg, QB), False)
                        if t == SLOT_OF[QA] and not (last and hg >= NG - 2):
                            q_products(g + 2, 0, (hg + 2) % NG, chunk_at(b, hg, QA), False)
                        if not tail:
                            for c in range(2):
                                if t == SLOT_OF[(V01, V23)[c]]:
                                    v_remainder(g + 1, c, (hg + 1) % 2, chunk_at(b, hg, (V01, V23)[c])[1], False)
                        for c in range(2):
                            if t == SLOT_OF[OT0 + c]:
                                ot_low(g, c, chunk_at(b, hg, OT0 + c, last))
                        if t == SLOT_OF[WO]:
                            accumulate((hg + NG - 1) % NG, g, chunk_at(b, hg, WO, last))
                        if hg == 1 and t == SLOT_OF[BACK]:
                            residual(b, chunk_at(b, hg, BACK))
                        if t == STEPS - 2:
                            reciprocals(g, hg % 2)
                        if hg == 1:
                            if t == 4:
                                dve.wait_ge(resd, b + 1)
                                nc.vector.memset(wait_pad[:, :], 0.0)
                                ln_stats(b, b, stats2, mv2, veps2, ln2)
                            if t == 9:
                                dve.wait_ge(xn2_saved, 16 * b + 16)
                                ln_apply(b, b, xn2_t, mv2, rstd2, ln2, ln2_rstd)
                        if hg == 2 and t == SLOT_OF[LG]:
                            take_logits(b, chunk_at(b, hg, LG, last))
                        if hg == 0 and t == 3 and not last:
                            ln_stats(b + 2, b + 1, stats, mv, veps, ln)
                        if hg == 2 and not last:
                            if t == 3:
                                ln_apply(b + 2, b + 1, xn, mv, rstd, ln, ln_rstd)
                            if t == SLOT_OF[LNT]:
                                xt_low(b + 1, chunk_at(b, hg, LNT)[1])

            raw = prod[:, :, :, :, :].rearrange("p a b c s -> p (a b c s)")
            nqk = 4 * NG * P
            dve.wait_ge(in_x0, 16)
            ln_stats(1, 0, stats, mv, veps, ln)
            ln_apply(1, 0, xn, mv, rstd, ln, ln_rstd)
            dve.wait_ge(wsplit_hi, 1)
            nc.vector.tensor_tensor(wqk_lo[:, :, :, :].rearrange("p g k m -> p (g k m)"), raw[:, 0:nqk],
                                    wqk_hi[:, :, :, :].rearrange("p g k m -> p (g k m)").bitcast(F32), ALU.subtract).then_inc(wsplit, 1)
            xt_low(0, 0)
            dve.wait_ge(wsplit_hi, 2)
            nc.vector.tensor_tensor(wv_lo[:, :, :].rearrange("p g m -> p (g m)"), raw[:, nqk:nqk + NG * GW],
                                    wv_hi[:, :, :].rearrange("p g m -> p (g m)").bitcast(F32), ALU.subtract).then_inc(wsplit, 1)
            dve.wait_ge(wsplit, 2)
            dve.wait_ge(in_rope, 16)
            for ab in range(2):
                q_products(0, ab, 0, first_chunk(3 + ab), True)
            for c in range(2):
                v_remainder(0, c, 0, first_chunk(5 + c)[1], True)
            for kq in range(2):
                dve.wait_ge(qmul if kq else kmul, 2)
                nc.vector.tensor_tensor(rot[:, kq, :, :], prod[:, kq, 0, :, :], prod[:, kq, 1, :, :], ALU.add).then_inc(radd, 1)
            q_products(1, 0, 1, first_chunk(7), False)
            for kq in range(2):
                dve.wait_ge(rhi, kq + 1)
                nc.vector.tensor_tensor(halves[:, :, 2 if kq else 3, :], rot[:, kq, :, :], halves[:, :, kq, :].bitcast(F32),
                                        ALU.subtract).then_inc(rlo, 1)
            dve.wait_ge(in_w, 96)
            dve.wait_ge(bsum, 1)
            nc.vector.tensor_tensor(bias_col[:, :], ps_s[:, 0, 0:1], bo_s[:, :], ALU.add).then_inc(biased, 1)
            dve.wait_ge(woh, 1)
            nc.vector.tensor_tensor(wo_lo[:, :, :], wo_raw, wo_hi[:, :, :].bitcast(F32), ALU.subtract).then_inc(wol, 1)
            for n in range(3):
                rowmax(n, n)
            pt_low(0, 0)
            dve.wait_ge(in_x, 16)
            with dve.Fori(0, BATCH - 1) as b:
                batch(b, False)
            batch(BATCH - 1, True)
            normalise(NG * BATCH - 1, 1)
            for c in range(2):
                ot_low(NG * BATCH, c, end_chunk(c))
            accumulate(NG - 1, NG * BATCH, end_chunk(2))
            residual(BATCH, end_chunk(3))
            dve.wait_ge(resd, BATCH + 1)
            ln_stats(BATCH, BATCH, stats2, mv2, veps2, ln2)
            dve.wait_ge(xn2_saved, 16 * BATCH + 16)
            ln_apply(BATCH, BATCH, xn2_t, mv2, rstd2, ln2, ln2_rstd)
            take_logits(BATCH, end_chunk(5))

        @block.tensor
        def _(pe):
            pe.sem_inc(turned, 3)
            pe.sem_inc(pvd, 3)

            def split3(out, a_hi, a_lo, b_hi, b_lo, start=True, stop=True):
                nc.tensor.matmul(out, a_hi, b_hi, start=start, stop=False)
                nc.tensor.matmul(out, a_hi, b_lo, start=False, stop=False)
                return nc.tensor.matmul(out, a_lo, b_hi, start=False, stop=stop)

            def bank_read(kind, g, hg, b, last):
                order = [(i, k) for i in range(NG) for k in chunks_of(i, last)]
                at = order.index((hg, kind))
                if at >= 2:
                    hg_of, before = order[at - 2]
                    g = g + hg_of - hg
                else:
                    before = chunks_of(NG - 1)[at - 2]
                    g = g - 1
                if before in (KA, KB):
                    pe.wait_ge(kbd, 2 * (g + 2) + 1 + before - KA)
                elif before == QA:
                    pe.wait_ge(qmul, 2 * (g + 2) + 1)
                elif before == QB:
                    pe.wait_ge(qmul, 2 * (g + 1) + 2)
                elif before in (OT0, OT1):
                    pe.wait_ge(otl, 2 * g + 1 + before - OT0)
                elif before in (V01, V23):
                    pe.wait_ge(vr, 2 * (g + 1) + 1 + before - V01)
                elif before == WO:
                    pe.wait_ge(added, g + 2)
                elif before == BACK:
                    pe.wait_ge(resd, b + 1)
                elif before == LNT:
                    pe.wait_ge(xt_l, b + 2)
                elif before == LN2:
                    pe.wait_ge(xt2d, b + 1)
                elif before == LG:
                    pe.wait_ge(lgd, b + 1)

            def project_qk(kind, hg, bank):
                split3(ps_m[:, bank, :], wqk_hi[:, hg, kind, :], wqk_lo[:, hg, kind, :], xt_hi[:, :], xt_lo[:, :]).then_inc(chunk, 1)

            def project_v(c, hg, bank):
                for u in range(2):
                    t = 2 * c + u
                    last = split3(ps_m[:, bank, u * GW:(u + 1) * GW], xt_hi[:, t * P:(t + 1) * P], xt_lo[:, t * P:(t + 1) * P],
                                  wv_hi[:, hg, :], wv_lo[:, hg, :])
                last.then_inc(chunk, 1)

            def project(kind, hg, bank):
                if kind <= QB:
                    project_qk(kind, hg, bank)
                else:
                    project_v(0 if kind == V01 else 1, hg, bank)

            def turn_x(b, xn, ln, bank):
                pe.wait_ge(ln, 13 * b + 13)
                for t in range(QT):
                    last = nc.tensor.transpose(ps_m[:, bank, t * P:(t + 1) * P], xn[:, t, :], ident[:, :])
                last.then_inc(chunk, 1)

            def router(b, bank):
                pe.wait_ge(xt2d, b + 1)
                for t in range(QT):
                    last = nc.tensor.matmul(ps_m[:, bank, t * EXPERTS:(t + 1) * EXPERTS], xt2[:, t * P:(t + 1) * P], wg_s[:, :],
                                            start=True, stop=True)
                last.then_inc(chunk, 1)

            def turn_o(c, n_norm, bank):
                pe.wait_ge(normed, n_norm)
                for u in range(2):
                    for f in range(2):
                        k = 2 * f + u
                        last = nc.tensor.transpose(ps_m[:, bank, k * P:(k + 1) * P], o_sb[:, 2 * c + u, f * P:(f + 1) * P], ident[:, :])
                last.then_inc(chunk, 1)

            def out_project(hg, f, bank):
                w = 2 * hg + f
                return split3(ps_m[:, bank, :], wo_hi[:, w, :], wo_lo[:, w, :], ot_hi[:, f, :, :].rearrange("p t q -> p (t q)"),
                              ot_lo[:, f, :, :].rearrange("p t q -> p (t q)"), start=(f == 0), stop=(f == 1))

            def turn_back(bank):
                for t in range(QT):
                    last = nc.tensor.transpose(ps_m[:, bank, t * P:(t + 1) * P], acc[:, t * P:(t + 1) * P], ident[:, :])
                last.then_inc(chunk, 1)

            def scores(n, j, g):
                u, h, _ = place(j)
                if u == 0:
                    pe.wait_ge(stacked[h], 64 * (g + 1))
                pe.wait_ge(expd, n + 2)
                st = stack[h]
                for i, cols in tiles_of(u):
                    out = ps_s[:, j % 2, cols]
                    q0, w = i * P, (i + 1) * P
                    nc.tensor.matmul(out, st[:, 1, q0:q0 + P], st[:, 0, 0:w], start=True, stop=False)
                    nc.tensor.matmul(out, st[:, 2, q0:q0 + P], st[:, 0, 0:w], start=False, stop=False)
                    last = nc.tensor.matmul(out[:, i * P:w], ident_b[:, :], causal[:, :], start=False, stop=True)
                last.then_inc(scored, 1)

            def turn_p(n, j):
                u = j % NU
                pe.wait_ge(expd, n + 4)
                pe.wait_ge(ptlo, n + 1)
                for k in range(len(UNITS[u])):
                    last = nc.tensor.transpose(ps_pt[:, j % 2, k * P:(k + 1) * P], probs[u][:, k * P:(k + 1) * P], ident[:, :])
                last.then_inc(turned, 1)

            def values(n, j, g):
                u, h, par = place(j)
                if j % STEPS == 0:
                    pe.wait_ge(v3, 2 * g + 2)
                if h == 0 and u < 2:
                    pe.wait_ge(normed, 2 * g + u + 1)
                pe.wait_ge(ptlo, n + 3)
                for blk, (i, k) in enumerate(UNITS[u]):
                    out = ps_o[:, i // 2, i % 2, h * DHEAD:(h + 1) * DHEAD]
                    for pt, parts in ((pt_hi[u], (0, 1, 2)), (pt_lo[u], (0, 1))):
                        for v in parts:
                            last = nc.tensor.matmul(out, pt[:, blk, :], v_parts[:, par, v, k, h * DHEAD:(h + 1) * DHEAD],
                                                    start=(k == 0 and pt is pt_hi[u] and v == 0),
                                                    stop=(k == i and pt is pt_lo[u] and v == 1))
                last.then_inc(pvd, 1)

            def issue(kind, g, hg, b, bank):
                if kind in (KA, KB, QA):
                    if hg == 2:
                        pe.wait_ge(xt_l, b + 2)
                    project(kind, (hg + 2) % NG, bank)
                elif kind in (QB, V01, V23):
                    project(kind, (hg + 1) % NG, bank)
                elif kind in (OT0, OT1):
                    turn_o(kind - OT0, 2 * g + kind - OT0 + 1, bank)
                elif kind == BACK:
                    pe.wait_ge(added, g + 1)
                    turn_back(bank)
                elif kind == LNT:
                    turn_x(b + 1, xn, ln, bank)
                elif kind == LN2:
                    turn_x(b, xn2_t, ln2, bank)
                elif kind == LG:
                    router(b, bank)

            def batch(b, last):
                for hg in range(NG):
                    g = NG * b + hg
                    for t in range(STEPS):
                        j = STEPS * hg + t
                        n = BSTEPS * b + j
                        if not (last and j + 3 >= BSTEPS):
                            scores(n + 3, j + 3, g + (t + 3) // STEPS)
                        if not (last and j + 1 >= BSTEPS):
                            turn_p(n + 1, j + 1)
                        wo_bank = chunk_at(b, hg, WO, last)[1]
                        if t == SLOT_OF[WO]:
                            out_project((hg + NG - 1) % NG, 1, wo_bank).then_inc(chunk, 1)
                        for kind in chunks_of(hg, last):
                            if t == SLOT_OF[kind] and kind != WO:
                                bank_read(kind, g, hg, b, last)
                                issue(kind, g, hg, b, chunk_at(b, hg, kind, last)[1])
                        if t == SLOT_OF[WO] - 1:
                            bank_read(WO, g, hg, b, last)
                            pe.wait_ge(otl, 2 * g + 2)
                            out_project((hg + NG - 1) % NG, 0, wo_bank)
                        values(n, j, g)

            pe.wait_ge(const, 6)
            pe.wait_ge(in_qkv, 64)
            turn_x(0, xn, ln, 0)
            pe.wait_ge(wsplit, 1)
            pe.wait_ge(xt_l, 1)
            project(KA, 0, 1)
            for m, (kind, hg, read, value) in enumerate((
                    (KB, 0, xt_l, 1), (QA, 0, kbd, 1), (QB, 0, kbd, 2), (V01, 0, qmul, 1),
                    (V23, 0, qmul, 2), (QA, 1, vr, 1), (KA, 1, vr, 2), (KB, 1, qmul, 3))):
                pe.wait_ge(read, value)
                project(kind, hg, m % 2)
            pe.wait_ge(in_w, 96)
            for k in range(2 * NG):
                last = nc.tensor.matmul(ps_s[:, 0, 0:1], wo_raw[:, k, :], bv_s[:, k:k + 1], start=(k == 0), stop=(k == 2 * NG - 1))
            last.then_inc(bsum, 1)
            pe.wait_ge(biased, 1)
            pe.wait_ge(wol, 1)
            for n in range(3):
                scores(n, n, 0)
            turn_p(0, 0)
            with pe.Fori(0, BATCH - 1) as b:
                batch(b, False)
            batch(BATCH - 1, True)
            ends = NG * BATCH
            pe.wait_ge(otl, 2 * ends)
            turn_o(0, 2 * ends + 1, end_chunk(0)[1])
            pe.wait_ge(added, ends + 1)
            turn_o(1, 2 * ends + 2, end_chunk(1)[1])
            pe.wait_ge(otl, 2 * ends + 2)
            out_project(NG - 1, 0, end_chunk(2)[1])
            out_project(NG - 1, 1, end_chunk(2)[1]).then_inc(chunk, 1)
            pe.wait_ge(added, ends + 2)
            turn_back(end_chunk(3)[1])
            turn_x(BATCH, xn2_t, ln2, end_chunk(4)[1])
            pe.wait_ge(resd, BATCH + 1)
            router(BATCH, end_chunk(5)[1])


def mixture(nc, ctx, x_res, xn2, logits, xt2_all, routed, base, w_shared, w_experts, consts, out):
    def sb(name, shape, dt):
        return ctx.enter_context(nc.sbuf_tensor(name, shape, dt))

    def sem(name):
        return ctx.enter_context(nc.semaphore(name))

    E, T = EXPERTS, TILES
    WALL = 3 * INTER
    ws_hi = sb("ws_hi", [P, WALL], F32R)
    ws_lo = sb("ws_lo", [P, WALL], F32R)
    w_raw = sb("w_raw", [P, 2, WALL], F32)
    we = sb("we", [P, 2, E, WALL], F32R)
    we_hi, we_lo = we[:, 0, :, :], we[:, 1, :, :]
    ident, tri, ones, rev, tile_no, token_no = (consts[n] for n in ("ident", "tri", "ones_b", "rev", "tile_no", "token_no"))
    top = sb("top", [P, T], F32)
    hit = sb("hit", [P, T, E], F32)
    hot = sb("hot", [P, T, E], F32)
    hot_b = sb("hot_b", [P, T, E], BF16)
    cum = [sb(f"cum{i}", [P, E, T], F32) for i in range(2)]
    excl = sb("excl", [P, E, T], F32)
    count_i = sb("count_i", [P, E], I32)
    tiles_i = sb("tiles_i", [P, E], I32)
    ends = [sb(f"ends{i}", [P, E], F32) for i in range(2)]
    starts = sb("starts", [P, E], F32)
    slot_f = sb("slot_f", [P, T], F32)
    slot_u = sb("slot_u", [P, T], U32)
    past = sb("past", [P, RTILES, E], F32)
    owner_f = sb("owner_f", [P, RTILES], F32)
    owner = sb("owner", [P, RTILES], I32)
    xt_raw = sb("xt_raw", [P, 2, SEQ], F32)
    xt_hi = sb("fxt_hi", [P, 2, SEQ], F32R)
    xt_lo = sb("fxt_lo", [P, 2, SEQ], F32R)
    rxt_hi = sb("rxt_hi", [P, 2, P], F32R)
    rxt_lo = sb("rxt_lo", [P, 2, P], F32R)
    acts = sb("acts", [P, 4, INTER], F32)
    gate, hid = acts[:, 0:2, :], acts[:, 2:4, :]
    ws_raw = acts[:, 0:3, :].rearrange("p c w -> p (c w)")
    ht_hi = sb("ht_hi", [P, 2, INTER], F32R)
    ht_lo = sb("ht_lo", [P, 2, INTER], F32R)
    rows = sb("rows", [P, RING, ROW], F32)
    res = sb("res", [P, RING, EMB], F32)
    yt = res[:, :, :].rearrange("p v e -> p (v e)").rearrange("p (v s) -> p v s", v=2)

    ps_h = ctx.enter_context(nc.psum_tensor("ps_h", [P, 2, 2, 512], F32))
    ps_x = ctx.enter_context(nc.psum_tensor("ps_x", [P, 512], F32))
    ps_t = ctx.enter_context(nc.psum_tensor("ps_t", [P, 512], F32))
    ps_y = ctx.enter_context(nc.psum_tensor("ps_y", [P, 2, 512], F32))

    in_ws = sem("fin_ws")
    in_w = [sem(f"fin_w{i}") for i in range(2)]
    in_x = [sem(f"fin_x{i}") for i in range(2)]
    wshi = sem("wshi")
    wslo = sem("wslo")
    whi = sem("whi")
    wlo = sem("wlo")
    rt = sem("rt")
    hotd = sem("hotd")
    counted = sem("counted")
    slotted = sem("slotted")
    owned = sem("owned")
    spread = sem("spread")
    sxh = sem("sxh")
    sxl = sem("sxl")
    sh = sem("sh")
    sg = sem("sg")
    shm = sem("shm")
    shh = sem("shh")
    shl = sem("shl")
    syc = sem("syc")
    sye = sem("sye")
    syt = sem("syt")
    sr = sem("sr")
    based = sem("based")
    rin = [sem(f"rin{i}") for i in range(RING)]
    gin = [sem(f"gin{i}") for i in range(RING)]
    outd = [sem(f"outd{i}") for i in range(RING)]
    rxt = sem("rxt")
    rxh = sem("rxh")
    rxl = sem("rxl")
    rh = sem("rh")
    rg = sem("rg")
    rhm = sem("rhm")
    rht = sem("rht")
    rhh = sem("rhh")
    rhl = sem("rhl")
    ry = sem("ry")
    rp = sem("rp")
    ra = sem("ra")
    zero = sem("zero")
    block = ctx.enter_context(nc.Block())
    PAIRS = BATCH // 2
    FIRST_ROWS = 3
    TURNS = -(-RTILES // RING)
    LAST = RTILES - RING * (TURNS - 1)

    @block.sync
    def _(sp):
        for v in range(2):
            sp.dma_start(xt_raw[:, v, :], xt2_all[v + 1]).then_inc(in_x[v], 16)
            if v == 0:
                sp.dma_start(ws_raw[:, :], w_shared).then_inc(in_ws, 16)
            sp.dma_start(w_raw[:, v, :], w_experts[v]).then_inc(in_w[v], 16)

        def first_rows():
            sp.wait_ge(spread, 16 * T)
            for v in range(FIRST_ROWS):
                sp.dma_start(rows[:, v, :], routed[v * P:(v + 1) * P, :]).then_inc(rin[v], 16)

        def pair(k, last):
            for v in range(2):
                b = 2 * k + v
                if not last:
                    e_off = sp.snap((b + 2) * (P * WALL))
                    x_off = sp.snap((b + 3) * (P * SEQ))
                    sp.wait_ge(sxl, b + 1)
                    sp.dma_start(xt_raw[:, v, :], bass.AP(tensor=xt2_all.tensor, offset=x_off, ap=[[SEQ, P], [1, SEQ]])
                                 ).then_inc(in_x[v], 16)
                    sp.wait_ge(wlo, b + 1)
                    sp.dma_start(w_raw[:, v, :], bass.AP(tensor=w_experts.tensor, offset=e_off, ap=[[WALL, P], [1, WALL]])
                                 ).then_inc(in_w[v], 16)
            for v in range(2):
                b = 2 * k + v
                dst, src = base[bass.ds(b * SEQ, SEQ), :], x_res[:, bass.ds((b + 1) * QT, QT), :]
                if not last:
                    d_off, s_off = sp.snap(b * (SEQ * EMB)), sp.snap((b + 1) * (QT * EMB))
                    full = x_res[:, 0:QT, :]
                    dst = bass.AP(tensor=base.tensor, offset=d_off, ap=[[EMB, P], [P * EMB, QT], [1, EMB]])
                    src = bass.AP(tensor=full.tensor, offset=s_off, ap=[list(a) for a in full.ap])
                else:
                    dst = dst.rearrange("(t p) e -> p t e", p=P)
                if last and v == 1:
                    first_rows()
                sp.wait_ge(sr, b + 3)
                sp.dma_start(dst, src).then_inc(based, 16)

        with sp.Fori(0, PAIRS - 1) as k:
            pair(k, False)
        pair(PAIRS - 1, True)

        for v in range(FIRST_ROWS, RING):
            sp.dma_start(rows[:, v, :], routed[v * P:(v + 1) * P, :]).then_inc(rin[v], 16)
        with sp.Fori(1, TURNS - 1) as k:
            for v in range(RING):
                src = bass.AP(tensor=routed.tensor, offset=sp.snap((RING * k + v) * (P * ROW)), ap=[[ROW, P], [1, ROW]])
                sp.wait_ge(outd[v], 16 * k)
                sp.dma_start(rows[:, v, :], src).then_inc(rin[v], 16)
        for v in range(LAST):
            first = (RING * (TURNS - 1) + v) * P
            sp.wait_ge(outd[v], 16 * (TURNS - 1))
            sp.dma_start(rows[:, v, :], routed[first:first + P, :]).then_inc(rin[v], 16)
        sp.wait_ge(based, 16 * BATCH)
        for v in range(RING):
            sp.wait_ge(outd[v], 16 * (TURNS if v < LAST else TURNS - 1))

    @block.gpsimd
    def _(pool):
        nc.gpsimd.memset(yt[:, 1, :], 0.0).then_inc(zero, 1)
        pool.wait_ge(slotted, 2)
        for b in range(BATCH):
            for t in range(QT * b, QT * (b + 1)):
                nc.gpsimd.indirect_dma_start(
                    out=routed, out_offset=bass.IndirectOffsetOnAxis(ap=slot_u[:, t:t + 1], axis=0),
                    in_=xn2[:, QT + t, :], in_offset=None).then_inc(spread, 16)
            pool.wait_ge(whi, b + 1)
            nc.gpsimd.tensor_tensor(we_lo[:, b, :], w_raw[:, b % 2, :], we_hi[:, b, :].bitcast(F32), ALU.subtract).then_inc(wlo, 1)

        bound = pool.to_reg(TOKENS - 1)

        def gather(k, v):
            pool.wait_ge(rin[v], 16 * k + 16)
            nc.gpsimd.indirect_dma_start(
                out=res[:, v, :], out_offset=None, in_=base,
                in_offset=bass.IndirectOffsetOnAxis(ap=rows[:, v, EMB:ROW].bitcast(U32), axis=0),
                bounds_check=bound, oob_is_err=False).then_inc(gin[v], 16)

        def scatter(k, v):
            pool.wait_ge(ra, RING * k + v + 3)
            nc.gpsimd.indirect_dma_start(
                out=out, out_offset=bass.IndirectOffsetOnAxis(ap=rows[:, v, EMB:ROW].bitcast(U32), axis=0),
                in_=res[:, v, :], in_offset=None, bounds_check=bound, oob_is_err=False).then_inc(outd[v], 16)

        pool.wait_ge(sr, BATCH + 2)
        nc.gpsimd.memset(res[:, :, :], 0.0).then_inc(zero, 1)
        pool.wait_ge(zero, 2)
        pool.wait_ge(based, 16 * BATCH)
        for v in range(AHEAD):
            gather(0, v)

        def turn(k, last):
            for v in range(LAST if last else RING):
                if v + AHEAD < (LAST if last else RING):
                    gather(k, v + AHEAD)
                elif not last:
                    gather(k + 1, v + AHEAD - RING)
                scatter(k, v)

        for k in range(TURNS):
            turn(k, k == TURNS - 1)

    @block.scalar
    def _(act):
        act.sem_inc(sye, 2)
        act.wait_ge(in_ws, 16)
        nc.scalar.copy(ws_hi[:, :], ws_raw[:, :]).then_inc(wshi, 1)

        def x_high(k, v):
            act.wait_ge(in_x[v], 16 * k + 16)
            nc.scalar.copy(xt_hi[:, v, :], xt_raw[:, v, :]).then_inc(sxh, 1)

        def gelu(s, p):
            act.wait_ge(sh, s + 1)
            act.wait_ge(shm, s + 1)
            nc.scalar.activation(gate[:, p, :], ps_h[:, p, 0, :], ACT.Gelu).then_inc(sg, 1)

        def h_high(s, p):
            act.wait_ge(shm, s + 3)
            act.wait_ge(syc, s + 1)
            nc.scalar.copy(ht_hi[:, p, :], hid[:, p, :]).then_inc(shh, 1)

        def w_high(k, v):
            act.wait_ge(in_w[v], 16 * k + 16)
            e = 2 * k + v
            nc.scalar.copy(we_hi[:, bass.ds(e, 1), :].rearrange("p o w -> p (o w)"), w_raw[:, v, :]).then_inc(whi, 1)

        def y_copy(b, v):
            act.wait_ge(syc, CHUNK * b + CHUNK + 2)
            act.wait_ge(syt, b + 1)
            nc.scalar.copy(yt[:, v, :], ps_y[:, v, :]).then_inc(sye, 1)

        def pair(k, last):
            for v in range(2):
                for c in range(CHUNK):
                    s, p = 8 * k + CHUNK * v + c, c % 2
                    ending = last and v == 1
                    if c == 1 and not ending:
                        x_high(k + v, 1 - v)
                    if not (ending and c == CHUNK - 1):
                        h_high(s + 1, 1 - p)
                    if not (ending and c >= CHUNK - 2):
                        gelu(s + 2, p)
                    if c == 0:
                        w_high(k, v)
                y_copy(2 * k + v, v)

        x_high(0, 0)
        gelu(0, 0)
        h_high(0, 0)
        gelu(1, 1)
        with act.Fori(0, PAIRS - 1) as k:
            pair(k, False)
        pair(PAIRS - 1, True)

        def row_high(j, v):
            act.wait_ge(rxt, j + 1)
            nc.scalar.copy(rxt_hi[:, v % 2, :], ps_x[:, 0:P]).then_inc(rxh, 1)

        def row_gelu(j, v):
            act.wait_ge(rh, j + 1)
            act.wait_ge(rhm, j + 1)
            nc.scalar.activation(gate[:, v % 2, :], ps_h[:, v % 2, 0, :], ACT.Gelu).then_inc(rg, 1)

        def turned_high(j, v):
            act.wait_ge(rht, j + 1)
            nc.scalar.copy(ht_hi[:, v % 2, :], ps_t[:, :]).then_inc(rhh, 1)

        def turn(k, last):
            for v in range(LAST if last else RING):
                j = RING * k + v
                if not (last and v + 3 >= LAST):
                    row_high(j + 3, v + 3)
                if not (last and v + 2 >= LAST):
                    row_gelu(j + 2, v)
                if not (last and v + 1 >= LAST):
                    turned_high(j + 1, v + 1)

        for v in range(2):
            row_high(v, v)
            row_gelu(v, v)
        row_high(2, 2)
        turned_high(0, 0)
        with act.Fori(0, TURNS - 1) as k:
            turn(k, False)
        turn(TURNS - 1, True)

    @block.vector
    def _(dve):
        dve.sem_inc(shm, 2)
        dve.sem_inc(sr, 1)
        dve.sem_inc(rhm, 2)
        dve.sem_inc(rxl, 1)
        dve.sem_inc(rhl, 1)
        dve.sem_inc(ra, 2)
        V = nc.vector
        def x_low(b, v):
            dve.wait_ge(sxh, b + 1)
            V.tensor_tensor(xt_lo[:, v, :], xt_raw[:, v, :], xt_hi[:, v, :].bitcast(F32), ALU.subtract).then_inc(sxl, 1)

        steps = [0]

        def link(ins):
            steps[0] += 1
            ins.then_inc(rt, 1)
            dve.wait_ge(rt, steps[0])

        lg = logits[:, QT:, :]
        by_t = lambda a: a[:, :].unsqueeze(2).broadcast_to([P, T, E])
        by_e = lambda a: a[:, :].unsqueeze(1).broadcast_to([P, T, E])
        link(V.tensor_reduce(top[:, :], lg, AX_X, ALU.max))
        link(V.tensor_tensor(hit[:, :, :], lg, by_t(top), ALU.is_equal))
        link(V.tensor_tensor(hit[:, :, :], hit[:, :, :], by_e(rev), ALU.mult))
        link(V.tensor_reduce(top[:, :], hit[:, :, :], AX_X, ALU.max))
        link(V.tensor_tensor(hot[:, :, :], by_e(rev), by_t(top), ALU.is_equal))
        V.tensor_copy(hot_b[:, :, :], hot[:, :, :]).then_inc(hotd, 1)
        V.tensor_copy(xn2[:, QT:, EMB:ROW].bitcast(U32), token_no[:, :].unsqueeze(2)).then_inc(slotted, 1)
        dve.wait_ge(wshi, 1)
        nc.vector.tensor_tensor(ws_lo[:, :], ws_raw[:, :], ws_hi[:, :].bitcast(F32), ALU.subtract).then_inc(wslo, 1)
        x_low(0, 0)
        dve.wait_ge(counted, 1)
        ranks = ps_t[:, 0:T * E].rearrange("p (t e) -> p t e", e=E)
        counts = ps_t[:, T * E:2 * T * E].rearrange("p (t e) -> p e t", e=E)
        link(V.tensor_copy(cum[0][:, :, :], counts))
        src, d = 0, 1
        while d < T:
            V.tensor_copy(cum[1 - src][:, :, 0:d], cum[src][:, :, 0:d])
            link(V.tensor_tensor(cum[1 - src][:, :, d:], cum[src][:, :, d:], cum[src][:, :, 0:T - d], ALU.add))
            src, d = 1 - src, 2 * d
        link(V.tensor_tensor(excl[:, :, :], counts, cum[src][:, :, :], ALU.subtract))
        link(V.tensor_scalar(count_i[:, :], cum[src][:, :, T - 1], float(P - 1), None, ALU.add))
        link(V.tensor_scalar(tiles_i[:, :], count_i[:, :], P.bit_length() - 1, None, ALU.arith_shift_right))
        link(V.tensor_copy(ends[0][:, :], tiles_i[:, :]))
        esrc, d = 0, 1
        while d < E:
            V.tensor_copy(ends[1 - esrc][:, 0:d], ends[esrc][:, 0:d])
            link(V.tensor_tensor(ends[1 - esrc][:, d:], ends[esrc][:, d:], ends[esrc][:, 0:E - d], ALU.add))
            esrc, d = 1 - esrc, 2 * d
        link(V.tensor_tensor(starts[:, :], ends[esrc][:, :], tiles_i[:, :], ALU.subtract))
        link(V.tensor_tensor(hit[:, :, :], ranks, excl[:, :, :].rearrange("p e t -> p t e"), ALU.subtract))
        link(V.scalar_tensor_tensor(out=hit[:, :, :], in0=by_e(starts), scalar=float(P), in1=hit[:, :, :],
                                    op0=ALU.mult, op1=ALU.add))
        link(V.tensor_tensor(hit[:, :, :], hit[:, :, :], hot[:, :, :], ALU.mult))
        link(V.tensor_reduce(slot_f[:, :], hit[:, :, :], AX_X, ALU.add))
        V.tensor_copy(slot_u[:, :], slot_f[:, :]).then_inc(slotted, 1)
        tiles_by_e = [P, RTILES, E]
        link(V.tensor_tensor(past[:, :, :], tile_no[:, :].unsqueeze(2).broadcast_to(tiles_by_e),
                             ends[esrc][:, :].unsqueeze(1).broadcast_to(tiles_by_e), ALU.is_ge))
        link(V.tensor_reduce(owner_f[:, :], past[:, :, :], AX_X, ALU.add))
        V.tensor_scalar(owner[:, :], owner_f[:, :], float(E - 1), None, ALU.min).then_inc(owned, 1)

        def multiply(s, p):
            dve.wait_ge(sg, s + 1)
            V.tensor_tensor(hid[:, p, :], ps_h[:, p, 1, :], gate[:, p, :], ALU.mult).then_inc(shm, 1)

        def h_low(s, p):
            dve.wait_ge(shh, s + 1)
            V.tensor_tensor(ht_lo[:, p, :], hid[:, p, :], ht_hi[:, p, :].bitcast(F32), ALU.subtract).then_inc(shl, 1)

        def add_shared(b):
            dve.wait_ge(syt, b + 3)
            xs = x_res[:, bass.ds((b + 1) * QT, QT), :].rearrange("p t e -> p (t e)")
            V.tensor_tensor(xs, ps_t[:, :], xs, ALU.add).then_inc(sr, 1)

        def pair(k, last):
            for v in range(2):
                b = 2 * k + v
                for c in range(CHUNK):
                    s, p = 8 * k + CHUNK * v + c, c % 2
                    ending = last and v == 1
                    if c == 1 and not ending:
                        x_low(b + 1, 1 - v)
                    if not (ending and c == CHUNK - 1):
                        h_low(s + 1, 1 - p)
                    if not (ending and c >= CHUNK - 2):
                        multiply(s + 2, p)
                    if c == 0:
                        add_shared(b - 1)

        multiply(0, 0)
        h_low(0, 0)
        multiply(1, 1)
        with dve.Fori(0, PAIRS - 1) as k:
            pair(k, False)
        pair(PAIRS - 1, True)
        add_shared(BATCH - 1)

        def row_low(j, v):
            dve.wait_ge(rxh, j + 1)
            V.tensor_tensor(rxt_lo[:, v % 2, :], ps_x[:, 0:P], rxt_hi[:, v % 2, :].bitcast(F32), ALU.subtract).then_inc(rxl, 1)

        def row_multiply(j, v):
            dve.wait_ge(rg, j + 1)
            V.tensor_tensor(hid[:, v % 2, :], ps_h[:, v % 2, 1, :], gate[:, v % 2, :], ALU.mult).then_inc(rhm, 1)

        def turned_low(j, v):
            dve.wait_ge(rhh, j + 1)
            V.tensor_tensor(ht_lo[:, v % 2, :], ps_t[:, :], ht_hi[:, v % 2, :].bitcast(F32), ALU.subtract).then_inc(rhl, 1)

        def add_rows(j, k, v):
            dve.wait_ge(ry, j + 1)
            dve.wait_ge(gin[v], 16 * k + 16)
            V.tensor_tensor(res[:, v, :], ps_y[:, v % 2, 0:EMB], res[:, v, :], ALU.add).then_inc(rp, 1)
            dve.wait_ge(rp, j + 1)
            V.tensor_tensor(res[:, v, :], ps_y[:, v % 2, EMB:2 * EMB], res[:, v, :], ALU.add).then_inc(ra, 1)

        def turn(k, last):
            for v in range(LAST if last else RING):
                j = RING * k + v
                if not (last and v + 3 >= LAST):
                    row_low(j + 3, v + 3)
                if not (last and v + 2 >= LAST):
                    row_multiply(j + 2, v)
                if not (last and v + 1 >= LAST):
                    turned_low(j + 1, v + 1)
                add_rows(j, k, v)

        for v in range(2):
            row_low(v, v)
            row_multiply(v, v)
        row_low(2, 2)
        turned_low(0, 0)
        with dve.Fori(0, TURNS - 1) as k:
            turn(k, False)
        turn(TURNS - 1, True)

    @block.tensor
    def _(pe):
        pe.sem_inc(syc, 2)
        pe.sem_inc(syt, 1)

        def split3(o, a_hi, a_lo, b_hi, b_lo, start, stop, skip=False):
            nc.tensor.matmul(o, a_hi, b_hi, start=start, stop=False, skip_group_check=skip)
            nc.tensor.matmul(o, a_hi, b_lo, start=False, stop=False, skip_group_check=skip)
            return nc.tensor.matmul(o, a_lo, b_hi, start=False, stop=stop, skip_group_check=skip)

        pe.wait_ge(hotd, 1)
        oh = hot_b[:, :, :].rearrange("p t e -> p (t e)")
        nc.tensor.matmul(ps_t[:, 0:T * E], tri[:, :], oh, start=True, stop=True)
        nc.tensor.matmul(ps_t[:, T * E:2 * T * E], ones[:, :], oh, start=True, stop=True).then_inc(counted, 1)

        def hidden(s, v, c):
            pe.wait_ge(shm, s + 1)
            for w in range(2):
                cols = slice(w * INTER + c * P, w * INTER + (c + 1) * P)
                last = split3(ps_h[:, c % 2, w, :], ws_hi[:, cols], ws_lo[:, cols], xt_hi[:, v, :], xt_lo[:, v, :], True, True)
            last.then_inc(sh, 1)

        def project(s, b, v, c):
            if c == 0:
                pe.wait_ge(sye, b + 1)
            pe.wait_ge(shl, s + 1)
            w3 = slice(2 * INTER + c * EMB, 2 * INTER + (c + 1) * EMB)
            split3(ps_y[:, v, :], ws_hi[:, w3], ws_lo[:, w3], ht_hi[:, c % 2, :], ht_lo[:, c % 2, :],
                   c == 0, c == CHUNK - 1).then_inc(syc, 1)

        def turn_y(b, v):
            pe.wait_ge(sye, b + 3)
            pe.wait_ge(sr, b + 2)
            for i in range(QT):
                last = nc.tensor.transpose(ps_t[:, i * P:(i + 1) * P], yt[:, v, i * P:(i + 1) * P], ident[:, :])
            last.then_inc(syt, 1)

        def pair(k, last):
            for v in range(2):
                b = 2 * k + v
                for c in range(CHUNK):
                    s = 8 * k + CHUNK * v + c
                    if c < CHUNK - 2:
                        hidden(s + 2, v, c + 2)
                    elif not (last and v == 1):
                        if c == CHUNK - 2:
                            pe.wait_ge(sxl, b + 2)
                        hidden(s + 2, 1 - v, c + 2 - CHUNK)
                    if c == 0:
                        turn_y(b - 1, 1 - v)
                    project(s, b, v, c)

        pe.wait_ge(wslo, 1)
        pe.wait_ge(sxl, 1)
        hidden(0, 0, 0)
        hidden(1, 0, 1)
        pe.wait_ge(slotted, 2)
        pe.wait_ge(zero, 1)
        with pe.Fori(0, PAIRS - 1) as k:
            pair(k, False)
        pair(PAIRS - 1, True)
        turn_y(BATCH - 1, 1)

        def expert(j):
            return pe.value_load(owner[0:1, bass.ds(j, 1)], min_val=0, max_val=E - 1)

        def weights(w, e, first, width):
            return w[:, bass.ds(e, 1), first:first + width].rearrange("p o w -> p (o w)")

        def turn_rows(j, k, v):
            pe.wait_ge(rin[v % RING], 16 * k + 16)
            pe.wait_ge(rxl, j + 1)
            nc.tensor.transpose(ps_x[:, 0:P], rows[:, v % RING, 0:EMB], ident[:, :]).then_inc(rxt, 1)

        def row_hidden(j, v, e):
            pe.wait_ge(rxl, j + 2)
            pe.wait_ge(rhm, j + 1)
            for w in range(2):
                last = split3(ps_h[:, v % 2, w, :], rxt_hi[:, v % 2, :], rxt_lo[:, v % 2, :],
                              weights(we_hi, e, w * INTER, INTER), weights(we_lo, e, w * INTER, INTER), True, True)
            last.then_inc(rh, 1)

        def turn_hidden(j, v):
            pe.wait_ge(rhm, j + 3)
            pe.wait_ge(rhl, j + 1)
            for c in range(CHUNK):
                last = nc.tensor.transpose(ps_t[:, c * P:(c + 1) * P], hid[:, v % 2, c * P:(c + 1) * P], ident[:, :])
            last.then_inc(rht, 1)

        def row_project(j, v, e):
            pe.wait_ge(rhl, j + 2)
            pe.wait_ge(ra, j + 1)
            for c in range(CHUNK):
                cols = slice(c * P, (c + 1) * P)
                w3 = slice(2 * INTER + c * EMB, 2 * INTER + (c + 1) * EMB)
                both = we[:, :, bass.ds(e, 1), w3].rearrange("p s o w -> p s (o w)")
                nc.tensor.matmul(ps_y[:, v % 2, 0:2 * EMB].rearrange("p (s w) -> p s w", s=2), ht_hi[:, v % 2, cols], both,
                                 start=(c == 0), stop=False)
                last = nc.tensor.matmul(ps_y[:, v % 2, 0:EMB], ht_lo[:, v % 2, cols],
                                        weights(we_hi, e, 2 * INTER + c * EMB, EMB), start=False, stop=(c == CHUNK - 1))
            last.then_inc(ry, 1)

        def turn(k, last):
            tiles = LAST if last else RING
            owners = [expert(RING * k + v) for v in range(3)]
            for v in range(tiles):
                j = RING * k + v
                if not (last and v + 3 >= tiles):
                    turn_rows(j + 3, k + (v + 3) // RING, v + 3)
                if not (last and v + 2 >= tiles):
                    row_hidden(j + 2, v, owners[v + 2])
                if not (last and v + 3 >= tiles) and v + 1 < tiles:
                    owners.append(expert(j + 3))
                if not (last and v + 1 >= tiles):
                    turn_hidden(j + 1, v + 1)
                row_project(j, v, owners[v])

        pe.wait_ge(owned, 1)
        pe.wait_ge(wlo, E)
        pe.wait_ge(sr, BATCH + 2)
        firsts = [expert(v) for v in range(2)]
        for v in range(2):
            turn_rows(v, 0, v)
            row_hidden(v, v, firsts[v])
        turn_rows(2, 0, 2)
        turn_hidden(0, 0)
        with pe.Fori(0, TURNS - 1) as k:
            turn(k, False)
        turn(TURNS - 1, True)


def build(nc, t, out):
    dram = lambda name, shape: nc.dram_tensor(name, shape, F32, kind="Internal").ap()
    routed = dram("routed", [SLOTS, ROW])
    base = dram("base", [TOKENS, EMB])
    xt2_all = dram("xt2_all", [BATCH + 1, P, SEQ])
    with ExitStack() as ctx:
        sb = lambda name, shape, dt: ctx.enter_context(nc.sbuf_tensor(name, shape, dt))
        x_res = sb("x_res", [P, (BATCH + 1) * QT, EMB], F32)
        xn2 = sb("xn2", [P, (BATCH + 1) * QT, ROW], F32)
        logits = sb("logits", [P, (BATCH + 1) * QT, EXPERTS], F32)
        consts = {"ident": sb("ident", [P, P], F32), "tri": sb("tri", [P, P], BF16), "ones_b": sb("ones_b", [P, P], BF16),
                  "rev": sb("rev", [P, EXPERTS], F32),
                  "tile_no": sb("tile_no", [P, RTILES], F32), "token_no": sb("token_no", [P, TILES], U32)}
        with ExitStack() as actx:
            attention(nc, actx, t["x_in"], t["wqk"], t["wv"], t["wo"], t["bqk"], t["bv"], t["bo"], t, x_res, xn2, logits,
                      xt2_all, routed.rearrange("(t p) r -> p t r", p=P), consts)
        with ExitStack() as fctx:
            mixture(nc, fctx, x_res, xn2, logits, xt2_all, routed, base, t["w_shared"], t["w_experts"], consts,
                    out.rearrange("b s e -> (b s) e"))


def kernel(**inputs):
    import numpy as np
    import concourse.bacc as _bacc
    from concourse import mybir as _mybir
    from concourse.bass_utils import run_bass_kernel_spmd as _run

    a = {k: np.ascontiguousarray(v) for k, v in inputs.items()}
    D, H = DHEAD, HEADS
    def halves(w):
        w = w.reshape(w.shape[0], GROUPS, GROUP, 2, HALF)
        return w.transpose(0, 1, 3, 2, 4).reshape(w.shape[0], GROUPS, 2, P)
    wq, wkv = a["L0_attn_Wq"], a["L0_attn_Wkv"]
    wqk = np.concatenate([halves(wkv[:, :H * D]), halves(wq)], axis=2).reshape(P, -1)
    bqk = np.concatenate([halves(a["L0_attn_bkv"][None, :H * D]), halves(a["L0_attn_bq"][None])], axis=2)
    inv = (np.float32(1.0) / np.float32(10000.0) ** (np.arange(0, D, 2, dtype=np.float32) / np.float32(D))).astype(np.float32)
    ang = np.arange(SEQ, dtype=np.float32)[:, None] * inv[None, :]
    cos, sin = (np.tile(f(ang).astype(np.float32).T, (GROUP, 1)) for f in (np.cos, np.sin))
    rope = np.stack([np.stack([np.stack([cos, sin], 1), np.stack([-sin, cos], 1)], 1) * s
                     for s in (np.float32(1.0), np.float32(D ** -0.5))], 1).astype(np.float32)
    import ml_dtypes
    q, k = np.arange(P)[:, None], np.arange(P)[None, :]
    arrays = {
        "x_in": a["L0_attn_x"], "wqk": wqk, "wv": wkv[:, H * D:],
        "wo": a["L0_attn_Wo"].reshape(2 * GROUPS, P, EMB).transpose(1, 0, 2).reshape(P, -1),
        "bqk": bqk[0].transpose(2, 0, 1), "bv": a["L0_attn_bkv"][H * D:].reshape(2 * GROUPS, P).T, "bo": a["L0_attn_bo"],
        "rope": rope, "ident": np.eye(P, dtype=np.float32), "ident_b": np.eye(P).astype(ml_dtypes.bfloat16),
        "causal": np.where(k > q, NEG, 0.0).astype(ml_dtypes.bfloat16),
    }
    def expert(w1, w2, w3):
        lead = w1.shape[:-2]
        w3 = np.moveaxis(w3.reshape(*lead, CHUNK, P, EMB), -3, -2).reshape(*lead, P, CHUNK * EMB)
        return np.concatenate([w1, w2, w3], axis=-1)
    arrays.update({
        "wg": a["L0_ffn_Wg"], "w_shared": expert(a["L0_ffn_w1s"], a["L0_ffn_w2s"], a["L0_ffn_w3s"]),
        "w_experts": expert(a["L0_ffn_W1"], a["L0_ffn_W2"], a["L0_ffn_W3"]),
        "tri": (q < k).astype(ml_dtypes.bfloat16), "ones_b": np.ones((P, P), ml_dtypes.bfloat16),
        "rev": np.tile(np.arange(EXPERTS, 0, -1, dtype=np.float32), (P, 1)),
        "tile_no": np.tile(np.arange(RTILES, dtype=np.float32), (P, 1)),
        "token_no": (np.arange(TILES)[None, :] * P + np.arange(P)[:, None]).astype(np.uint32),
    })
    arrays = {k: np.ascontiguousarray(v) for k, v in arrays.items()}
    nc = _bacc.Bacc("TRN2", target_bir_lowering=False, num_devices=1)
    t = {k: nc.dram_tensor(k + "_dram", v.shape, _mybir.dt.from_np(v.dtype), kind="ExternalInput").ap() for k, v in arrays.items()}
    out = nc.dram_tensor("out_dram", a["L0_attn_x"].shape, F32, kind="ExternalOutput").ap()
    build(nc, t, out)
    r = _run(nc, [{k + "_dram": v for k, v in arrays.items()}], core_ids=[0])
    return r.results[0]["out_dram"]
```
